# Optimizing a Trainium2 kernel written in Bass

```python
import numpy as np
import jax
import jax.numpy as jnp

def _softmax(x, axis=-1):
    return jax.nn.softmax(x, axis=axis)

def _gelu(x):
    return jax.nn.gelu(x, approximate=True)

def _silu(x):
    return jax.nn.silu(x)

def _sigmoid(x):
    return jax.nn.sigmoid(x)

def _layernorm(x, axis=-1, eps=1e-05):
    m = jnp.mean(x, axis=axis, keepdims=True)
    v = jnp.var(x, axis=axis, keepdims=True)
    return (x - m) / jnp.sqrt(v + eps)

def _scatter_add(tgt, idx, src, axis=0):
    return tgt.at[idx].add(src)

def _segment_sum(src, seg, n):
    return jax.ops.segment_sum(src, seg, n)
kernel_name = 'mk_xattn_ffn_d2_seqx_r2_599342'

def setup_inputs(seed: int=0):
    np.random.seed(seed)
    _w = jnp.asarray

    def _rec_inputs():
        import jax
        import jax.numpy as jnp
        _rk = jax.random.key(seed)
        x = -0.0002928 + 1 * jax.random.normal(jax.random.fold_in(_rk, 1), (8, 100, 512), jnp.float32)
        _lenS = 100 - jax.random.randint(jax.random.fold_in(_rk, 7), (8,), 0, max(1, 100 // 4) + 1, jnp.int32)
        _lenS2 = 722 - jax.random.randint(jax.random.fold_in(_rk, 8), (8,), 0, max(1, 722 // 4) + 1, jnp.int32)
        _ctx_1024P = jax.random.normal(jax.random.fold_in(_rk, 11), (8, 16, 512), jnp.float32)
        _ctx_1024c = jax.random.dirichlet(jax.random.fold_in(_rk, 511), 0.3 * jnp.ones((16,), jnp.float32), (8, 722))
        _ctx_1024t = jnp.einsum('bsk,bkd->bsd', _ctx_1024c, _ctx_1024P)
        _ctx_1024t = _ctx_1024t * jax.lax.rsqrt(jnp.mean(jnp.square(_ctx_1024t)) + 1e-12) * 0.953939
        ctx_1024 = 2.81802e-05 + 1.00001 * (_ctx_1024t + 0.3 * jax.random.normal(jax.random.fold_in(_rk, 611), (8, 722, 512), jnp.float32))
        return (x, ctx_1024)
    x, ctx_1024 = _rec_inputs()

    def _L0_xattn_setup():
        import jax, jax.numpy as jnp
        import numpy as np
        D_MODEL = 512
        N_HEADS = 16
        HEAD_DIM = D_MODEL // N_HEADS
        key = jax.random.key(seed)
        k1, k2, k3, k4, k5, k6 = jax.random.split(key, 6)
        B, T_q, T_kv = (4, 512, 2048)
        s = 1.0 / np.sqrt(D_MODEL)
        return {'query': jax.random.normal(k1, (B, T_q, D_MODEL), dtype=jnp.float32), 'kv_source': jax.random.normal(k2, (B, T_kv, D_MODEL), dtype=jnp.float32), 'w_q': jax.random.normal(k3, (D_MODEL, D_MODEL), dtype=jnp.float32) * s, 'w_k': jax.random.normal(k4, (D_MODEL, D_MODEL), dtype=jnp.float32) * s, 'w_v': jax.random.normal(k5, (D_MODEL, D_MODEL), dtype=jnp.float32) * s, 'w_o': jax.random.normal(k6, (D_MODEL, D_MODEL), dtype=jnp.float32) * s}
    _L0_xattn_all = _L0_xattn_setup()
    _L0_xattn_in = {k: v for k, v in _L0_xattn_all.items() if k in ('w_q', 'w_k', 'w_v', 'w_o')}
    del _L0_xattn_all

    def _L0_ffn_setup():
        import jax, jax.numpy as jnp
        import numpy as np
        DIM = 512
        NUM_EXPERTS = 8
        ACTIVE_EXPERTS = 2
        EXPERT_DIM = 1024
        key = jax.random.key(seed)
        k1, k2, k3, k4 = jax.random.split(key, 4)
        x = jax.random.normal(k1, (1, 1024, DIM), dtype=jnp.float32)
        gate_w = jax.random.normal(k2, (NUM_EXPERTS, DIM), dtype=jnp.float32) * 0.02
        balance_bias = jnp.zeros((NUM_EXPERTS,), dtype=jnp.float32)
        w1 = jax.random.normal(k3, (NUM_EXPERTS, EXPERT_DIM, DIM), dtype=jnp.float32) * 0.02
        w2 = jax.random.normal(k4, (NUM_EXPERTS, DIM, EXPERT_DIM), dtype=jnp.float32) * 0.02
        return {'x': x, 'gate_w': gate_w, 'balance_bias': balance_bias, 'w1': w1, 'w2': w2}
    _L0_ffn_all = _L0_ffn_setup()
    _L0_ffn_in = {k: v for k, v in _L0_ffn_all.items() if k in ('gate_w', 'balance_bias', 'w1', 'w2')}
    del _L0_ffn_all

    def _L1_xattn_setup():
        import jax, jax.numpy as jnp
        import numpy as np
        D_MODEL = 512
        NUM_HEADS = 16
        D_K = D_MODEL // NUM_HEADS
        key = jax.random.key(seed)
        ks = jax.random.split(key, 11)
        B, L = (4, 1024)
        s = 0.02
        return {'query': jax.random.normal(ks[0], (B, L, D_MODEL), jnp.float32), 'key': jax.random.normal(ks[1], (B, L, D_MODEL), jnp.float32), 'value': jax.random.normal(ks[2], (B, L, D_MODEL), jnp.float32), 'Wq': jax.random.normal(ks[3], (D_MODEL, D_MODEL), jnp.float32) * s, 'bq': jnp.zeros((D_MODEL,), jnp.float32), 'Wk': jax.random.normal(ks[4], (D_MODEL, D_MODEL), jnp.float32) * s, 'bk': jnp.zeros((D_MODEL,), jnp.float32), 'Wv': jax.random.normal(ks[5], (D_MODEL, D_MODEL), jnp.float32) * s, 'bv': jnp.zeros((D_MODEL,), jnp.float32), 'Wo': jax.random.normal(ks[6], (D_MODEL, D_MODEL), jnp.float32) * s, 'bo': jnp.zeros((D_MODEL,), jnp.float32)}
    _L1_xattn_all = _L1_xattn_setup()
    _L1_xattn_in = {k: v for k, v in _L1_xattn_all.items() if k in ('Wq', 'bq', 'Wk', 'bk', 'Wv', 'bv', 'Wo', 'bo')}
    del _L1_xattn_all

    def _L1_ffn_setup():
        import jax, jax.numpy as jnp
        import numpy as np
        B, T, D, E, H = (8, 1024, 512, 8, 128)
        LN_EPS = 1e-05
        key = jax.random.key(seed)
        ks = jax.random.split(key, 4)
        return {'x': jax.random.normal(ks[0], (B, T, D), dtype=jnp.float32), 'Wg': jax.random.normal(ks[1], (E, D), dtype=jnp.float32) * 0.02, 'ln_scale': jnp.ones((E, D), dtype=jnp.float32), 'ln_bias': jnp.zeros((E, D), dtype=jnp.float32), 'W1': jax.random.normal(ks[2], (E, D, H), dtype=jnp.float32) * 0.02, 'b1': jnp.zeros((E, H), dtype=jnp.float32), 'W2': jax.random.normal(ks[3], (E, H, D), dtype=jnp.float32) * 0.02, 'b2': jnp.zeros((E, D), dtype=jnp.float32)}
    _L1_ffn_all = _L1_ffn_setup()
    _L1_ffn_in = {k: v for k, v in _L1_ffn_all.items() if k in ('Wg', 'ln_scale', 'ln_bias', 'W1', 'b1', 'W2', 'b2')}
    del _L1_ffn_all
    return {'x': x, 'ctx_1024': ctx_1024, 'L0_xattn_w_q': _L0_xattn_in['w_q'], 'L0_xattn_w_k': _L0_xattn_in['w_k'], 'L0_xattn_w_v': _L0_xattn_in['w_v'], 'L0_xattn_w_o': _L0_xattn_in['w_o'], 'L0_ffn_gate_w': _L0_ffn_in['gate_w'], 'L0_ffn_balance_bias': _L0_ffn_in['balance_bias'], 'L0_ffn_w1': _L0_ffn_in['w1'], 'L0_ffn_w2': _L0_ffn_in['w2'], 'L1_xattn_Wq': _L1_xattn_in['Wq'], 'L1_xattn_bq': _L1_xattn_in['bq'], 'L1_xattn_Wk': _L1_xattn_in['Wk'], 'L1_xattn_bk': _L1_xattn_in['bk'], 'L1_xattn_Wv': _L1_xattn_in['Wv'], 'L1_xattn_bv': _L1_xattn_in['bv'], 'L1_xattn_Wo': _L1_xattn_in['Wo'], 'L1_xattn_bo': _L1_xattn_in['bo'], 'L1_ffn_Wg': _L1_ffn_in['Wg'], 'L1_ffn_ln_scale': _L1_ffn_in['ln_scale'], 'L1_ffn_ln_bias': _L1_ffn_in['ln_bias'], 'L1_ffn_W1': _L1_ffn_in['W1'], 'L1_ffn_b1': _L1_ffn_in['b1'], 'L1_ffn_W2': _L1_ffn_in['W2'], 'L1_ffn_b2': _L1_ffn_in['b2']}

def reference(x, ctx_1024, L0_xattn_w_q, L0_xattn_w_k, L0_xattn_w_v, L0_xattn_w_o, L0_ffn_gate_w, L0_ffn_balance_bias, L0_ffn_w1, L0_ffn_w2, L1_xattn_Wq, L1_xattn_bq, L1_xattn_Wk, L1_xattn_bk, L1_xattn_Wv, L1_xattn_bv, L1_xattn_Wo, L1_xattn_bo, L1_ffn_Wg, L1_ffn_ln_scale, L1_ffn_ln_bias, L1_ffn_W1, L1_ffn_b1, L1_ffn_W2, L1_ffn_b2):
    import jax
    import jax.numpy as jnp

    def _L0_xattn_ref(query, kv_source, w_q, w_k, w_v, w_o):
        import jax, jax.numpy as jnp
        import numpy as np
        D_MODEL = 512
        N_HEADS = 16
        HEAD_DIM = D_MODEL // N_HEADS
        B, T_q, _ = query.shape
        T_kv = kv_source.shape[1]
        q = (query @ w_q.T).reshape(B, T_q, N_HEADS, HEAD_DIM)
        k = (kv_source @ w_k.T).reshape(B, T_kv, N_HEADS, HEAD_DIM)
        v = (kv_source @ w_v.T).reshape(B, T_kv, N_HEADS, HEAD_DIM)
        scale = HEAD_DIM ** (-0.5)
        attn = jax.nn.softmax(jnp.einsum('bqhd,bkhd->bhqk', q, k) * scale, axis=-1)
        out = jnp.einsum('bhqk,bkhd->bqhd', attn, v).reshape(B, T_q, D_MODEL)
        return out @ w_o.T

    def _L0_ffn_ref(x, gate_w, balance_bias, w1, w2):
        import jax, jax.numpy as jnp
        import numpy as np
        DIM = 512
        NUM_EXPERTS = 8
        ACTIVE_EXPERTS = 2
        EXPERT_DIM = 1024
        B, S, D = x.shape
        T = B * S
        xf = x.reshape(T, D)
        gate_logits = jnp.einsum('td,ed->te', xf, gate_w)
        gate_scores = jax.nn.sigmoid(gate_logits + balance_bias)
        topk_scores, topk_idx = jax.lax.top_k(gate_scores, ACTIVE_EXPERTS)
        topk_scores = topk_scores / (topk_scores.sum(axis=-1, keepdims=True) + 1e-06)
        comb = jnp.zeros((T, NUM_EXPERTS), dtype=x.dtype)
        comb = comb.at[jnp.arange(T)[:, None], topk_idx].add(topk_scores)
        h = jax.nn.silu(jnp.einsum('td,ehd->teh', xf, w1))
        expert_out = jnp.einsum('teh,edh->ted', h, w2)
        out = jnp.einsum('te,ted->td', comb, expert_out)
        return out.reshape(B, S, D)

    def _L1_xattn_ref(query, key, value, Wq, bq, Wk, bk, Wv, bv, Wo, bo):
        import jax, jax.numpy as jnp
        import numpy as np
        D_MODEL = 512
        NUM_HEADS = 16
        D_K = D_MODEL // NUM_HEADS
        B, Lq, _ = query.shape
        Lk = key.shape[1]
        q = (query @ Wq.T + bq).reshape(B, Lq, NUM_HEADS, D_K).transpose(0, 2, 1, 3)
        k = (key @ Wk.T + bk).reshape(B, Lk, NUM_HEADS, D_K).transpose(0, 2, 1, 3)
        v = (value @ Wv.T + bv).reshape(B, Lk, NUM_HEADS, D_K).transpose(0, 2, 1, 3)
        scores = jnp.einsum('bhqd,bhkd->bhqk', q, k) / jnp.sqrt(jnp.float32(D_K))
        attn = jax.nn.softmax(scores, axis=-1)
        out = jnp.einsum('bhqk,bhkd->bhqd', attn, v)
        out = out.transpose(0, 2, 1, 3).reshape(B, Lq, D_MODEL)
        return out @ Wo.T + bo

    def _L1_ffn_ref(x, Wg, ln_scale, ln_bias, W1, b1, W2, b2):
        import jax, jax.numpy as jnp
        import numpy as np
        B, T, D, E, H = (8, 1024, 512, 8, 128)
        LN_EPS = 1e-05
        Bs, Ts, Ds = x.shape
        xt = x.reshape(Bs * Ts, Ds)
        logits = xt @ Wg.T
        top1 = jnp.argmax(logits, axis=-1)
        mu = jnp.mean(xt, axis=-1, keepdims=True)
        var = jnp.mean(jnp.square(xt - mu), axis=-1, keepdims=True)
        xhat = (xt - mu) * jax.lax.rsqrt(var + LN_EPS)
        n_experts = Wg.shape[0]

        def body(y, p):
            s_e, b_e, w1, bb1, w2, bb2, eid = p
            h = jax.nn.gelu((xhat * s_e + b_e) @ w1 + bb1, approximate=False)
            out = h @ w2 + bb2
            mask = (top1 == eid)[:, None].astype(out.dtype)
            return (y + mask * out, None)
        y0 = jnp.zeros_like(xt)
        y, _ = jax.lax.scan(body, y0, (ln_scale, ln_bias, W1, b1, W2, b2, jnp.arange(n_experts)))
        return y.reshape(Bs, Ts, Ds)
    x = x + _L0_xattn_ref(_layernorm(x, axis=-1), ctx_1024, L0_xattn_w_q, L0_xattn_w_k, L0_xattn_w_v, L0_xattn_w_o)
    x = x + _L0_ffn_ref(_layernorm(x, axis=-1), L0_ffn_gate_w, L0_ffn_balance_bias, L0_ffn_w1, L0_ffn_w2)
    x = x + _L1_xattn_ref(_layernorm(x, axis=-1), ctx_1024, ctx_1024, L1_xattn_Wq, L1_xattn_bq, L1_xattn_Wk, L1_xattn_bk, L1_xattn_Wv, L1_xattn_bv, L1_xattn_Wo, L1_xattn_bo)
    x = x + _L1_ffn_ref(_layernorm(x, axis=-1), L1_ffn_Wg, L1_ffn_ln_scale, L1_ffn_ln_bias, L1_ffn_W1, L1_ffn_b1, L1_ffn_W2, L1_ffn_b2)
    return x

_drawn_inputs = setup_inputs


def setup_inputs(seed=0):
    import zlib

    import numpy as np

    out = dict(_drawn_inputs(seed))
    spreads = {'L0_ffn_balance_bias': (0.0, 0.1),
     'L1_xattn_bq': (0.0, 0.8),
     'L1_xattn_bk': (0.0, 0.8),
     'L1_xattn_bv': (0.0, 0.1),
     'L1_xattn_bo': (0.0, 0.1),
     'L1_ffn_ln_scale': (1.0, 0.6),
     'L1_ffn_ln_bias': (0.0, 0.8),
     'L1_ffn_b1': (0.0, 0.682),
     'L1_ffn_b2': (0.0, 0.1)}
    factors = {'L1_xattn_Wq': 6.306, 'L1_xattn_Wk': 6.229}
    for name, (base, spread) in spreads.items():
        noise = np.random.default_rng([zlib.crc32(name.encode()), seed]).standard_normal(out[name].shape)
        drawn = base * np.exp(spread * noise) if base else spread * noise
        out[name] = jnp.asarray(drawn.astype(out[name].dtype))
    for name, factor in factors.items():
        out[name] = (out[name] * factor).astype(out[name].dtype)
    return out
```

```python
from contextlib import ExitStack

import concourse.bass as bass
import numpy as np
from concourse import mybir

NB, TQ, D = 8, 100, 512
NT = NB * TQ
NK = 722
NH, DH = 16, 32
NE = 8
HID0 = 1024
HID1 = 128
P = 128
C = D // P
HALF_K = NK // 2
HALF_T = NT // 2
KT_TILES = -(-NK // P)
LAST_K = NK - (KT_TILES - 1) * P
HT = HID0 // P
W_SCALE = 256.0
UNSCALE = 1.0 / W_SCALE
Q_UNSCALE = UNSCALE / float(np.sqrt(DH))
LN_EPS = 1e-5


def key_rows(t):
    return LAST_K if t == KT_TILES - 1 else P


UNITS = [("V", 0), ("K", 0, 0), ("K", 0, 1), ("V", 1), ("K", 1, 0), ("K", 1, 1), ("V", 2),
         ("K", 2, 0), ("K", 2, 1), ("V", 3), ("K", 3, 0), ("K", 3, 1), ("V", 4), ("V", 5)]
NU = len(UNITS)
SLOTS = [0, 2, 3, 4, 6, 7, 8, 10, 11, 12, 14, 15, 16, 17]
STEPS = NH + 2
UNIT_AT = {s: u for u, s in enumerate(SLOTS)}
K_UNIT = {(u[1], u[2]): n for n, u in enumerate(UNITS) if u[0] == "K"}


def build(nc, a):
    fp32, fp16, u32 = mybir.dt.float32, mybir.dt.float16, mybir.dt.uint32
    ALU = mybir.AluOpType
    ACT = mybir.ActivationFunctionType
    AX = mybir.AxisListType

    ctx = ExitStack()
    with ctx:
        def sb(name, shape, dt=fp32):
            return ctx.enter_context(nc.sbuf_tensor(name, shape, dt))

        def sem(name):
            return ctx.enter_context(nc.semaphore(name))

        x = sb("x", [P, NB, D])
        tok = sb("tok", [P, NB, D])
        xT = sb("xT", [P, 2, C, NT], fp16)
        xTf = sb("xTf", [P, C, NT])
        yT = xTf
        QT = xTf[:, :, :].rearrange("p c t -> p (c t)").bitcast(fp16).rearrange(
            "p (s c t) -> p s c t", s=2, c=C)
        W = sb("W", [P, 4, 2, C, D], fp16)
        ident = sb("ident", [P, P])
        eid = sb("eid", [P, NB, NE])
        gateT = sb("gateT", [P, 2, C, NE])
        bal = sb("bal", [P, NB, NE])
        bvB = sb("bvB", [P, D])
        boB = sb("boB", [P, D])
        padB = sb("padB", [P, 2, D], fp16)
        ones = sb("ones", [P, HALF_T], fp16)
        lnsT = sb("lnsT", [P, C, NE])
        lnbT = sb("lnbT", [P, C, NE])
        b1T = sb("b1T", [P, NE])
        biasH = sb("biasH", [P, NE])
        bst = sb("bst", [P, NB, 6])
        mv = sb("mv", [P, NB, 2])
        ve = sb("ve", [P, NB])
        sd = sb("sd", [P, NB])
        rstd = sb("rstd", [P, NB])
        red = sb("red", [P, NH // 2, DH])
        redm = sb("redm", [P, NH // 2, DH])
        rowsum = sb("rowsum", [P, 2, NH])
        rrec = sb("rrec", [P, NH // 2])
        negmax = sb("negmax", [P, 2])

        AREA = 26688
        arena = sb("arena", [P, AREA])
        at = [0]

        def part(words, dt=fp32):
            v = arena[:, at[0]:at[0] + words]
            at[0] += words
            return v if dt == fp32 else v.bitcast(dt)

        ctxF = part(C * NK).rearrange("p (c n) -> p c n", c=C)
        ctxH = [part(C * NK, fp16).rearrange("p (s c n) -> p s c n", s=2, c=C) for _ in range(2)]
        KT = [part(NK, fp16).rearrange("p (s n) -> p s n", s=2) for _ in range(2)]
        stage_at = at[0]
        Kst = part(NH * NK // 2, fp16).rearrange("p (h n) -> p h n", h=NH)
        V = [part(KT_TILES * NH * DH, fp16).rearrange("p (t h s d) -> p t h s d", t=KT_TILES, h=NH, s=2)
             for _ in range(2)]
        Qst = [part(NH * TQ // 2, fp16).rearrange("p (h q) -> p h q", h=NH) for _ in range(2)]
        Pr = [part(KT_TILES * P) for _ in range(2)]
        PT = [part(KT_TILES * TQ, fp16).rearrange("p (s t q) -> p s t q", s=2, t=KT_TILES) for _ in range(2)]
        assert at[0] <= AREA
        Wf = arena[:, stage_at:stage_at + 4 * C * D].rearrange("p (w c n) -> p w c n", w=4, c=C)

        at[0] = 0
        wf = part(C * HID0)
        w1 = part(C * HID0, fp16).rearrange("p (s c n) -> p s c n", s=2, c=C)
        hs = [part(HALF_T) for _ in range(2)]
        hp = [part(HALF_T) for _ in range(2)]
        assert at[0] <= stage_at
        hc = part(HT * NT, fp16).rearrange("p (s j t) -> p s j t", s=2, j=HT)
        comb = part(NE * NT).rearrange("p (e t) -> p e t", e=NE)
        w2 = part(C * HID0, fp16).rearrange("p (s j n) -> p s j n", s=2, j=HT)
        assert at[0] <= AREA
        wf1 = wf.rearrange("p (c n) -> p c n", c=C)
        at[0] = 2 * C * HID0
        g_e = part(NB * NE).rearrange("p (b e) -> p b e", b=NB)
        g_s = part(NB * NE).rearrange("p (b e) -> p b e", b=NB)
        g_m = part(NB * 8).rearrange("p (b e) -> p b e", b=NB)
        g_i = part(NB * 8, u32).rearrange("p (b e) -> p b e", b=NB)
        g_f = part(NB * 8).rearrange("p (b e) -> p b e", b=NB)
        g_1 = part(NB * NE).rearrange("p (b e) -> p b e", b=NB)
        g_2 = part(NB * NE).rearrange("p (b e) -> p b e", b=NB)
        g_c = part(NB * NE).rearrange("p (b e) -> p b e", b=NB)
        g_n = part(NB)
        Wflat = W[:, :, :, :, :].rearrange("p w s c n -> p (w s c n)")
        b2f = Wflat[:, 0:2 * D].bitcast(fp32)
        b2h = Wflat[:, 2 * D:4 * D].rearrange("p (s n) -> p s n", s=2)
        maskT = Wflat[:, 4 * D:4 * D + NT]
        biasF = tok[:, 0:2, :]
        biasHi = tok[:, 2, :].bitcast(fp16).rearrange("p (s n) -> p s n", s=2)

        psum = ctx.enter_context(nc.psum_tensor("psum", [P, 8, 512], fp32))
        S_BANK, T_BANK, O_BANK, J_BANK = 0, 2, 4, 6

        x_in, ident_in, small_in, bias_in = sem("x_in"), sem("ident_in"), sem("small_in"), sem("bias_in")
        w_in = [sem(f"w_in{k}") for k in range(4)]
        w_hi, w_split = sem("w_hi"), sem("w_split")
        const_set, bias_split, pad_set = sem("const_set"), sem("bias_split"), sem("pad_set")
        ln_chain, ln_var, ln_sd, ln_out = sem("ln_chain"), sem("ln_var"), sem("ln_sd"), sem("ln_out")
        ts_ps, ts_hi, ts_lo = sem("ts_ps"), sem("ts_hi"), sem("ts_lo")
        q_ps, q_hi, q_lo = sem("q_ps"), sem("q_hi"), sem("q_lo")
        qst_in = [sem(f"qst_in{k}") for k in range(2)]
        kst_in = [sem(f"kst_in{g}") for g in range(C)]
        ctx_in, ctx_begun, ctx_hi, ctx_split = sem("ctx_in"), sem("ctx_begun"), sem("ctx_hi"), sem("ctx_split")
        proj_ps, proj_hi, proj_lo = sem("proj_ps"), sem("proj_hi"), sem("proj_lo")
        scores, maxed, probs = sem("scores"), sem("maxed"), sem("probs")
        probsT, pt_hi, pt_lo = sem("probsT"), sem("pt_hi"), sem("pt_lo")
        pv, norm_chain, attn_out = sem("pv"), sem("norm_chain"), sem("attn_out")
        o_ps, o_add, bo_add = sem("o_ps"), sem("o_add"), sem("bo_add")
        g_ps, g_neg, g_exp, g_chain, g_done = sem("g_ps"), sem("g_neg"), sem("g_exp"), sem("g_chain"), sem("g_done")
        comb_ps, comb_out = sem("comb_ps"), sem("comb_out")
        wf_in, fw_hi, fw_split = sem("wf_in"), sem("fw_hi"), sem("fw_split")
        h_ps, h_act, h_mul, h_hi, h_lo = sem("h_ps"), sem("h_act"), sem("h_mul"), sem("h_hi"), sem("h_lo")
        y_ps, y_add, y_zero, yt_ps, x_new = sem("y_ps"), sem("y_add"), sem("y_zero"), sem("yt_ps"), sem("x_new")
        b2_in, b2_hi, b2_split, mask_ps, mask_out = (sem("b2_in"), sem("b2_hi"), sem("b2_split"), sem("mask_ps"),
                                                     sem("mask_out"))
        bh_ps, bh_out, w1_scaled = sem("bh_ps"), sem("bh_out"), sem("w1_scaled")
        out_written = sem("out_written")


        block = ctx.enter_context(nc.Block())

        @block.sync
        def _(sp):
            def load_weights(layer, k):
                sp.dma_start(Wf[:, k, :, :], a[("wk", "wv", "wq", "wo")[k] + str(layer)]).then_inc(w_in[k], 16)

            def apart():
                sp.wait_ge(x_in, 16)

            def load_ctx(b):
                sp.dma_start(ctxF[:, :, :], a["ctx"][bass.ds(b, 1), :, :, :].rearrange("o p c n -> p (o c) n"))\
                    .then_inc(ctx_in, 16)

            def stack_q(b, par):
                for r in range(4):
                    for j in range(4):
                        src = QT[32 * j:32 * j + 32, r // 2, :, bass.ds(b * TQ, TQ)]
                        sp.dma_start(Qst[par][32 * r:32 * r + 32, j:NH:4, :], src).then_inc(qst_in[par], 16)

            def stack_k(gb, g):
                sp.wait_ge(proj_lo, gb * NU + K_UNIT[(g, 1)] + 1)
                for r in range(4):
                    for j in range(4):
                        sp.dma_start(Kst[32 * r:32 * r + 32, 4 * g + j, :], KT[g % 2][32 * j:32 * j + 32, r % 2, :])\
                            .then_inc(kst_in[g], 16)

            sp.dma_start(x[0:TQ, :, :], a["x"]).then_inc(x_in, 16)
            sp.dma_start(ident[:, :], a["ident"]).then_inc(ident_in, 16)
            sp.dma_start(biasF[0:1, 0, :], a["bq"]).then_inc(bias_in, 16)
            sp.dma_start(biasF[0:1, 1, :], a["bk"]).then_inc(bias_in, 16)
            sp.dma_start(biasF[32:33, 0, :], a["bq"]).then_inc(bias_in, 16)
            sp.dma_start(biasF[32:33, 1, :], a["bk"]).then_inc(bias_in, 16)
            load_weights(0, 2)
            load_ctx(0)
            for k in (0, 1, 3):
                load_weights(0, k)
            sp.dma_start(eid[0:TQ, :, :], a["eid"].partition_broadcast(TQ)).then_inc(small_in, 16)
            sp.dma_start(gateT[:, 0, :, :], a["gate0"]).then_inc(small_in, 16)
            sp.dma_start(gateT[:, 1, :, :], a["gate1"]).then_inc(small_in, 16)
            for b in range(NB):
                sp.dma_start(bal[0:TQ, b, :], a["bal"].partition_broadcast(TQ)).then_inc(small_in, 16)
            sp.dma_start(bvB[0:TQ, :], a["bv"].partition_broadcast(TQ)).then_inc(small_in, 16)
            sp.dma_start(boB[0:TQ, :], a["bo"].partition_broadcast(TQ)).then_inc(small_in, 16)
            sp.dma_start(lnsT[:, :, :], a["lns"]).then_inc(small_in, 16)
            sp.dma_start(lnbT[:, :, :], a["lnb"]).then_inc(small_in, 16)
            sp.dma_start(b1T[:, :], a["b1"]).then_inc(small_in, 16)

            for layer in range(2):
                g0 = layer * NB
                if layer == 1:
                    sp.wait_ge(y_add, 8 * NE)
                    load_ctx(0)
                sp.wait_ge(ctx_split, g0 + 1)
                load_ctx(1)
                sp.wait_ge(q_lo, 8 * layer + 8)
                stack_q(0, 0)
                for g in range(C):
                    stack_k(g0, g)

                def step(b, gb, par, more, last):
                    if more:
                        sp.wait_ge(ctx_split, gb + 2)
                        apart()
                        load_ctx(b + 2)
                    if last:
                        return
                    stack_q(b + 1, 1 - par)
                    for g in range(C):
                        stack_k(gb + 1, g)

                with sp.Fori(0, 3) as i:
                    for par in range(2):
                        step(2 * i + par, g0 + 2 * i + par, par, True, False)
                step(NB - 2, g0 + NB - 2, 0, False, False)
                step(NB - 1, g0 + NB - 1, 1, False, True)

                if layer == 0:
                    sp.wait_ge(pv, NH * NB)
                    sp.dma_start(wf, a["w1_0"][0]).then_inc(wf_in, 16)
                    for k in (0, 1, 2, 3):
                        load_weights(1, k)
                    sp.wait_ge(fw_split, 1)
                    sp.dma_start(wf, a["w2_0"][0]).then_inc(wf_in, 16)
                    with sp.Fori(1, NE) as e:
                        sp.wait_ge(fw_split, 2 * e)
                        apart()
                        sp.dma_start(wf, a["w1_0"][bass.ds(e, 1), :, :].rearrange("o p n -> p (o n)"))\
                            .then_inc(wf_in, 16)
                        sp.wait_ge(fw_split, 2 * e + 1)
                        apart()
                        sp.dma_start(wf, a["w2_0"][bass.ds(e, 1), :, :].rearrange("o p n -> p (o n)"))\
                            .then_inc(wf_in, 16)
                else:
                    sp.wait_ge(pv, 2 * NH * NB)
                    sp.dma_start(wf, a["w1_1"]).then_inc(wf_in, 16)
                    sp.wait_ge(o_add, 2 * NB)
                    sp.dma_start(b2f[0:NE, :], a["b2"]).then_inc(b2_in, 16)
                    sp.wait_ge(fw_split, 2 * NE + 1)
                    sp.dma_start(wf, a["w2_1"]).then_inc(wf_in, 16)

            for b in range(NB):
                sp.wait_ge(x_new, NB + b + 1)
                sp.dma_start(a["out"][:, b, :], x[0:TQ, b, :]).then_inc(out_written, 16)
            sp.wait_ge(out_written, 16 * NB)

        @block.gpsimd
        def _(pool):
            def split_ctx(gb, par):
                pool.wait_ge(ctx_in, 16 * (gb + 1))
                pool.sem_inc(ctx_begun, 1)
                nc.gpsimd.tensor_copy(ctxH[par][:, 0, :, :], ctxF[:, :, :]).then_inc(ctx_hi, 1)
                pool.wait_ge(ctx_hi, gb + 1)
                nc.gpsimd.tensor_tensor(ctxH[par][:, 1, :, :], ctxF[:, :, :], ctxH[par][:, 0, :, :], ALU.subtract)\
                    .then_inc(ctx_split, 1)

            for layer in range(2):
                g0 = layer * NB
                split_ctx(g0, 0)
                split_ctx(g0 + 1, 1)
                with pool.Fori(0, 3) as i:
                    for par in range(2):
                        gb = g0 + 2 * i + par
                        pool.wait_ge(proj_ps, (gb + 1) * NU)
                        split_ctx(gb + 2, par)

        @block.tensor
        def _(pe):
            mm = nc.tensor.matmul

            def bank(k, rows, cols):
                return psum[0:rows, k, 0:cols]

            def transpose_rows(stage, ready, count):
                for b in range(NB):
                    pe.wait_ge(ready, count(b))
                    if b >= 2:
                        pe.wait_ge(ts_lo, NB * stage + b - 1)
                    for c in range(C):
                        last = nc.tensor.transpose(psum[:, T_BANK + b % 2, c * TQ:(c + 1) * TQ],
                                                   tok[0:TQ, b, c * P:(c + 1) * P], ident[0:TQ, 0:TQ])
                    last.then_inc(ts_ps, 1)

            def three(out, lhs, rhs, first=True, last=True):
                n = len(lhs)
                for c in range(n):
                    (lh, ll), (rh, rl) = lhs[c], rhs[c]
                    for k, (l_, r_) in enumerate(((lh, rh), (lh, rl), (ll, rh))):
                        ins = mm(out, l_, r_, start=first and c == 0 and k == 0,
                                 stop=last and c == n - 1 and k == 2)
                return ins

            def queries(layer):
                for u in range(2 * C):
                    g, half = u // 2, u % 2
                    if u == 0:
                        pe.wait_ge(w_split, 4 * layer + 1)
                        pe.wait_ge(ts_lo, NB * 3 * layer + NB)
                    if u >= 2:
                        pe.wait_ge(q_lo, 8 * layer + u - 1)
                    out = bank(J_BANK + u % 2, P, HALF_T)
                    if layer == 1:
                        mm(out, padB[:, 0, g * P:(g + 1) * P], ones[:, :], start=True, stop=False)
                    three(out, [(W[:, 2, 0, c, g * P:(g + 1) * P], W[:, 2, 1, c, g * P:(g + 1) * P]) for c in range(C)],
                          [tuple(xT[:, s, c, half * HALF_T:(half + 1) * HALF_T] for s in range(2)) for c in range(C)],
                          first=layer == 0).then_inc(q_ps, 1)

            def project(layer, gb, par, u, static_first=False):
                n = gb * NU + u
                if u == 0:
                    pe.wait_ge(ctx_split, gb + 1)
                if static_first and u < 2:
                    pe.wait_ge(q_lo, 8 * layer + 8)
                    pe.wait_ge(w_split, 4 * layer + 3)
                else:
                    pe.wait_ge(proj_lo, n - 1)
                k = J_BANK + u % 2
                if UNITS[u][0] == "K":
                    _, g, half = UNITS[u]
                    out = bank(k, P, HALF_K)
                    if layer == 1:
                        mm(out, padB[:, 1, g * P:(g + 1) * P], ones[:, 0:HALF_K], start=True, stop=False)
                    ins = three(
                        out, [(W[:, 0, 0, c, g * P:(g + 1) * P], W[:, 0, 1, c, g * P:(g + 1) * P]) for c in range(C)],
                        [tuple(ctxH[par][:, s, c, half * HALF_K:(half + 1) * HALF_K] for s in range(2))
                         for c in range(C)], first=layer == 0)
                else:
                    t = UNITS[u][1]
                    r = key_rows(t)
                    ins = three(
                        bank(k, r, D),
                        [tuple(ctxH[par][:, s, c, t * P:t * P + r] for s in range(2)) for c in range(C)],
                        [(W[:, 1, 0, c, :], W[:, 1, 1, c, :]) for c in range(C)])
                ins.then_inc(proj_ps, 1)

            def score(gb, par, h):
                if h % 4 == 0:
                    pe.wait_ge(kst_in[h // 4], 256 * (gb + 1))
                if h > 0:
                    pe.wait_ge(probs, gb * NH + h)
                for half in range(2):
                    last = mm(psum[0:TQ, S_BANK + half, 0:HALF_K], Qst[par][:, h, :],
                              Kst[:, h, half * HALF_K:(half + 1) * HALF_K], start=True, stop=True)
                last.then_inc(scores, 1)

            def probs_transpose(gb, h):
                pe.wait_ge(probs, gb * NH + h + 1)
                if h > 0:
                    pe.wait_ge(pt_lo, gb * NH + h)
                for t in range(KT_TILES):
                    last = nc.tensor.transpose(psum[:, T_BANK + t // 3, (t % 3) * TQ:(t % 3 + 1) * TQ],
                                               Pr[h % 2][0:TQ, t * P:(t + 1) * P], ident[0:TQ, 0:TQ])
                last.then_inc(probsT, 1)

            def values(gb, par, h):
                if h == 0:
                    pe.wait_ge(proj_lo, (gb + 1) * NU)
                pe.wait_ge(pt_lo, gb * NH + h + 1)
                half, k = h // 8, h % 8
                for t in range(KT_TILES):
                    r = key_rows(t)
                    for s in range(2):
                        last = mm(psum[0:TQ, O_BANK + half, k * 2 * DH:(k + 1) * 2 * DH],
                                  PT[h % 2][0:r, s, t, :],
                                  V[par][0:r, t, h, :, :].rearrange("p s d -> p (s d)"),
                                  start=t == 0 and s == 0, stop=t == KT_TILES - 1 and s == 1)
                last.then_inc(pv, 1)

            def attend(layer, gb, par, more):
                pe.wait_ge(qst_in[par], (gb // 2 + 1) * 256 if isinstance(gb, int) else (gb - par) * 128 + 256)
                for s in range(STEPS):
                    if s < NH:
                        score(gb, par, s)
                    if more and s in UNIT_AT:
                        project(layer, gb + 1, 1 - par, UNIT_AT[s])
                    if 1 <= s <= NH:
                        probs_transpose(gb, s - 1)
                    if s >= 2:
                        values(gb, par, s - 2)

            def output_rows(layer):
                for b in range(NB):
                    if b == 0:
                        pe.wait_ge(w_split, 4 * layer + 4)
                        pe.wait_ge(ts_lo, NB * (3 * layer + 1) + NB)
                    if b >= 2:
                        pe.wait_ge(o_add, NB * layer + b - 1)
                    three(bank(b % 2, TQ, D),
                          [tuple(xT[:, s, c, b * TQ:(b + 1) * TQ] for s in range(2)) for c in range(C)],
                          [(W[:, 3, 0, c, :], W[:, 3, 1, c, :]) for c in range(C)]).then_inc(o_ps, 1)

            def gate(layer):
                pe.wait_ge(ts_lo, NB * (3 * layer + 2) + NB)
                pe.wait_ge(small_in, 16 * 16)
                for b in range(NB):
                    for c in range(C):
                        last = mm(psum[0:TQ, O_BANK, b * NE:(b + 1) * NE], xTf[:, c, b * TQ:(b + 1) * TQ],
                                  gateT[:, layer, c, :], start=c == 0, stop=c == C - 1)
                last.then_inc(g_ps, 1)

            def spread_gates(layer):
                pe.wait_ge(g_done, layer + 1)
                for e in range(NE):
                    for half in range(2):
                        n = 2 * e + half
                        if n >= 2:
                            pe.wait_ge(comb_out, 16 * layer + n - 1)
                        for k in range(4):
                            b = 4 * half + k
                            last = mm(psum[:, n % 2, k * TQ:(k + 1) * TQ],
                                      g_c[0:TQ, b, e:e + 1].broadcast_to([TQ, P]), ident[0:TQ, 0:TQ],
                                      start=True, stop=True)
                        last.then_inc(comb_ps, 1)

            def expert(xe, first, layer):
                pe.wait_ge(fw_split, 2 * xe + 1)
                for n in range(2 * HT):
                    j, half = n // 2, n % 2
                    if not (first and n < 4):
                        pe.wait_ge(h_act, xe * 2 * HT + n - 3)
                    three(bank(n % 4, P, HALF_T),
                          [(w1[:, 0, c, j * P:(j + 1) * P], w1[:, 1, c, j * P:(j + 1) * P]) for c in range(C)],
                          [tuple(xT[:, s, c, half * HALF_T:(half + 1) * HALF_T] for s in range(2))
                           for c in range(C)]).then_inc(h_ps, 1)
                pe.wait_ge(fw_split, 2 * xe + 2)
                for u in range(2 * C):
                    m, half = u // 2, u % 2
                    if not (first and u < 4):
                        pe.wait_ge(y_add, xe * 2 * C + u - 3)
                    out = bank(4 + u % 4, P, HALF_T)
                    if layer == 1:
                        for s in range(2):
                            mm(out, b2h[0:NE, s, m * P:(m + 1) * P], maskT[0:NE, half * HALF_T:(half + 1) * HALF_T],
                               start=s == 0, stop=False)
                    for j in range(HT):
                        if m == 0:
                            pe.wait_ge(h_lo, xe * 2 * HT + 2 * j + half + 1)
                        ins = three(out, [(w2[:, 0, j, m * P:(m + 1) * P], w2[:, 1, j, m * P:(m + 1) * P])],
                                    [tuple(hc[:, s, j, half * HALF_T:(half + 1) * HALF_T] for s in range(2))],
                                    first=j == 0 and layer == 0, last=j == HT - 1)
                    ins.then_inc(y_ps, 1)

            def y_rows(layer):
                pe.wait_ge(y_add, 2 * C * (NE if layer == 0 else NE + 1))
                for b in range(NB):
                    if b >= 2:
                        pe.wait_ge(x_new, NB * layer + b - 1)
                    for c in range(C):
                        last = nc.tensor.transpose(psum[0:TQ, T_BANK + b % 2, c * P:(c + 1) * P],
                                                   yT[:, c, b * TQ:(b + 1) * TQ], ident[:, :])
                    last.then_inc(yt_ps, 1)

            pe.wait_ge(ident_in, 16)
            pe.wait_ge(const_set, 1)
            for layer in range(2):
                g0 = layer * NB
                transpose_rows(3 * layer, ln_out, lambda b: NB * 2 * layer + b + 1)
                queries(layer)
                for u in range(NU):
                    project(layer, g0, 0, u, static_first=True)
                pe.wait_ge(pad_set, layer + 1)
                with pe.Fori(0, 3) as i:
                    for par in range(2):
                        attend(layer, g0 + 2 * i + par, par, True)
                attend(layer, g0 + NB - 2, 0, True)
                attend(layer, g0 + NB - 1, 1, False)
                transpose_rows(3 * layer + 1, attn_out, lambda b: 2 * (NB * layer + b) + 2)
                output_rows(layer)
                transpose_rows(3 * layer + 2, ln_out, lambda b: NB * (2 * layer + 1) + b + 1)
                gate(layer)
                if layer == 1:
                    pe.wait_ge(wf_in, 16 * (2 * NE + 1))
                    for e in range(NE):
                        for c in range(C):
                            last = mm(psum[:, O_BANK + 1, e:e + 1], wf1[:, c, e * P:(e + 1) * P],
                                      lnbT[:, c, e:e + 1], start=c == 0, stop=c == C - 1)
                    last.then_inc(bh_ps, 1)
                spread_gates(layer)
                if layer == 0:
                    pe.wait_ge(y_zero, 1)
                    expert(0, True, 0)
                    with pe.Fori(1, NE) as e:
                        expert(e, False, 0)
                else:
                    for half in range(2):
                        for k in range(4):
                            b = 4 * half + k
                            last = mm(psum[0:NE, 6 + half, k * TQ:(k + 1) * TQ], g_c[0:TQ, b, :], ident[0:TQ, 0:TQ],
                                      start=True, stop=True)
                        last.then_inc(mask_ps, 1)
                    pe.wait_ge(mask_out, 2)
                    pe.wait_ge(b2_split, 1)
                    pe.wait_ge(y_zero, 2)
                    pe.wait_ge(comb_out, 32)
                    expert(NE, True, 1)
                y_rows(layer)

        @block.scalar
        def _(act):
            def split_weight(layer, idx, k):
                act.wait_ge(w_in[k], 16 * (layer + 1))
                nc.scalar.activation(W[:, k, 0, :, :], Wf[:, k, :, :], ACT.Copy, scale=W_SCALE).then_inc(w_hi, 1)

            def layernorm_root(n):
                act.wait_ge(ln_var, n + 1)
                nc.scalar.activation(sd[0:TQ, :], ve[0:TQ, :], ACT.Sqrt).then_inc(ln_sd, 1)

            def transposed_high(stage, keep):
                for b in range(NB):
                    act.wait_ge(ts_ps, NB * stage + b + 1)
                    src = psum[:, T_BANK + b % 2, 0:C * TQ].rearrange("p (c t) -> p c t", c=C)
                    if keep:
                        nc.scalar.activation(xTf[:, :, b * TQ:(b + 1) * TQ], src, ACT.Copy)
                    nc.scalar.activation(xT[:, 0, :, b * TQ:(b + 1) * TQ], src, ACT.Copy).then_inc(ts_hi, 1)

            def queries_high(layer):
                for u in range(2 * C):
                    g, half = u // 2, u % 2
                    act.wait_ge(q_ps, 8 * layer + u + 1)
                    nc.scalar.activation(QT[:, 0, g, half * HALF_T:(half + 1) * HALF_T],
                                         psum[:, J_BANK + u % 2, 0:HALF_T], ACT.Copy, scale=Q_UNSCALE)\
                        .then_inc(q_hi, 1)

            def unit_high(gb, par, u, static_first=False):
                act.wait_ge(proj_ps, gb * NU + u + 1)
                k = J_BANK + u % 2
                if UNITS[u][0] == "K":
                    _, g, half = UNITS[u]
                    if half == 0 and g >= 2:
                        act.wait_ge(kst_in[g - 2], 256 * (gb + 1))
                    elif half == 0 and not static_first:
                        act.wait_ge(kst_in[g + 2], 256 * gb)
                    out, src = KT[g % 2][:, 0, half * HALF_K:(half + 1) * HALF_K], psum[:, k, 0:HALF_K]
                else:
                    t = UNITS[u][1]
                    r = key_rows(t)
                    out, src = V[par][0:r, t, :, 0, :], psum[0:r, k, :].rearrange("p (h d) -> p h d", h=NH)
                nc.scalar.activation(out, src, ACT.Copy, scale=UNSCALE).then_inc(proj_hi, 1)

            def probabilities(gb, par, h):
                act.wait_ge(maxed, gb * NH + h + 1)
                nc.scalar.activation(Pr[h % 2][0:TQ, 0:NK].rearrange("q (s n) -> q s n", s=2),
                                     psum[0:TQ, S_BANK:S_BANK + 2, 0:HALF_K], ACT.Exp,
                                     bias=negmax[0:TQ, h % 2:h % 2 + 1],
                                     accum_out=rowsum[0:TQ, par, h:h + 1]).then_inc(probs, 1)

            def probsT_high(gb, h):
                act.wait_ge(probsT, gb * NH + h + 1)
                if h >= 2:
                    act.wait_ge(pv, gb * NH + h - 1)
                nc.scalar.activation(PT[h % 2][:, 0, :, :].rearrange("p (s t) q -> p s (t q)", s=2),
                                     psum[:, T_BANK:T_BANK + 2, 0:3 * TQ], ACT.Copy).then_inc(pt_hi, 1)

            def attend(gb, par, more):
                for s in range(STEPS + 1):
                    if 2 <= s < NH + 2:
                        probsT_high(gb, s - 2)
                    if more and s - 1 in UNIT_AT:
                        unit_high(gb + 1, 1 - par, UNIT_AT[s - 1])
                    if s < NH:
                        probabilities(gb, par, s)

            def weight_pieces(xe, which, k, out, src):
                act.wait_ge(wf_in, 16 * (2 * xe + which + 1))
                nc.scalar.activation(out, src, ACT.Copy, scale=W_SCALE).then_inc(fw_hi, 1)

            def expert(xe, first, layer):
                for k in range(C):
                    if layer == 1 and k == 0:
                        act.wait_ge(w1_scaled, 1)
                    weight_pieces(xe, 0, k, w1[:, 0, k, :], wf1[:, k, :])

                def high(n):
                    j, half = n // 2, n % 2
                    act.wait_ge(h_mul, xe * 2 * HT + n + 1)
                    nc.scalar.activation(hc[:, 0, j, half * HALF_T:(half + 1) * HALF_T], hp[n % 2], ACT.Copy)\
                        .then_inc(h_hi, 1)

                for n in range(2 * HT):
                    j = n // 2
                    act.wait_ge(h_ps, xe * 2 * HT + n + 1)
                    if not (first and n < 2):
                        act.wait_ge(h_mul, xe * 2 * HT + n - 1)
                    if layer == 0:
                        nc.scalar.activation(hs[n % 2], psum[:, n % 4, 0:HALF_T], ACT.Silu, scale=UNSCALE)\
                            .then_inc(h_act, 1)
                    else:
                        if n == 0:
                            act.wait_ge(bh_out, 1)
                        nc.scalar.activation(hs[n % 2], psum[:, n % 4, 0:HALF_T], ACT.Gelu, scale=UNSCALE,
                                             bias=biasH[:, j:j + 1]).then_inc(h_act, 1)
                    if n >= 1:
                        high(n - 1)
                    if n >= 8 and n % 2 == 0:
                        k = n // 2 - 4
                        weight_pieces(xe, 1, k, w2[:, 0, 2 * k:2 * k + 2, :],
                                      wf[:, 2 * k * D:(2 * k + 2) * D].rearrange("p (j n) -> p j n", j=2))
                high(2 * HT - 1)

            for layer in range(2):
                g0 = layer * NB
                if layer == 0:
                    split_weight(0, 0, 2)
                layernorm_root(2 * layer)
                transposed_high(3 * layer, False)
                queries_high(layer)
                if layer == 0:
                    split_weight(0, 1, 0)
                    split_weight(0, 2, 1)
                    split_weight(0, 3, 3)
                act.wait_ge(w_split, 4 * layer + 4)
                for u in range(NU):
                    unit_high(g0, 0, u, static_first=True)
                with act.Fori(0, 3) as i:
                    for par in range(2):
                        attend(g0 + 2 * i + par, par, True)
                attend(g0 + NB - 2, 0, True)
                attend(g0 + NB - 1, 1, False)
                transposed_high(3 * layer + 1, False)
                if layer == 0:
                    act.wait_ge(pv, NH * NB)
                    for n, k in enumerate((2, 0, 1)):
                        split_weight(1, n, k)
                    act.wait_ge(o_ps, NB)
                    split_weight(1, 3, 3)
                layernorm_root(2 * layer + 1)
                transposed_high(3 * layer + 2, True)
                if layer == 0:
                    act.wait_ge(g_neg, 1)
                    nc.scalar.activation(g_e[0:TQ, :, :], g_e[0:TQ, :, :], ACT.Exp, scale=-1.0).then_inc(g_exp, 1)
                else:
                    act.wait_ge(b2_in, 16)
                    nc.scalar.activation(b2h[0:NE, 0, :], b2f[0:NE, :], ACT.Copy, scale=W_SCALE).then_inc(b2_hi, 1)
                for n in range(2 * NE):
                    e, half = n // 2, n % 2
                    act.wait_ge(comb_ps, 16 * layer + n + 1)
                    nc.scalar.activation(comb[:, e, half * HALF_T:(half + 1) * HALF_T], psum[:, n % 2, 0:HALF_T],
                                         ACT.Copy).then_inc(comb_out, 1)
                if layer == 0:
                    expert(0, True, 0)
                    with act.Fori(1, NE) as e:
                        expert(e, False, 0)
                else:
                    for half in range(2):
                        act.wait_ge(mask_ps, half + 1)
                        nc.scalar.activation(maskT[0:NE, half * HALF_T:(half + 1) * HALF_T],
                                             psum[0:NE, 6 + half, 0:HALF_T], ACT.Copy).then_inc(mask_out, 1)
                    expert(NE, True, 1)

        @block.vector
        def _(dve):
            v = nc.vector

            def low(out, src, scale, high):
                return v.scalar_tensor_tensor(out, src, scale, high, ALU.mult, ALU.subtract)

            def split_weight(layer, idx, k):
                dve.wait_ge(w_hi, 4 * layer + idx + 1)
                low(W[:, k, 1, :, :].rearrange("p c n -> p (c n)"), Wf[:, k, :, :].rearrange("p c n -> p (c n)"),
                    W_SCALE, W[:, k, 0, :, :].rearrange("p c n -> p (c n)")).then_inc(w_split, 1)

            def layernorm(n, ready, count):
                for b in range(NB):
                    if ready is not None:
                        dve.wait_ge(ready, count(b))
                    last = v.bn_stats(bst[0:TQ, b, :], x[0:TQ, b, :])
                last.then_inc(ln_chain, 1)
                dve.wait_ge(ln_chain, 3 * n + 1)
                for b in range(NB):
                    last = v.bn_aggr(mv[0:TQ, b, :], bst[0:TQ, b, :])
                last.then_inc(ln_chain, 1)
                dve.wait_ge(ln_chain, 3 * n + 2)
                v.tensor_scalar(ve[0:TQ, :], mv[0:TQ, :, 1], LN_EPS, None, ALU.add).then_inc(ln_var, 1)
                dve.wait_ge(ln_sd, n + 1)
                v.reciprocal(rstd[0:TQ, :], sd[0:TQ, :]).then_inc(ln_chain, 1)
                dve.wait_ge(ln_chain, 3 * n + 3)
                for b in range(NB):
                    v.tensor_scalar(tok[0:TQ, b, :], x[0:TQ, b, :], mv[0:TQ, b, 0:1], rstd[0:TQ, b:b + 1],
                                    ALU.subtract, ALU.mult).then_inc(ln_out, 1)

            def transposed_low(stage):
                for b in range(NB):
                    dve.wait_ge(ts_hi, NB * stage + b + 1)
                    src = psum[:, T_BANK + b % 2, 0:C * TQ].rearrange("p (c t) -> p c t", c=C)
                    low(xT[:, 1, :, b * TQ:(b + 1) * TQ], src, 1.0, xT[:, 0, :, b * TQ:(b + 1) * TQ]).then_inc(ts_lo, 1)

            def queries_low(layer):
                for u in range(2 * C):
                    g, half = u // 2, u % 2
                    dve.wait_ge(q_hi, 8 * layer + u + 1)
                    cols = slice(half * HALF_T, (half + 1) * HALF_T)
                    low(QT[:, 1, g, cols], psum[:, J_BANK + u % 2, 0:HALF_T], Q_UNSCALE, QT[:, 0, g, cols])\
                        .then_inc(q_lo, 1)

            def unit_low(gb, par, u):
                dve.wait_ge(proj_hi, gb * NU + u + 1)
                k = J_BANK + u % 2
                if UNITS[u][0] == "K":
                    _, g, half = UNITS[u]
                    cols = slice(half * HALF_K, (half + 1) * HALF_K)
                    low(KT[g % 2][:, 1, cols], psum[:, k, 0:HALF_K], UNSCALE, KT[g % 2][:, 0, cols])\
                        .then_inc(proj_lo, 1)
                else:
                    t = UNITS[u][1]
                    r = key_rows(t)
                    low(V[par][0:r, t, :, 1, :], psum[0:r, k, :].rearrange("p (h d) -> p h d", h=NH), UNSCALE,
                        V[par][0:r, t, :, 0, :]).then_inc(proj_lo, 1)

            def row_max(gb, h):
                dve.wait_ge(scores, gb * NH + h + 1)
                v.tensor_reduce(negmax[0:TQ, h % 2:h % 2 + 1], psum[0:TQ, S_BANK:S_BANK + 2, 0:HALF_K], AX.XY, ALU.max,
                                negate=True).then_inc(maxed, 1)

            def probsT_low(gb, h):
                dve.wait_ge(pt_hi, gb * NH + h + 1)
                low(PT[h % 2][:, 1, :, :].rearrange("p (s t) q -> p s (t q)", s=2),
                    psum[:, T_BANK:T_BANK + 2, 0:3 * TQ], 1.0,
                    PT[h % 2][:, 0, :, :].rearrange("p (s t) q -> p s (t q)", s=2)).then_inc(pt_lo, 1)

            def normalise(layer, b, gb, par, half):
                n = 2 * gb + half
                dve.wait_ge(pv, gb * NH + 8 * half + 8)
                v.reciprocal(rrec[0:TQ, :], rowsum[0:TQ, par, 8 * half:8 * half + 8]).then_inc(norm_chain, 1)
                v.tensor_reduce(red[0:TQ, :, :], psum[0:TQ, O_BANK + half, :].rearrange("q (h s d) -> q h d s", h=8, s=2),
                                AX.X, ALU.add).then_inc(norm_chain, 1)
                base = 2 * n if layer == 0 else 4 * NB + 3 * (n - 2 * NB)
                dve.wait_ge(norm_chain, base + 2)
                scale = rrec[0:TQ, :].unsqueeze(2).broadcast_to([TQ, 8, DH])
                w = D // 2
                out = tok[0:TQ, bass.ds(b, 1), half * w:(half + 1) * w].rearrange("q o (h d) -> q (o h) d", h=8)
                if layer == 0:
                    v.tensor_tensor(out, red[0:TQ, :, :], scale, ALU.mult).then_inc(attn_out, 1)
                else:
                    v.tensor_tensor(redm[0:TQ, :, :], red[0:TQ, :, :], scale, ALU.mult).then_inc(norm_chain, 1)
                    dve.wait_ge(norm_chain, base + 3)
                    v.tensor_tensor(out, redm[0:TQ, :, :],
                                    bvB[0:TQ, half * w:(half + 1) * w].rearrange("q (h d) -> q h d", h=8), ALU.add)\
                        .then_inc(attn_out, 1)

            def attend(layer, b, gb, par, more):
                for s in range(STEPS + 1):
                    if s < NH:
                        row_max(gb, s)
                    if 2 <= s < NH + 2:
                        probsT_low(gb, s - 2)
                    if more and s - 1 in UNIT_AT:
                        unit_low(gb + 1, 1 - par, UNIT_AT[s - 1])
                    if s == 11:
                        normalise(layer, b, gb, par, 0)
                normalise(layer, b, gb, par, 1)

            def output_add(layer):
                for b in range(NB):
                    dve.wait_ge(o_ps, NB * layer + b + 1)
                    v.scalar_tensor_tensor(x[0:TQ, b, :], psum[0:TQ, b % 2, :], UNSCALE, x[0:TQ, b, :],
                                           ALU.mult, ALU.add).then_inc(o_add, 1)

            def find_top(n, src):
                for b in range(NB):
                    last = v.max(g_m[0:TQ, b, :], src[0:TQ, b, :])
                last.then_inc(g_chain, 1)
                dve.wait_ge(g_chain, n + 1)
                for b in range(NB):
                    last = v.max_index(g_i[0:TQ, b, :], g_m[0:TQ, b, :], src[0:TQ, b, :])
                last.then_inc(g_chain, 1)
                dve.wait_ge(g_chain, n + 2)
                v.tensor_copy(g_f[0:TQ, :, :], g_i[0:TQ, :, :]).then_inc(g_chain, 1)
                dve.wait_ge(g_chain, n + 3)

            def route_two():
                dve.wait_ge(g_ps, 1)
                v.tensor_tensor(g_e[0:TQ, :, :], psum[0:TQ, O_BANK, 0:NB * NE].rearrange("q (b e) -> q b e", b=NB),
                                bal[0:TQ, :, :], ALU.add).then_inc(g_neg, 1)
                dve.wait_ge(g_exp, 1)
                v.tensor_scalar(g_1[0:TQ, :, :], g_e[0:TQ, :, :], 1.0, None, ALU.add).then_inc(g_chain, 1)
                dve.wait_ge(g_chain, 1)
                v.reciprocal(g_s[0:TQ, :, :], g_1[0:TQ, :, :]).then_inc(g_chain, 1)
                dve.wait_ge(g_chain, 2)
                find_top(2, g_s)
                v.tensor_tensor(g_1[0:TQ, :, :], eid[0:TQ, :, :], g_f[0:TQ, :, 0:1].broadcast_to([TQ, NB, NE]),
                                ALU.is_equal).then_inc(g_chain, 1)
                v.tensor_tensor(g_2[0:TQ, :, :], eid[0:TQ, :, :], g_f[0:TQ, :, 1:2].broadcast_to([TQ, NB, NE]),
                                ALU.is_equal).then_inc(g_chain, 1)
                v.tensor_tensor(g_n[0:TQ, :], g_m[0:TQ, :, 0], g_m[0:TQ, :, 1], ALU.add).then_inc(g_chain, 1)
                dve.wait_ge(g_chain, 8)
                v.tensor_tensor(g_c[0:TQ, :, :], g_1[0:TQ, :, :], g_2[0:TQ, :, :], ALU.add).then_inc(g_chain, 1)
                v.tensor_scalar(g_n[0:TQ, :], g_n[0:TQ, :], 1e-6, None, ALU.add).then_inc(g_chain, 1)
                dve.wait_ge(g_chain, 10)
                v.tensor_tensor(g_1[0:TQ, :, :], g_c[0:TQ, :, :], g_s[0:TQ, :, :], ALU.mult).then_inc(g_chain, 1)
                v.reciprocal(g_m[0:TQ, :, 0], g_n[0:TQ, :]).then_inc(g_chain, 1)
                dve.wait_ge(g_chain, 12)
                v.tensor_tensor(g_c[0:TQ, :, :], g_1[0:TQ, :, :], g_m[0:TQ, :, 0:1].broadcast_to([TQ, NB, NE]),
                                ALU.mult).then_inc(g_done, 1)

            def route_one():
                dve.wait_ge(g_ps, 2)
                v.tensor_copy(g_s[0:TQ, :, :], psum[0:TQ, O_BANK, 0:NB * NE].rearrange("q (b e) -> q b e", b=NB))\
                    .then_inc(g_chain, 1)
                dve.wait_ge(g_chain, 13)
                find_top(13, g_s)
                v.tensor_tensor(g_c[0:TQ, :, :], eid[0:TQ, :, :], g_f[0:TQ, :, 0:1].broadcast_to([TQ, NB, NE]),
                                ALU.is_equal).then_inc(g_done, 1)

            def y_piece(xe, u):
                m, half = u // 2, u % 2
                dve.wait_ge(y_ps, xe * 2 * C + u + 1)
                cols = slice(half * HALF_T, (half + 1) * HALF_T)
                v.scalar_tensor_tensor(yT[:, m, cols], psum[:, 4 + u % 4, 0:HALF_T], UNSCALE, yT[:, m, cols],
                                       ALU.mult, ALU.add).then_inc(y_add, 1)

            def expert(xe, first, layer):
                for k in range(C):
                    dve.wait_ge(fw_hi, 8 * xe + k + 1)
                    last = low(w1[:, 1, k, :], wf1[:, k, :], W_SCALE, w1[:, 0, k, :])
                    if k == C - 1:
                        last.then_inc(fw_split, 1)
                    if not first:
                        y_piece(xe - 1, 2 * k)
                        y_piece(xe - 1, 2 * k + 1)

                def low_half(n):
                    j, half = n // 2, n % 2
                    cols = slice(half * HALF_T, (half + 1) * HALF_T)
                    dve.wait_ge(h_hi, xe * 2 * HT + n + 1)
                    v.tensor_tensor(hc[:, 1, j, cols], hp[n % 2], hc[:, 0, j, cols], ALU.subtract).then_inc(h_lo, 1)

                for n in range(2 * HT):
                    j, half = n // 2, n % 2
                    dve.wait_ge(h_act, xe * 2 * HT + n + 1)
                    cols = slice(half * HALF_T, (half + 1) * HALF_T)
                    g = comb[:, j, cols] if layer == 1 else \
                        comb[:, bass.ds(xe, 1), cols].rearrange("p o t -> p (o t)")
                    if not (first and n < 2):
                        dve.wait_ge(h_lo, xe * 2 * HT + n - 1)
                    v.tensor_tensor(hp[n % 2], hs[n % 2], g, ALU.mult).then_inc(h_mul, 1)
                    if n >= 1:
                        low_half(n - 1)
                    if n >= 9 and n % 2 == 1:
                        k = (n - 9) // 2
                        dve.wait_ge(fw_hi, 8 * xe + 4 + k + 1)
                        last = low(w2[:, 1, 2 * k:2 * k + 2, :].rearrange("p j n -> p (j n)"),
                                   wf[:, 2 * k * D:(2 * k + 2) * D], W_SCALE,
                                   w2[:, 0, 2 * k:2 * k + 2, :].rearrange("p j n -> p (j n)"))
                        if k == C - 1:
                            last.then_inc(fw_split, 1)
                low_half(2 * HT - 1)

            def x_update(layer):
                for b in range(NB):
                    dve.wait_ge(yt_ps, NB * layer + b + 1)
                    v.tensor_tensor(x[0:TQ, b, :], psum[0:TQ, T_BANK + b % 2, :], x[0:TQ, b, :], ALU.add)\
                        .then_inc(x_new, 1)

            v.memset(padB[:, :, :], 0.0).then_inc(bias_split, 1)
            v.memset(ones[:, :], 1.0).then_inc(const_set, 1)
            dve.wait_ge(bias_in, 64)
            dve.wait_ge(bias_split, 1)
            v.tensor_scalar(padB[0:1, :, :], biasF[0:1, :, :], W_SCALE, None, ALU.mult)
            v.tensor_scalar(biasHi[32:33, :, :], biasF[32:33, :, :], W_SCALE, None, ALU.mult).then_inc(bias_split, 1)
            dve.wait_ge(bias_split, 2)
            low(padB[32:33, :, :], biasF[32:33, :, :], W_SCALE, biasHi[32:33, :, :]).then_inc(bias_split, 1)
            dve.wait_ge(bias_split, 3)
            dve.wait_ge(x_in, 16)

            for layer in range(2):
                g0 = layer * NB
                layernorm(2 * layer, None if layer == 0 else x_new, lambda b: b + 1)
                if layer == 0:
                    split_weight(0, 0, 2)
                transposed_low(3 * layer)
                queries_low(layer)
                if layer == 0:
                    for n, k in enumerate((0, 1, 3)):
                        split_weight(0, n + 1, k)
                for u in range(NU):
                    unit_low(g0, 0, u)
                for k in range(2):
                    last = v.memset(Pr[k][0:TQ, NK:KT_TILES * P], 0.0)
                last.then_inc(pad_set, 1)
                with dve.Fori(0, 3) as i:
                    for par in range(2):
                        attend(layer, 2 * i + par, g0 + 2 * i + par, par, True)
                attend(layer, NB - 2, g0 + NB - 2, 0, True)
                attend(layer, NB - 1, g0 + NB - 1, 1, False)
                transposed_low(3 * layer + 1)
                if layer == 0:
                    for n, k in enumerate((2, 0, 1)):
                        split_weight(1, n, k)
                output_add(layer)
                if layer == 1:
                    dve.wait_ge(o_add, 2 * NB)
                    for b in range(NB):
                        last = v.tensor_tensor(x[0:TQ, b, :], x[0:TQ, b, :], boB[0:TQ, :], ALU.add)
                    last.then_inc(bo_add, 1)
                if layer == 0:
                    split_weight(1, 3, 3)
                layernorm(2 * layer + 1, o_add if layer == 0 else bo_add, lambda b: b + 1 if layer == 0 else 1)
                transposed_low(3 * layer + 2)
                if layer == 0:
                    route_two()
                else:
                    route_one()
                    dve.wait_ge(bh_ps, 1)
                    v.tensor_tensor(biasH[:, :], psum[:, O_BANK + 1, 0:NE], b1T[:, :], ALU.add).then_inc(bh_out, 1)
                    for c in range(C):
                        w = wf1[:, c, :].rearrange("p (e n) -> p e n", e=NE)
                        last = v.tensor_tensor(w, w, lnsT[:, c, :].unsqueeze(2).broadcast_to([P, NE, P]), ALU.mult)
                    last.then_inc(w1_scaled, 1)
                    dve.wait_ge(w1_scaled, 1)
                    dve.wait_ge(b2_hi, 1)
                    low(b2h[0:NE, 1, :], b2f[0:NE, :], W_SCALE, b2h[0:NE, 0, :]).then_inc(b2_split, 1)
                v.memset(yT[:, :, :], 0.0).then_inc(y_zero, 1)
                dve.wait_ge(y_zero, layer + 1)
                dve.wait_ge(comb_out, 16 * (layer + 1))
                if layer == 0:
                    expert(0, True, 0)
                    with dve.Fori(1, NE) as e:
                        expert(e, False, 0)
                    for u in range(2 * C):
                        y_piece(NE - 1, u)
                else:
                    expert(NE, True, 1)
                    for u in range(2 * C):
                        y_piece(NE, u)
                x_update(layer)


def kernel(x, ctx_1024, L0_xattn_w_q, L0_xattn_w_k, L0_xattn_w_v, L0_xattn_w_o, L0_ffn_gate_w,
           L0_ffn_balance_bias, L0_ffn_w1, L0_ffn_w2, L1_xattn_Wq, L1_xattn_bq, L1_xattn_Wk, L1_xattn_bk,
           L1_xattn_Wv, L1_xattn_bv, L1_xattn_Wo, L1_xattn_bo, L1_ffn_Wg, L1_ffn_ln_scale, L1_ffn_ln_bias,
           L1_ffn_W1, L1_ffn_b1, L1_ffn_W2, L1_ffn_b2):
    import concourse.bacc as bacc
    from concourse.bass_utils import run_bass_kernel_spmd

    def chunks(w):
        w = np.asarray(w)
        return w.reshape(-1, P, w.shape[-1]).transpose(1, 0, 2)

    w1_0, w2_0 = np.asarray(L0_ffn_w1), np.asarray(L0_ffn_w2)
    arrays = {
        "x": np.asarray(x).transpose(1, 0, 2),
        "ctx": np.asarray(ctx_1024).transpose(0, 2, 1).reshape(NB, C, P, NK).transpose(0, 2, 1, 3),
        "wq0": chunks(np.asarray(L0_xattn_w_q).T), "wk0": chunks(np.asarray(L0_xattn_w_k).T),
        "wv0": chunks(np.asarray(L0_xattn_w_v).T), "wo0": chunks(np.asarray(L0_xattn_w_o).T),
        "wq1": chunks(np.asarray(L1_xattn_Wq).T), "wk1": chunks(np.asarray(L1_xattn_Wk).T),
        "wv1": chunks(np.asarray(L1_xattn_Wv).T), "wo1": chunks(np.asarray(L1_xattn_Wo).T),
        "bq": np.asarray(L1_xattn_bq).reshape(1, D), "bk": np.asarray(L1_xattn_bk).reshape(1, D),
        "bv": np.asarray(L1_xattn_bv).reshape(D), "bo": np.asarray(L1_xattn_bo).reshape(D),
        "gate0": chunks(np.asarray(L0_ffn_gate_w).T), "gate1": chunks(np.asarray(L1_ffn_Wg).T),
        "bal": np.asarray(L0_ffn_balance_bias).reshape(NE),
        "w1_0": np.stack([chunks(w1_0[e].T).reshape(P, -1) for e in range(NE)]),
        "w2_0": np.stack([chunks(w2_0[e].T).reshape(P, -1) for e in range(NE)]),
        "w1_1": chunks(np.asarray(L1_ffn_W1).transpose(1, 0, 2).reshape(D, NE * HID1)).reshape(P, -1),
        "w2_1": np.asarray(L1_ffn_W2).transpose(1, 0, 2).reshape(P, -1),
        "lns": chunks(np.asarray(L1_ffn_ln_scale).T), "lnb": chunks(np.asarray(L1_ffn_ln_bias).T),
        "b1": np.asarray(L1_ffn_b1).T, "b2": np.asarray(L1_ffn_b2),
        "ident": np.eye(P, dtype=np.float32),
        "eid": np.tile(np.arange(NE, dtype=np.float32), (NB, 1)),
    }
    nc = bacc.Bacc("TRN2", target_bir_lowering=False, num_devices=1)
    feeds, a = {}, {}
    for name, value in arrays.items():
        value = np.ascontiguousarray(value)
        feeds[f"in_{name}"] = value
        a[name] = nc.dram_tensor(f"in_{name}", value.shape, mybir.dt.from_np(value.dtype), kind="ExternalInput").ap()
    a["out"] = nc.dram_tensor("out_rows", (TQ, NB, D), mybir.dt.float32, kind="ExternalOutput").ap()
    build(nc, a)
    r = run_bass_kernel_spmd(nc, [feeds], core_ids=[0])
    return np.ascontiguousarray(r.results[0]["out_rows"].transpose(1, 0, 2))
```

```python
from contextlib import ExitStack

import concourse.bass as bass
import numpy as np
from concourse import mybir

NB, TQ, D = 8, 100, 512
NT = NB * TQ
NK = 722
NH, DH = 16, 32
NE = 8
HID0 = 1024
HID1 = 128
P = 128
C = D // P
HALF_K = NK // 2
HALF_T = NT // 2
KT_TILES = -(-NK // P)
LAST_K = NK - (KT_TILES - 1) * P
HT = HID0 // P
W_SCALE = 256.0
UNSCALE = 1.0 / W_SCALE
Q_UNSCALE = UNSCALE / float(np.sqrt(DH))
LN_EPS = 1e-5


def key_rows(t):
    return LAST_K if t == KT_TILES - 1 else P


UNITS = [("V", 0), ("K", 0, 0), ("K", 0, 1), ("V", 1), ("K", 1, 0), ("K", 1, 1), ("V", 2),
         ("K", 2, 0), ("K", 2, 1), ("V", 3), ("K", 3, 0), ("V", 4), ("K", 3, 1), ("V", 5)]
NU = len(UNITS)
STEPS = NH + 2
K_UNIT = {(u[1], u[2]): n for n, u in enumerate(UNITS) if u[0] == "K"}
PAIR_LAST = [K_UNIT[(1, 1)], K_UNIT[(3, 1)]]


def chunk_steps():
    width = [D if u[0] == "V" else HALF_K for u in UNITS]
    total, done = C * sum(width), 0
    steps = [[] for _ in range(STEPS)]
    for u in range(NU):
        for c in range(C):
            done += width[u]
            steps[min(STEPS - 1, (done * STEPS - 1) // total)].append((u, c))
    return steps


CHUNKS_AT = chunk_steps()
ENDS_AT = [[u for u, c in step if c == C - 1] for step in CHUNKS_AT]
for pair in range(2):
    assert PAIR_LAST[pair] in sum(ENDS_AT[8 * pair + 7:], [])
assert max(map(len, ENDS_AT)) <= 2


def build(nc, a):
    fp32, fp16, u32 = mybir.dt.float32, mybir.dt.float16, mybir.dt.uint32
    ALU = mybir.AluOpType
    ACT = mybir.ActivationFunctionType
    AX = mybir.AxisListType

    ctx = ExitStack()
    with ctx:
        def sb(name, shape, dt=fp32):
            return ctx.enter_context(nc.sbuf_tensor(name, shape, dt))

        def sem(name):
            return ctx.enter_context(nc.semaphore(name))

        x = sb("x", [P, NB, D])
        tok = sb("tok", [P, NB, D])
        xT = sb("xT", [P, 2, C, NT], fp16)
        xTf = sb("xTf", [P, C, NT])
        yT = xTf
        QT = xTf[:, :, :].rearrange("p c t -> p (c t)").bitcast(fp16).rearrange(
            "p (s c t) -> p s c t", s=2, c=C)
        W = sb("W", [P, 4, 2, C, D], fp16)
        ident = sb("ident", [P, P])
        ident16 = sb("ident16", [P, P], fp16)
        eid = sb("eid", [P, 1, NE])
        gateT = sb("gateT", [P, 2, C, NE])
        bal = sb("bal", [P, 1, NE])
        bvB = sb("bvB", [P, D])
        padB = sb("padB", [P, 2, D], fp16)
        ones = sb("ones", [P, 2], fp16)
        lnsT = sb("lnsT", [P, C, NE])
        lnbT = sb("lnbT", [P, C, NE])
        b1T = sb("b1T", [P, NE])
        biasH = sb("biasH", [P, NE])
        bst = sb("bst", [P, NB, 6])
        mv = sb("mv", [P, NB, 2])
        ve = sb("ve", [P, NB])
        mhalf = sb("mhalf", [P, 1])
        rstd = sb("rstd", [P, NB])
        red = sb("red", [P, NH // 2, DH])
        rowsum = sb("rowsum", [P, 2, NH])
        rrec = sb("rrec", [P, NH // 2])
        negmax = sb("negmax", [P, 2])

        AREA = 28144
        arena = sb("arena", [P, AREA])
        at = [0]

        def part(words, dt=fp32):
            v = arena[:, at[0]:at[0] + words]
            at[0] += words
            return v if dt == fp32 else v.bitcast(dt)

        ctxF = part(C * NK).rearrange("p (c n) -> p c n", c=C)
        ctxH = [part(C * NK, fp16).rearrange("p (s c n) -> p s c n", s=2, c=C) for _ in range(2)]
        KT = part(C * NK, fp16).rearrange("p (s g n) -> p s g n", s=2, g=C)
        kst_at = at[0]
        Kst = part(NH * NK // 2, fp16).rearrange("p (h n) -> p h n", h=NH)
        V = [part(KT_TILES * NH * DH, fp16).rearrange("p (t h s d) -> p t h s d", t=KT_TILES, h=NH, s=2)
             for _ in range(2)]
        qst_at = at[0]
        Qst = [part(NH * TQ // 2, fp16).rearrange("p (h q) -> p h q", h=NH) for _ in range(2)]
        pr_at = at[0]
        Pr = [part(KT_TILES * P) for _ in range(2)]
        PT = [part(KT_TILES * P, fp16).rearrange("p (s t q) -> p s t q", s=2, t=KT_TILES) for _ in range(2)]
        assert at[0] <= AREA

        def stage_at(words):
            return arena[:, words:words + C * D].rearrange("p (c n) -> p c n", c=C)

        out_stage = stage_at(0)
        Wf = [[stage_at(kst_at), stage_at(kst_at + C * D), stage_at(qst_at), out_stage],
              [stage_at(0), stage_at(C * NK), stage_at(2 * C * NK), out_stage]]
        boB = arena[:, pr_at:pr_at + D]

        at[0] = 0
        wf = part(C * HID0)
        w1 = part(C * HID0, fp16).rearrange("p (s c n) -> p s c n", s=2, c=C)
        hs = [part(HALF_T) for _ in range(4)]
        hp = hs[2:]
        hc = part(HT * NT, fp16).rearrange("p (s j t) -> p s j t", s=2, j=HT)
        comb = part(NE * NT).rearrange("p (e t) -> p e t", e=NE)
        w2 = part(C * HID0, fp16).rearrange("p (s j n) -> p s j n", s=2, j=HT)
        ytmp = [part(HALF_T) for _ in range(2)]
        g_e = part(NB * NE).rearrange("p (b e) -> p b e", b=NB)
        g_s = part(NB * NE).rearrange("p (b e) -> p b e", b=NB)
        g_m = part(NB * 8).rearrange("p (b e) -> p b e", b=NB)
        g_i = part(NB * 8, u32).rearrange("p (b e) -> p b e", b=NB)
        g_f = part(NB * 8).rearrange("p (b e) -> p b e", b=NB)
        g_1 = part(NB * NE).rearrange("p (b e) -> p b e", b=NB)
        g_2 = part(NB * NE).rearrange("p (b e) -> p b e", b=NB)
        g_c = part(NB * NE).rearrange("p (b e) -> p b e", b=NB)
        g_h = part(NB * NE, fp16).rearrange("p (s b e) -> p s b e", s=2, b=NB)
        g_n = part(NB)
        assert at[0] <= AREA
        wf1 = wf.rearrange("p (c n) -> p c n", c=C)
        wfe = wf.rearrange("p (c e n) -> p c e n", c=C, e=NE)
        w1e = w1[:, :, :, :].rearrange("p s c (e n) -> p s c e n", e=NE)
        Wflat = W[:, :, :, :, :].rearrange("p w s c n -> p (w s c n)")
        b2f = Wflat[:, 0:2 * D].bitcast(fp32)
        b2h = Wflat[:, 2 * D:4 * D].rearrange("p (s n) -> p s n", s=2)
        maskT = Wflat[:, 4 * D:4 * D + NT]
        biasF = tok[:, 0:2, :]
        biasHi = tok[:, 2, :].bitcast(fp16).rearrange("p (s n) -> p s n", s=2)

        psum = ctx.enter_context(nc.psum_tensor("psum", [P, 8, 512], fp32))
        S_BANK, T_BANK, O_BANK, J_BANK = 0, 2, 4, 6

        x_in, ident_in, small_in, bias_in = sem("x_in"), sem("ident_in"), sem("small_in"), sem("bias_in")
        bo_in, bo_add, const_set, bias_split = sem("bo_in"), sem("bo_add"), sem("const_set"), sem("bias_split")
        pad_set, id16_set, lns_scaled = sem("pad_set"), sem("id16_set"), sem("lns_scaled")
        w_in = [sem(f"w_in{k}") for k in range(4)]
        w_hi, w_split = sem("w_hi"), sem("w_split")
        ln_st, ln_ag, ln_var, ln_rs, ln_out = sem("ln_st"), sem("ln_ag"), sem("ln_var"), sem("ln_rs"), sem("ln_out")
        ts_ps, ts_hi, ts_lo = sem("ts_ps"), sem("ts_hi"), sem("ts_lo")
        ot_ps, ot_hi, ot_lo = sem("ot_ps"), sem("ot_hi"), sem("ot_lo")
        q_ps, q_hi, q_lo = sem("q_ps"), sem("q_hi"), sem("q_lo")
        qst_in = [sem(f"qst_in{k}") for k in range(2)]
        kst_in = [sem(f"kst_in{k}") for k in range(2)]
        ctx_in, ctx_begun, ctx_hi, ctx_split = sem("ctx_in"), sem("ctx_begun"), sem("ctx_hi"), sem("ctx_split")
        ctx0_hi = sem("ctx0_hi")
        proj_ps, proj_hi, proj_lo = sem("proj_ps"), sem("proj_hi"), sem("proj_lo")
        scores, maxed, probs = sem("scores"), sem("maxed"), sem("probs")
        probsT, pt_hi, pt_lo = sem("probsT"), sem("pt_hi"), sem("pt_lo")
        pv, norm_chain, attn_rows, attn_out = sem("pv"), sem("norm_chain"), sem("attn_rows"), sem("attn_out")
        o_ps, o_add = sem("o_ps"), sem("o_add")
        g_ps, g_pre, g_exp, g_chain, g_done = sem("g_ps"), sem("g_pre"), sem("g_exp"), sem("g_chain"), sem("g_done")
        comb_ps, comb_out = sem("comb_ps"), sem("comb_out")
        wf_in, fw_hi, fw_split = sem("wf_in"), sem("fw_hi"), sem("fw_split")
        h_ps, h_act, h_mul, h_hi, h_lo = sem("h_ps"), sem("h_act"), sem("h_mul"), sem("h_hi"), sem("h_lo")
        y_ps, y_mul, y_add = sem("y_ps"), sem("y_mul"), sem("y_add")
        yt_ps, x_new = sem("yt_ps"), sem("x_new")
        b2_in, b2_hi, b2_split = sem("b2_in"), sem("b2_hi"), sem("b2_split")
        mask_ps, mask_out = sem("mask_ps"), sem("mask_out")
        bh_ps, bh_out, w1m_hi = sem("bh_ps"), sem("bh_out"), sem("w1m_hi")
        out_written = sem("out_written")

        OT_AT = {2 * k: k for k in range(NB - 1)}
        PROD_AT = {2 * k + 1 + i: (k, i) for k in range(NB - 1) for i in range(2)}
        ADD_AT = {2 * k + 3: k for k in range(NB - 1)}
        MOMENTS_AT = {2 * k + 4: k for k in range(NB - 1)}
        APPLY_AT = {2 * k + 6: k for k in range(6)}
        LNT_AT = {2 * k + 7: k for k in range(6)}

        def weight_chunks_at(s, layer, b):
            if b == NB - 2 and 8 <= s < 12:
                return [(layer, 3, s - 8)]
            if b == NB - 1 and layer == 0 and 6 <= s < 12:
                return [(1, n // 4, n % 4) for n in (2 * (s - 6), 2 * (s - 6) + 1)]
            return []

        def expert_blocks_at(s, layer, b):
            if layer == 1 and b == NB - 1 and 6 <= s < 14:
                return [(n // NE, n % NE) for n in range(4 * (s - 6), 4 * (s - 5))]
            return []

        def w_count(layer, k, c):
            return 16 * layer + 4 * k + c + 1

        block = ctx.enter_context(nc.Block())

        @block.sync
        def _(sp):
            def load_weights(layer, k):
                sp.dma_start(Wf[layer][k], a[("wk", "wv", "wq", "wo")[k] + str(layer)]).then_inc(w_in[k], 16)

            def apart():
                sp.wait_ge(x_in, 16)

            def load_ctx(b):
                sp.dma_start(ctxF[:, :, :], a["ctx"][bass.ds(b, 1), :, :, :].rearrange("o p c n -> p (o c) n"))\
                    .then_inc(ctx_in, 16)

            def stack_q(b, par):
                for r in range(3):
                    for j in range(4):
                        src = QT[32 * j:32 * j + 32, r // 2, :, bass.ds(b * TQ, TQ)]
                        sp.dma_start(Qst[par][32 * r:32 * r + 32, j:NH:4, :], src).then_inc(qst_in[par], 16)

            def stack_k(gb, pair):
                sp.wait_ge(proj_lo, gb * NU + PAIR_LAST[pair] + 1)
                for r in range(3):
                    for j in range(4):
                        sp.dma_start(Kst[32 * r:32 * r + 32, 8 * pair + j:8 * pair + 8:4, :],
                                     KT[32 * j:32 * j + 32, r % 2, 2 * pair:2 * pair + 2, :])\
                            .then_inc(kst_in[pair], 16)

            sp.dma_start(ctxF[:, :, :], a["ctx"][0]).then_inc(ctx_in, 16)
            load_weights(0, 0)
            load_weights(0, 1)
            sp.dma_start(x[0:TQ, :, :], a["x"]).then_inc(x_in, 16)
            load_weights(0, 2)
            sp.dma_start(ident[:, :], a["ident"]).then_inc(ident_in, 16)
            sp.dma_start(biasF[0:1, 0, :], a["bq"]).then_inc(bias_in, 16)
            sp.dma_start(biasF[0:1, 1, :], a["bk"]).then_inc(bias_in, 16)
            sp.dma_start(biasF[32:33, 0, :], a["bq"]).then_inc(bias_in, 16)
            sp.dma_start(biasF[32:33, 1, :], a["bk"]).then_inc(bias_in, 16)
            sp.dma_start(eid[0:TQ, 0, :], a["eid"].partition_broadcast(TQ)).then_inc(small_in, 16)
            sp.dma_start(gateT[:, 0, :, :], a["gate0"]).then_inc(small_in, 16)
            sp.dma_start(gateT[:, 1, :, :], a["gate1"]).then_inc(small_in, 16)
            sp.dma_start(bal[0:TQ, 0, :], a["bal"].partition_broadcast(TQ)).then_inc(small_in, 16)
            sp.dma_start(bvB[0:TQ, :], a["bv"].partition_broadcast(TQ)).then_inc(small_in, 16)
            sp.dma_start(lnsT[:, :, :], a["lns"]).then_inc(small_in, 16)
            sp.dma_start(lnbT[:, :, :], a["lnb"]).then_inc(small_in, 16)
            sp.dma_start(b1T[:, :], a["b1"]).then_inc(small_in, 16)

            for layer in range(2):
                g0 = layer * NB
                if layer == 1:
                    sp.wait_ge(fw_split, 2 * NE)
                    load_ctx(0)
                sp.wait_ge(ctx_split, g0 + 1)
                load_ctx(1)
                if layer == 1:
                    sp.wait_ge(y_ps, 2 * C * NE)
                    sp.dma_start(boB[0:TQ, :], a["bo"].partition_broadcast(TQ)).then_inc(bo_in, 16)
                sp.wait_ge(q_lo, 8 * layer + 8)
                stack_q(0, 0)
                stack_k(g0, 0)
                stack_k(g0, 1)

                def next_stacks(b, gb, par):
                    stack_q(b + 1, 1 - par)
                    for pair in range(2):
                        stack_k(gb + 1, pair)

                with sp.Fori(0, 3) as i:
                    for par in range(2):
                        b, gb = 2 * i + par, g0 + 2 * i + par
                        sp.wait_ge(ctx_split, gb + 2)
                        apart()
                        load_ctx(b + 2)
                        next_stacks(b, gb, par)
                sp.wait_ge(ctx_split, g0 + NB)
                load_weights(layer, 3)
                next_stacks(NB - 2, g0 + NB - 2, 0)
                sp.wait_ge(proj_ps, (g0 + NB) * NU)
                sp.wait_ge(w_split, w_count(layer, 3, 3))

                if layer == 0:
                    for k in range(3):
                        load_weights(1, k)
                    sp.wait_ge(w_split, w_count(1, 2, 3))
                    sp.dma_start(wf, a["w1_0"][0]).then_inc(wf_in, 16)
                    sp.wait_ge(fw_split, 1)
                    sp.dma_start(wf, a["w2_0"][0]).then_inc(wf_in, 16)
                    with sp.Fori(1, NE) as e:
                        sp.wait_ge(fw_split, 2 * e)
                        apart()
                        sp.dma_start(wf, a["w1_0"][bass.ds(e, 1), :, :].rearrange("o p n -> p (o n)"))\
                            .then_inc(wf_in, 16)
                        sp.wait_ge(fw_split, 2 * e + 1)
                        apart()
                        sp.dma_start(wf, a["w2_0"][bass.ds(e, 1), :, :].rearrange("o p n -> p (o n)"))\
                            .then_inc(wf_in, 16)
                else:
                    sp.dma_start(wf, a["w1_1"]).then_inc(wf_in, 16)
                    sp.dma_start(b2f[0:NE, :], a["b2"]).then_inc(b2_in, 16)
                    sp.wait_ge(fw_split, 2 * NE + 1)
                    sp.wait_ge(bh_ps, 1)
                    sp.dma_start(wf, a["w2_1"]).then_inc(wf_in, 16)

            for b in range(NB):
                sp.wait_ge(x_new, NB + b + 1)
                sp.dma_start(a["out"][:, b, :], x[0:TQ, b, :]).then_inc(out_written, 16)
            sp.wait_ge(out_written, 16 * NB)

        @block.gpsimd
        def _(pool):
            def split_ctx(gb, par):
                pool.wait_ge(ctx_in, 16 * (gb + 1))
                pool.sem_inc(ctx_begun, 1)
                nc.gpsimd.tensor_copy(ctxH[par][:, 0, :, :], ctxF[:, :, :]).then_inc(ctx_hi, 1)
                pool.wait_ge(ctx_hi, gb)
                nc.gpsimd.tensor_tensor(ctxH[par][:, 1, :, :], ctxF[:, :, :], ctxH[par][:, 0, :, :], ALU.subtract)\
                    .then_inc(ctx_split, 1)

            def norm_root(n, b):
                pool.wait_ge(ln_var, NB * n + b + 1)
                nc.gpsimd.tensor_tensor(rstd[0:TQ, b:b + 1], ve[0:TQ, b:b + 1], mhalf[0:TQ, :], ALU.pow)\
                    .then_inc(ln_rs, 1)

            pool.wait_ge(const_set, 1)
            for layer in range(2):
                g0 = layer * NB
                if layer == 1:
                    pool.wait_ge(h_ps, 2 * HT * NE)
                    split_ctx(g0, 0)
                for b in range(NB):
                    norm_root(2 * layer, b)
                split_ctx(g0 + 1, 1)
                with pool.Fori(0, 3) as i:
                    for par in range(2):
                        gb = g0 + 2 * i + par
                        pool.wait_ge(proj_ps, (gb + 1) * NU)
                        split_ctx(gb + 2, par)
                for b in range(NB):
                    norm_root(2 * layer + 1, b)

        @block.tensor
        def _(pe):
            mm = nc.tensor.matmul

            def bank(k, rows, cols):
                return psum[0:rows, k, 0:cols]

            def rows_transpose(k, b, done):
                for c in range(C):
                    last = nc.tensor.transpose(psum[:, k, c * TQ:(c + 1) * TQ],
                                               tok[0:TQ, b, c * P:(c + 1) * P], ident[0:TQ, 0:TQ])
                last.then_inc(done, 1)

            def three(out, lhs, rhs, first=True, last=True):
                n = len(lhs)
                for c in range(n):
                    (lh, ll), (rh, rl) = lhs[c], rhs[c]
                    for k, (l_, r_) in enumerate(((lh, rh), (lh, rl), (ll, rh))):
                        ins = mm(out, l_, r_, start=first and c == 0 and k == 0,
                                 stop=last and c == n - 1 and k == 2)
                return ins

            def xT_of(c, cols):
                return tuple(xT[:, s, c, cols] for s in range(2))

            def queries(layer, us):
                for u in us:
                    g, half = u // 2, u % 2
                    if u == 0:
                        pe.wait_ge(w_split, w_count(layer, 2, 3))
                        pe.wait_ge(ts_lo, NB * 2 * layer + NB)
                    if u >= 2:
                        pe.wait_ge(q_lo, 8 * layer + u - 1)
                    out = bank(O_BANK + u % 2, P, HALF_T)
                    if layer == 1:
                        mm(out, padB[:, 0, g * P:(g + 1) * P], ones[:, 0:1].broadcast_to([P, HALF_T]),
                           start=True, stop=False)
                    cols = slice(g * P, (g + 1) * P)
                    three(out, [(W[:, 2, 0, c, cols], W[:, 2, 1, c, cols]) for c in range(C)],
                          [xT_of(c, slice(half * HALF_T, (half + 1) * HALF_T)) for c in range(C)],
                          first=layer == 0).then_inc(q_ps, 1)

            def project(layer, gb, par, u, c, static_first=False):
                if c == 0:
                    if u == 0:
                        pe.wait_ge(ctx_split, gb + 1)
                    if static_first and u < 2:
                        if u == 0:
                            pe.wait_ge(w_split, w_count(layer, 1, 3))
                        if layer == 1:
                            pe.wait_ge(y_mul, 2 * C * NE)
                    else:
                        pe.wait_ge(proj_lo, gb * NU + u - 1)
                k = J_BANK + u % 2
                ends = dict(first=c == 0, last=c == C - 1)
                if UNITS[u][0] == "K":
                    _, g, half = UNITS[u]
                    out = bank(k, P, HALF_K)
                    if layer == 1 and c == 0:
                        mm(out, padB[:, 1, g * P:(g + 1) * P], ones[:, 0:1].broadcast_to([P, HALF_K]),
                           start=True, stop=False)
                        ends["first"] = False
                    cols = slice(g * P, (g + 1) * P)
                    ins = three(
                        out, [(W[:, 0, 0, c, cols], W[:, 0, 1, c, cols])],
                        [tuple(ctxH[par][:, s, c, half * HALF_K:(half + 1) * HALF_K] for s in range(2))], **ends)
                else:
                    t = UNITS[u][1]
                    r = key_rows(t)
                    ins = three(
                        bank(k, r, D), [tuple(ctxH[par][:, s, c, t * P:t * P + r] for s in range(2))],
                        [(W[:, 1, 0, c, :], W[:, 1, 1, c, :])], **ends)
                if c == C - 1:
                    ins.then_inc(proj_ps, 1)

            def score(gb, par, h):
                if h % 8 == 0:
                    pe.wait_ge(kst_in[h // 8], 192 * (gb + 1))
                if h > 0:
                    pe.wait_ge(probs, gb * NH + h)
                for half in range(2):
                    last = mm(psum[0:TQ, S_BANK + half, 0:HALF_K], Qst[par][0:96, h, :],
                              Kst[0:96, h, half * HALF_K:(half + 1) * HALF_K], start=True, stop=True)
                last.then_inc(scores, 1)

            def probs_transpose(gb, h):
                pe.wait_ge(probs, gb * NH + h + 1)
                for k in range(2):
                    if h > 0:
                        pe.wait_ge(pt_lo, 2 * (gb * NH + h) + k - 1)
                    for t in range(3):
                        last = nc.tensor.transpose(psum[:, T_BANK + k, t * TQ:(t + 1) * TQ],
                                                   Pr[h % 2][0:TQ, (3 * k + t) * P:(3 * k + t + 1) * P],
                                                   ident[0:TQ, 0:TQ])
                    last.then_inc(probsT, 1)

            def values(gb, par, h):
                if h == 0:
                    pe.wait_ge(proj_lo, (gb + 1) * NU)
                pe.wait_ge(pt_lo, 2 * (gb * NH + h + 1))
                half, k = h // 8, h % 8
                for t in range(KT_TILES):
                    r = key_rows(t)
                    for s in range(2):
                        last = mm(psum[:, O_BANK + half, k * 2 * DH:(k + 1) * 2 * DH],
                                  PT[h % 2][0:r, s, t, :],
                                  V[par][0:r, t, h, :, :].rearrange("p s d -> p (s d)"),
                                  start=t == 0 and s == 0, stop=t == KT_TILES - 1 and s == 1)
                last.then_inc(pv, 1)

            def output_transpose(layer, k):
                if 4 <= k < NB - 1:
                    pe.wait_ge(ts_lo, NB * (2 * layer + 1) + k - 3)
                elif k == NB - 1:
                    pe.wait_ge(ts_lo, NB * (2 * layer + 1) + 6)
                elif k == 0:
                    pe.wait_ge(proj_lo, NB * (layer + 1) * NU)
                else:
                    pe.wait_ge(ot_lo, NB * layer + k)
                if layer == 0:
                    pe.wait_ge(attn_rows, 2 * k + 2)
                else:
                    pe.wait_ge(attn_out, k + 1)
                rows_transpose(J_BANK, k, ot_ps)

            def output_product(layer, k, half):
                if k == 0 and half == 0:
                    pe.wait_ge(w_split, w_count(layer, 3, 3))
                if half == 0:
                    pe.wait_ge(ot_lo, NB * layer + k + 1)
                    if k > 0:
                        pe.wait_ge(o_add, NB * layer + k)
                cs = (2 * half, 2 * half + 1)
                ins = three(bank(J_BANK + 1, TQ, D), [xT_of(c, slice(k * TQ, (k + 1) * TQ)) for c in cs],
                            [(W[:, 3, 0, c, :], W[:, 3, 1, c, :]) for c in cs], first=half == 0, last=half == 1)
                if half == 1:
                    ins.then_inc(o_ps, 1)

            def norm_transpose(layer, k):
                if k <= 3:
                    pe.wait_ge(ot_lo, NB * layer + k + 4)
                else:
                    pe.wait_ge(ts_lo, NB * (2 * layer + 1) + k)
                if k >= 6:
                    pe.wait_ge(ot_lo, NB * layer + NB)
                pe.wait_ge(ln_out, NB * (2 * layer + 1) + k + 1)
                rows_transpose(J_BANK, k, ts_ps)

            def attend(layer, gb, par, more):
                pe.wait_ge(qst_in[par], (gb - par) * 96 + 192)
                for s in range(STEPS):
                    if s < NH:
                        score(gb, par, s)
                    if 1 <= s <= NH:
                        probs_transpose(gb, s - 1)
                    if s >= 2:
                        values(gb, par, s - 2)
                    if more:
                        for u, c in CHUNKS_AT[s]:
                            project(layer, gb + 1, 1 - par, u, c)
                    elif s in PROD_AT:
                        output_product(layer, *PROD_AT[s])
                    if not more and s in OT_AT:
                        output_transpose(layer, OT_AT[s])
                    if not more and s in LNT_AT:
                        norm_transpose(layer, LNT_AT[s])

            def gate(layer, b):
                if b == 0:
                    pe.wait_ge(small_in, 16 * 8)
                pe.wait_ge(ts_lo, NB * (2 * layer + 1) + b + 1)
                for c in range(C):
                    last = mm(psum[0:TQ, O_BANK, b * NE:(b + 1) * NE], xTf[:, c, b * TQ:(b + 1) * TQ],
                              gateT[:, layer, c, :], start=c == 0, stop=c == C - 1)
                if b == NB - 1:
                    last.then_inc(g_ps, 1)

            def hidden_biases():
                pe.wait_ge(wf_in, 16 * (2 * NE + 1))
                for e in range(NE):
                    for c in range(C):
                        last = mm(psum[:, O_BANK + 1, e:e + 1], wf1[:, c, e * P:(e + 1) * P],
                                  lnbT[:, c, e:e + 1], start=c == 0, stop=c == C - 1)
                last.then_inc(bh_ps, 1)

            def spread_gates(layer):
                pe.wait_ge(g_done, layer + 1)
                pe.wait_ge(id16_set, 1)
                pe.wait_ge(ts_lo, NB * (2 * layer + 2))
                halves = 2 if layer == 0 else 1
                for e in range(NE):
                    for half in range(2):
                        n = 2 * e + half
                        if n >= 2:
                            pe.wait_ge(comb_out, 16 * layer + n - 1)
                        for k in range(4):
                            b = 4 * half + k
                            for s in range(halves):
                                last = mm(psum[:, J_BANK + n % 2, k * TQ:(k + 1) * TQ],
                                          g_h[0:TQ, s, b, e:e + 1].broadcast_to([TQ, P]), ident16[0:TQ, 0:TQ],
                                          start=s == 0, stop=s == halves - 1)
                        last.then_inc(comb_ps, 1)

            def mask_rows():
                for half in range(2):
                    if half == 0:
                        pe.wait_ge(bh_out, 1)
                    for k in range(4):
                        last = mm(psum[0:NE, O_BANK + half, k * TQ:(k + 1) * TQ], g_c[0:TQ, 4 * half + k, :],
                                  ident[0:TQ, 0:TQ], start=True, stop=True)
                    last.then_inc(mask_ps, 1)

            def expert(xe, first, layer, between):
                pe.wait_ge(fw_split, 2 * xe + 1)
                for n in range(2 * HT):
                    half, j = n // HT, n % HT
                    if not (first and n < 4):
                        pe.wait_ge(h_act, xe * 2 * HT + n - 3)
                    if first and n == HT:
                        pe.wait_ge(ts_lo, NB * (2 * layer + 2))
                    cols = slice(j * P, (j + 1) * P)
                    three(bank(n % 4, P, HALF_T), [(w1[:, 0, c, cols], w1[:, 1, c, cols]) for c in range(C)],
                          [xT_of(c, slice(half * HALF_T, (half + 1) * HALF_T)) for c in range(C)]).then_inc(h_ps, 1)
                    for job in between.get(("h", n), []):
                        job()
                pe.wait_ge(fw_split, 2 * xe + 2)
                for u in range(2 * C):
                    half, m = u // C, u % C
                    if not (first and u < 4):
                        pe.wait_ge(y_mul, xe * 2 * C + u - 3)
                    out = bank(4 + u % 4, P, HALF_T)
                    cols = slice(half * HALF_T, (half + 1) * HALF_T)
                    if layer == 1:
                        for s in range(2):
                            mm(out, b2h[0:NE, s, m * P:(m + 1) * P], maskT[0:NE, cols], start=s == 0, stop=False)
                    for j in range(HT):
                        if m == 0:
                            pe.wait_ge(h_lo, xe * 2 * HT + half * HT + j + 1)
                        ins = three(out, [(w2[:, 0, j, m * P:(m + 1) * P], w2[:, 1, j, m * P:(m + 1) * P])],
                                    [tuple(hc[:, s, j, cols] for s in range(2))],
                                    first=j == 0 and layer == 0, last=j == HT - 1)
                    ins.then_inc(y_ps, 1)
                    for job in between.get(("y", u), []):
                        job()

            def y_rows(layer, b):
                if layer == 0:
                    pe.wait_ge(y_add, 2 + 2 * C * NE)
                else:
                    pe.wait_ge(y_mul, 2 * C * NE + C * (b // 4 + 1))
                if b >= 2:
                    pe.wait_ge(x_new, NB * layer + b - 1)
                for c in range(C):
                    last = nc.tensor.transpose(psum[0:TQ, T_BANK + b % 2, c * P:(c + 1) * P],
                                               yT[:, c, b * TQ:(b + 1) * TQ], ident[:, :])
                last.then_inc(yt_ps, 1)

            pe.wait_ge(const_set, 1)
            for layer in range(2):
                g0 = layer * NB

                def units(us):
                    for u in us:
                        for c in range(C):
                            project(layer, g0, 0, u, c, static_first=True)

                units(range(0, 2))
                if layer == 1:
                    for b in range(NB):
                        y_rows(0, b)
                units(range(2, 6))
                pe.wait_ge(ident_in, 16)
                for b in range(NB):
                    if b >= 2:
                        pe.wait_ge(ts_lo, NB * 2 * layer + b - 1)
                    elif layer == 1:
                        pe.wait_ge(x_new, 7 + b)
                    pe.wait_ge(ln_out, NB * 2 * layer + b + 1)
                    rows_transpose(T_BANK + b % 2, b, ts_ps)
                units(range(6, 8))
                queries(layer, range(2 * C))
                units(range(8, NU))
                pe.wait_ge(pad_set, layer + 1)
                with pe.Fori(0, 3) as i:
                    for par in range(2):
                        attend(layer, g0 + 2 * i + par, par, True)
                attend(layer, g0 + NB - 2, 0, True)
                attend(layer, g0 + NB - 1, 1, False)
                output_transpose(layer, NB - 1)
                norm_transpose(layer, NB - 2)
                for b in range(4):
                    gate(layer, b)
                output_product(layer, NB - 1, 0)
                output_product(layer, NB - 1, 1)
                for b in range(4, NB - 1):
                    gate(layer, b)

                def last_norm():
                    norm_transpose(layer, NB - 1)

                def last_gate():
                    gate(layer, NB - 1)

                if layer == 0:
                    expert(0, True, 0, {("h", 1): [last_norm], ("h", 2): [last_gate],
                                        ("h", 9): [lambda: spread_gates(0)],
                                        ("h", 15): [lambda: pe.wait_ge(comb_out, 16)]})
                    with pe.Fori(1, NE) as e:
                        expert(e, False, 0, {})
                else:
                    hidden_biases()

                    def before_output():
                        pe.wait_ge(comb_out, 32)
                        pe.wait_ge(mask_out, 2)
                        pe.wait_ge(b2_split, 1)

                    expert(NE, True, 1, {
                        ("h", 1): [last_norm, last_gate], ("h", 3): [lambda: spread_gates(1), mask_rows],
                        ("h", 15): [before_output],
                        ("y", 5): [lambda b=b: y_rows(1, b) for b in range(4)],
                        ("y", 7): [lambda b=b: y_rows(1, b) for b in range(4, 8)]})

        @block.scalar
        def _(act):
            copy = ACT.Copy

            def weight_high(layer, k, c):
                if c == 0:
                    act.wait_ge(w_in[k], 16 * (layer + 1))
                nc.scalar.activation(W[:, k, 0, c, :], Wf[layer][k][:, c, :], copy, scale=W_SCALE).then_inc(w_hi, 1)

            def block_high(c, e):
                if c == 0 and e == 0:
                    act.wait_ge(wf_in, 16 * (2 * NE + 1))
                    act.wait_ge(lns_scaled, 1)
                nc.scalar.activation(w1e[:, 0, c, e, :], wfe[:, c, e, :], copy, scale=lnsT[:, c, e:e + 1])\
                    .then_inc(w1m_hi, 1)

            def norm_high(n, b, k, keep):
                act.wait_ge(ts_ps, NB * n + b + 1)
                src = psum[:, k, 0:C * TQ].rearrange("p (c t) -> p c t", c=C)
                if keep:
                    nc.scalar.activation(xTf[:, :, b * TQ:(b + 1) * TQ], src, copy)
                nc.scalar.activation(xT[:, 0, :, b * TQ:(b + 1) * TQ], src, copy).then_inc(ts_hi, 1)

            def output_high(layer, b):
                act.wait_ge(ot_ps, NB * layer + b + 1)
                nc.scalar.activation(xT[:, 0, :, b * TQ:(b + 1) * TQ],
                                     psum[:, J_BANK, 0:C * TQ].rearrange("p (c t) -> p c t", c=C), copy)\
                    .then_inc(ot_hi, 1)

            def queries_high(layer):
                for u in range(2 * C):
                    g, half = u // 2, u % 2
                    act.wait_ge(q_ps, 8 * layer + u + 1)
                    nc.scalar.activation(QT[:, 0, g, half * HALF_T:(half + 1) * HALF_T],
                                         psum[:, O_BANK + u % 2, 0:HALF_T], copy, scale=Q_UNSCALE)\
                        .then_inc(q_hi, 1)

            def unit_high(gb, par, u, very_first=False):
                act.wait_ge(proj_ps, gb * NU + u + 1)
                k = J_BANK + u % 2
                if UNITS[u][0] == "K":
                    _, g, half = UNITS[u]
                    if half == 0 and g % 2 == 0 and not very_first:
                        act.wait_ge(kst_in[g // 2], 192 * gb)
                    out, src = KT[:, 0, g, half * HALF_K:(half + 1) * HALF_K], psum[:, k, 0:HALF_K]
                else:
                    t = UNITS[u][1]
                    r = key_rows(t)
                    out, src = V[par][0:r, t, :, 0, :], psum[0:r, k, :].rearrange("p (h d) -> p h d", h=NH)
                nc.scalar.activation(out, src, copy, scale=UNSCALE).then_inc(proj_hi, 1)

            def probabilities(gb, par, h):
                act.wait_ge(maxed, gb * NH + h + 1)
                nc.scalar.activation(Pr[h % 2][0:TQ, 0:NK].rearrange("q (s n) -> q s n", s=2),
                                     psum[0:TQ, S_BANK:S_BANK + 2, 0:HALF_K], ACT.Exp,
                                     bias=negmax[0:TQ, h % 2:h % 2 + 1],
                                     accum_out=rowsum[0:TQ, par, h:h + 1]).then_inc(probs, 1)

            def probsT_high(gb, h):
                if h >= 2:
                    act.wait_ge(pv, gb * NH + h - 1)
                for k in range(2):
                    act.wait_ge(probsT, 2 * (gb * NH + h) + k + 1)
                    nc.scalar.activation(PT[h % 2][:, 0, 3 * k:3 * k + 3, 0:TQ],
                                         psum[:, T_BANK + k, 0:3 * TQ].rearrange("p (t q) -> p t q", t=3), copy)\
                        .then_inc(pt_hi, 1)

            def attend(layer, b, gb, par, more):
                last_batch = not more
                for s in range(STEPS + 1):
                    if more and s >= 1:
                        for u in ENDS_AT[s - 1]:
                            unit_high(gb + 1, 1 - par, u)
                    if 1 <= s <= NH:
                        probsT_high(gb, s - 1)
                    if s < NH:
                        probabilities(gb, par, s)
                    if last_batch and s - 1 in OT_AT:
                        output_high(layer, OT_AT[s - 1])
                    if last_batch and s - 1 in LNT_AT:
                        norm_high(2 * layer + 1, LNT_AT[s - 1], J_BANK, True)
                    for chunk in weight_chunks_at(s, layer, b):
                        weight_high(*chunk)
                    for c, e in expert_blocks_at(s, layer, b):
                        block_high(c, e)

            def piece_high(xe, which, k, out, src):
                act.wait_ge(wf_in, 16 * (2 * xe + which + 1))
                nc.scalar.activation(out, src, copy, scale=W_SCALE).then_inc(fw_hi, 1)

            def w1_high(xe):
                for k in range(C):
                    piece_high(xe, 0, k, w1[:, 0, k, :], wf1[:, k, :])

            def w2_high(xe, k):
                piece_high(xe, 1, k, w2[:, 0, 2 * k:2 * k + 2, :],
                           wf[:, 2 * k * D:(2 * k + 2) * D].rearrange("p (j n) -> p j n", j=2))

            def comb_out_of(layer):
                for n in range(2 * NE):
                    e, half = n // 2, n % 2
                    act.wait_ge(comb_ps, 16 * layer + n + 1)
                    nc.scalar.activation(comb[:, e, half * HALF_T:(half + 1) * HALF_T],
                                         psum[:, J_BANK + n % 2, 0:HALF_T], copy).then_inc(comb_out, 1)

            def expert0(xe, first):
                if not first:
                    w1_high(xe)
                for n in range(2 * HT):
                    half, j = n // HT, n % HT
                    act.wait_ge(h_ps, xe * 2 * HT + n + 1)
                    if not (first and n < 4):
                        act.wait_ge(h_lo, xe * 2 * HT + n - 3)
                    src = psum[:, n % 4, 0:HALF_T]
                    nc.scalar.activation(hs[n % 4], src, ACT.Silu, scale=UNSCALE)
                    nc.scalar.activation(hc[:, 0, j, half * HALF_T:(half + 1) * HALF_T], src, ACT.Silu,
                                         scale=UNSCALE).then_inc(h_act, 1)
                    if first and n == 1:
                        norm_high(1, NB - 1, J_BANK, True)
                    if first and n == 4:
                        act.wait_ge(g_pre, 1)
                        nc.scalar.activation(g_e[0:TQ, :, :], g_e[0:TQ, :, :], ACT.Exp, scale=-1.0)\
                            .then_inc(g_exp, 1)
                    if first and n == 9:
                        comb_out_of(0)
                    if n >= 8 and n % 2 == 0:
                        w2_high(xe, n // 2 - 4)

            def expert1():
                xe = NE

                def high(n):
                    half, j = n // HT, n % HT
                    act.wait_ge(h_mul, xe * 2 * HT + n + 1 - 2 * HT * NE)
                    nc.scalar.activation(hc[:, 0, j, half * HALF_T:(half + 1) * HALF_T], hp[n % 2], copy)\
                        .then_inc(h_hi, 1)

                def gelu(n):
                    j = n % HT
                    act.wait_ge(h_ps, xe * 2 * HT + n + 1)
                    if n >= 2:
                        act.wait_ge(h_mul, n - 1)
                    nc.scalar.activation(hs[n % 2], psum[:, n % 4, 0:HALF_T], ACT.Gelu, scale=UNSCALE,
                                         bias=biasH[:, j:j + 1]).then_inc(h_act, 1)

                act.wait_ge(bh_out, 1)
                gelu(0)
                gelu(1)
                norm_high(3, NB - 1, J_BANK, True)
                comb_out_of(1)
                for half in range(2):
                    act.wait_ge(mask_ps, half + 1)
                    nc.scalar.activation(maskT[0:NE, half * HALF_T:(half + 1) * HALF_T],
                                         psum[0:NE, O_BANK + half, 0:HALF_T], copy).then_inc(mask_out, 1)
                high(0)
                for n in range(2, 2 * HT):
                    gelu(n)
                    high(n - 1)
                    if n >= 8 and n % 2 == 0:
                        w2_high(xe, n // 2 - 4)
                high(2 * HT - 1)

            for layer in range(2):
                g0 = layer * NB

                def units(us):
                    for u in us:
                        unit_high(g0, 0, u, very_first=layer == 0)

                if layer == 0:
                    act.wait_ge(ctx_in, 16)
                    for c in range(C):
                        nc.scalar.activation(ctxH[0][:, 0, c, :], ctxF[:, c, :], copy).then_inc(ctx0_hi, 1)
                    for k in (0, 1):
                        for c in range(C):
                            weight_high(0, k, c)
                    act.wait_ge(w_split, w_count(0, 1, 3))
                units(range(0, 6))
                if layer == 0:
                    act.wait_ge(ident_in, 16)
                    nc.scalar.activation(ident16[:, :], ident[:, :], copy).then_inc(id16_set, 1)
                    for c in range(C):
                        weight_high(0, 2, c)
                for b in range(NB):
                    norm_high(2 * layer, b, T_BANK + b % 2, False)
                units(range(6, 8))
                queries_high(layer)
                units(range(8, NU))
                act.wait_ge(pad_set, layer + 1)
                with act.Fori(0, 3) as i:
                    for par in range(2):
                        attend(layer, 0, g0 + 2 * i + par, par, True)
                attend(layer, NB - 2, g0 + NB - 2, 0, True)
                attend(layer, NB - 1, g0 + NB - 1, 1, False)
                output_high(layer, NB - 1)
                norm_high(2 * layer + 1, NB - 2, J_BANK, True)
                if layer == 0:
                    w1_high(0)
                    expert0(0, True)
                    with act.Fori(1, NE) as e:
                        expert0(e, False)
                else:
                    act.wait_ge(b2_in, 16)
                    nc.scalar.activation(b2h[0:NE, 0, :], b2f[0:NE, :], copy, scale=W_SCALE).then_inc(b2_hi, 1)
                    expert1()

        @block.vector
        def _(dve):
            v = nc.vector

            def low(out, src, scale, high):
                return v.scalar_tensor_tensor(out, src, scale, high, ALU.mult, ALU.subtract)

            def weight_low(layer, k, c):
                dve.wait_ge(w_hi, w_count(layer, k, c))
                low(W[:, k, 1, c, :], Wf[layer][k][:, c, :], W_SCALE, W[:, k, 0, c, :]).then_inc(w_split, 1)

            def block_low(c, e):
                dve.wait_ge(w1m_hi, NE * c + e + 1)
                ins = low(w1e[:, 1, c, e, :], wfe[:, c, e, :], lnsT[:, c, e:e + 1], w1e[:, 0, c, e, :])
                if c == C - 1 and e == NE - 1:
                    ins.then_inc(fw_split, 1)

            def norm_stats(n, b):
                v.bn_stats(bst[0:TQ, b, :], x[0:TQ, b, :]).then_inc(ln_st, 1)

            def norm_moments(n, b):
                dve.wait_ge(ln_st, NB * n + b + 1)
                v.bn_aggr(mv[0:TQ, b, :], bst[0:TQ, b, :]).then_inc(ln_ag, 1)

            def norm_variance(n, b):
                dve.wait_ge(ln_ag, NB * n + b + 1)
                v.tensor_scalar(ve[0:TQ, b:b + 1], mv[0:TQ, b, 1:2], LN_EPS, None, ALU.add).then_inc(ln_var, 1)

            def norm_apply(n, b):
                dve.wait_ge(ln_rs, NB * n + b + 1)
                v.tensor_scalar(tok[0:TQ, b, :], x[0:TQ, b, :], mv[0:TQ, b, 0:1], rstd[0:TQ, b:b + 1],
                                ALU.subtract, ALU.mult).then_inc(ln_out, 1)

            def norm_low(n, b, k):
                dve.wait_ge(ts_hi, NB * n + b + 1)
                cols = slice(b * TQ, (b + 1) * TQ)
                low(xT[:, 1, :, cols], psum[:, k, 0:C * TQ].rearrange("p (c t) -> p c t", c=C), 1.0,
                    xT[:, 0, :, cols]).then_inc(ts_lo, 1)

            def output_low(layer, b):
                dve.wait_ge(ot_hi, NB * layer + b + 1)
                cols = slice(b * TQ, (b + 1) * TQ)
                low(xT[:, 1, :, cols], psum[:, J_BANK, 0:C * TQ].rearrange("p (c t) -> p c t", c=C), 1.0,
                    xT[:, 0, :, cols]).then_inc(ot_lo, 1)

            def output_add(layer, b):
                dve.wait_ge(o_ps, NB * layer + b + 1)
                if layer == 1:
                    dve.wait_ge(bo_add, NB)
                v.scalar_tensor_tensor(x[0:TQ, b, :], psum[0:TQ, J_BANK + 1, :], UNSCALE, x[0:TQ, b, :],
                                       ALU.mult, ALU.add).then_inc(o_add, 1)
                dve.wait_ge(o_add, NB * layer + b + 1)
                norm_stats(2 * layer + 1, b)

            def queries_low(layer):
                for u in range(2 * C):
                    g, half = u // 2, u % 2
                    dve.wait_ge(q_hi, 8 * layer + u + 1)
                    cols = slice(half * HALF_T, (half + 1) * HALF_T)
                    low(QT[:, 1, g, cols], psum[:, O_BANK + u % 2, 0:HALF_T], Q_UNSCALE, QT[:, 0, g, cols])\
                        .then_inc(q_lo, 1)

            def unit_low(gb, par, u):
                dve.wait_ge(proj_hi, gb * NU + u + 1)
                k = J_BANK + u % 2
                if UNITS[u][0] == "K":
                    _, g, half = UNITS[u]
                    cols = slice(half * HALF_K, (half + 1) * HALF_K)
                    low(KT[:, 1, g, cols], psum[:, k, 0:HALF_K], UNSCALE, KT[:, 0, g, cols]).then_inc(proj_lo, 1)
                else:
                    t = UNITS[u][1]
                    r = key_rows(t)
                    low(V[par][0:r, t, :, 1, :], psum[0:r, k, :].rearrange("p (h d) -> p h d", h=NH), UNSCALE,
                        V[par][0:r, t, :, 0, :]).then_inc(proj_lo, 1)

            def row_max(gb, h):
                dve.wait_ge(scores, gb * NH + h + 1)
                v.tensor_reduce(negmax[0:TQ, h % 2:h % 2 + 1], psum[0:TQ, S_BANK:S_BANK + 2, 0:HALF_K], AX.XY, ALU.max,
                                negate=True).then_inc(maxed, 1)

            def probsT_low(gb, h):
                for k in range(2):
                    dve.wait_ge(pt_hi, 2 * (gb * NH + h) + k + 1)
                    low(PT[h % 2][:, 1, 3 * k:3 * k + 3, 0:TQ],
                        psum[:, T_BANK + k, 0:3 * TQ].rearrange("p (t q) -> p t q", t=3), 1.0,
                        PT[h % 2][:, 0, 3 * k:3 * k + 3, 0:TQ]).then_inc(pt_lo, 1)

            def normalise(layer, b, gb, par, half):
                n = 2 * gb + half
                dve.wait_ge(pv, gb * NH + 8 * half + 8)
                v.reciprocal(rrec[0:TQ, :], rowsum[0:TQ, par, 8 * half:8 * half + 8]).then_inc(norm_chain, 1)
                v.tensor_reduce(red[0:TQ, :, :], psum[0:TQ, O_BANK + half, :].rearrange("q (h s d) -> q h d s", h=8, s=2),
                                AX.X, ALU.add).then_inc(norm_chain, 1)
                dve.wait_ge(norm_chain, 2 * n + 2)
                w = D // 2
                out = tok[0:TQ, bass.ds(b, 1), half * w:(half + 1) * w].rearrange("q o (h d) -> q (o h) d", h=8)
                v.tensor_tensor(out, red[0:TQ, :, :], rrec[0:TQ, :].unsqueeze(2).broadcast_to([TQ, 8, DH]), ALU.mult)\
                    .then_inc(attn_rows, 1)

            def value_bias(b, gb):
                dve.wait_ge(attn_rows, 2 * gb + 2)
                rows = tok[0:TQ, bass.ds(b, 1), :].rearrange("q o d -> q (o d)")
                v.tensor_tensor(rows, rows, bvB[0:TQ, :], ALU.add).then_inc(attn_out, 1)

            def attend(layer, b, gb, par, more, peeled=False):
                last_batch = not more
                for s in range(STEPS + 1):
                    if s < NH:
                        row_max(gb, s)
                    if 1 <= s <= NH:
                        probsT_low(gb, s - 1)
                    if more and s >= 1:
                        for u in ENDS_AT[s - 1]:
                            unit_low(gb + 1, 1 - par, u)
                    if s == 11:
                        normalise(layer, b, gb, par, 0)
                    if last_batch:
                        if s - 1 in OT_AT:
                            output_low(layer, OT_AT[s - 1])
                        if s - 1 in LNT_AT:
                            norm_low(2 * layer + 1, LNT_AT[s - 1], J_BANK)
                        if s in ADD_AT:
                            output_add(layer, ADD_AT[s])
                        if s in MOMENTS_AT:
                            norm_moments(2 * layer + 1, MOMENTS_AT[s])
                            norm_variance(2 * layer + 1, MOMENTS_AT[s])
                        if s in APPLY_AT:
                            norm_apply(2 * layer + 1, APPLY_AT[s])
                    if peeled:
                        for chunk in weight_chunks_at(s, layer, b):
                            weight_low(*chunk)
                        for c, e in expert_blocks_at(s, layer, b):
                            block_low(c, e)
                normalise(layer, b, gb, par, 1)
                if layer == 1:
                    value_bias(b, gb)

            def find_top(n, src):
                for b in range(NB):
                    last = v.max(g_m[0:TQ, b, :], src[0:TQ, b, :])
                last.then_inc(g_chain, 1)
                dve.wait_ge(g_chain, n + 1)
                for b in range(NB):
                    last = v.max_index(g_i[0:TQ, b, :], g_m[0:TQ, b, :], src[0:TQ, b, :])
                last.then_inc(g_chain, 1)
                dve.wait_ge(g_chain, n + 2)
                v.tensor_copy(g_f[0:TQ, :, :], g_i[0:TQ, :, :]).then_inc(g_chain, 1)
                dve.wait_ge(g_chain, n + 3)

            full = [TQ, NB, NE]
            expert_ids = eid[0:TQ, :, :].broadcast_to(full)
            logits = psum[0:TQ, O_BANK, 0:NB * NE].rearrange("q (b e) -> q b e", b=NB)

            def route_two():
                dve.wait_ge(g_exp, 1)
                v.tensor_scalar(g_1[0:TQ, :, :], g_e[0:TQ, :, :], 1.0, None, ALU.add).then_inc(g_chain, 1)
                dve.wait_ge(g_chain, 1)
                v.reciprocal(g_s[0:TQ, :, :], g_1[0:TQ, :, :]).then_inc(g_chain, 1)
                dve.wait_ge(g_chain, 2)
                find_top(2, g_s)
                v.tensor_tensor(g_1[0:TQ, :, :], expert_ids, g_f[0:TQ, :, 0:1].broadcast_to(full),
                                ALU.is_equal).then_inc(g_chain, 1)
                v.tensor_tensor(g_2[0:TQ, :, :], expert_ids, g_f[0:TQ, :, 1:2].broadcast_to(full),
                                ALU.is_equal).then_inc(g_chain, 1)
                v.tensor_tensor(g_n[0:TQ, :], g_m[0:TQ, :, 0], g_m[0:TQ, :, 1], ALU.add).then_inc(g_chain, 1)
                dve.wait_ge(g_chain, 8)
                v.tensor_tensor(g_c[0:TQ, :, :], g_1[0:TQ, :, :], g_2[0:TQ, :, :], ALU.add).then_inc(g_chain, 1)
                v.tensor_scalar(g_n[0:TQ, :], g_n[0:TQ, :], 1e-6, None, ALU.add).then_inc(g_chain, 1)
                dve.wait_ge(g_chain, 10)
                v.tensor_tensor(g_1[0:TQ, :, :], g_c[0:TQ, :, :], g_s[0:TQ, :, :], ALU.mult).then_inc(g_chain, 1)
                v.reciprocal(g_m[0:TQ, :, 0], g_n[0:TQ, :]).then_inc(g_chain, 1)
                dve.wait_ge(g_chain, 12)
                v.tensor_tensor(g_c[0:TQ, :, :], g_1[0:TQ, :, :], g_m[0:TQ, :, 0:1].broadcast_to(full),
                                ALU.mult).then_inc(g_chain, 1)
                dve.wait_ge(g_chain, 13)
                v.tensor_copy(g_h[0:TQ, 0, :, :], g_c[0:TQ, :, :]).then_inc(g_chain, 1)
                dve.wait_ge(g_chain, 14)
                v.tensor_tensor(g_h[0:TQ, 1, :, :], g_c[0:TQ, :, :], g_h[0:TQ, 0, :, :], ALU.subtract)\
                    .then_inc(g_done, 1)

            def route_one():
                dve.wait_ge(g_ps, 2)
                v.tensor_copy(g_s[0:TQ, :, :], logits).then_inc(g_chain, 1)
                dve.wait_ge(g_chain, 15)
                find_top(15, g_s)
                v.tensor_tensor(g_c[0:TQ, :, :], expert_ids, g_f[0:TQ, :, 0:1].broadcast_to(full),
                                ALU.is_equal).then_inc(g_chain, 1)
                v.tensor_tensor(g_h[0:TQ, 0, :, :], expert_ids, g_f[0:TQ, :, 0:1].broadcast_to(full),
                                ALU.is_equal).then_inc(g_done, 1)

            def y_scale(xe, u):
                half, m = u // C, u % C
                dve.wait_ge(y_add, xe * 2 * C + u + 1)
                dve.wait_ge(y_ps, xe * 2 * C + u + 1)
                gates = comb[:, bass.ds(xe, 1), half * HALF_T:(half + 1) * HALF_T].rearrange("p o t -> p (o t)")
                v.scalar_tensor_tensor(ytmp[u % 2], psum[:, 4 + u % 4, 0:HALF_T], UNSCALE, gates, ALU.mult, ALU.mult)\
                    .then_inc(y_mul, 1)

            def y_sum(xe, u):
                half, m = u // C, u % C
                cols = slice(half * HALF_T, (half + 1) * HALF_T)
                dve.wait_ge(y_mul, xe * 2 * C + u + 1)
                v.tensor_tensor(yT[:, m, cols], yT[:, m, cols], ytmp[u % 2], ALU.add).then_inc(y_add, 1)

            def y_pieces(xe, us):
                for u in us:
                    y_scale(xe, u)
                    if u % 2 == 1:
                        y_sum(xe, u - 1)
                        y_sum(xe, u)

            def w1_low(xe, k):
                dve.wait_ge(fw_hi, 8 * xe + k + 1)
                ins = low(w1[:, 1, k, :], wf1[:, k, :], W_SCALE, w1[:, 0, k, :])
                if k == C - 1:
                    ins.then_inc(fw_split, 1)

            def w2_low(xe, k, done):
                dve.wait_ge(fw_hi, done)
                ins = low(w2[:, 1, 2 * k:2 * k + 2, :].rearrange("p j n -> p (j n)"),
                          wf[:, 2 * k * D:(2 * k + 2) * D], W_SCALE,
                          w2[:, 0, 2 * k:2 * k + 2, :].rearrange("p j n -> p (j n)"))
                if k == C - 1:
                    ins.then_inc(fw_split, 1)

            def expert0(xe, first):
                if not first:
                    for k in range(C):
                        w1_low(xe, k)
                        y_pieces(xe - 1, (2 * k, 2 * k + 1))
                for n in range(2 * HT):
                    half, j = n // HT, n % HT
                    dve.wait_ge(h_act, xe * 2 * HT + n + 1)
                    cols = slice(half * HALF_T, (half + 1) * HALF_T)
                    v.tensor_tensor(hc[:, 1, j, cols], hs[n % 4], hc[:, 0, j, cols], ALU.subtract).then_inc(h_lo, 1)
                    if first and n == 1:
                        norm_low(1, NB - 1, J_BANK)
                    if first and n == 3:
                        dve.wait_ge(g_ps, 1)
                        v.tensor_tensor(g_e[0:TQ, :, :], logits, bal[0:TQ, :, :].broadcast_to(full), ALU.add)\
                            .then_inc(g_pre, 1)
                        v.memset(yT[:, :, :], 0.0).then_inc(y_add, 2)
                    if first and n == 4:
                        route_two()
                    if n >= 8 and n % 2 == 0:
                        k = n // 2 - 4
                        w2_low(xe, k, 8 * xe + 4 + k + 1)

            def expert1():
                def low_half(n):
                    half, j = n // HT, n % HT
                    cols = slice(half * HALF_T, (half + 1) * HALF_T)
                    dve.wait_ge(h_hi, n + 1)
                    v.tensor_tensor(hc[:, 1, j, cols], hp[n % 2], hc[:, 0, j, cols], ALU.subtract).then_inc(h_lo, 1)

                norm_low(3, NB - 1, J_BANK)
                route_one()
                for n in range(2 * HT):
                    half, j = n // HT, n % HT
                    dve.wait_ge(h_act, NE * 2 * HT + n + 1)
                    dve.wait_ge(comb_out, 16 + 2 * j + half + 1)
                    if n >= 2:
                        dve.wait_ge(h_lo, NE * 2 * HT + n - 1)
                    v.tensor_tensor(hp[n % 2], hs[n % 2], comb[:, j, half * HALF_T:(half + 1) * HALF_T], ALU.mult)\
                        .then_inc(h_mul, 1)
                    if n >= 1:
                        low_half(n - 1)
                    if n >= 9 and n % 2 == 1:
                        k = (n - 9) // 2
                        w2_low(NE, k, 8 * NE + k + 1)
                low_half(2 * HT - 1)

            def x_update(layer, b):
                dve.wait_ge(yt_ps, NB * layer + b + 1)
                v.tensor_tensor(x[0:TQ, b, :], psum[0:TQ, T_BANK + b % 2, :], x[0:TQ, b, :], ALU.add)\
                    .then_inc(x_new, 1)

            v.memset(padB[:, :, :], 0.0).then_inc(bias_split, 1)
            v.memset(mhalf[:, :], -0.5)
            v.memset(ones[:, :], 1.0).then_inc(const_set, 1)

            def query_biases():
                dve.wait_ge(bias_in, 64)
                dve.wait_ge(bias_split, 1)
                v.tensor_scalar(padB[0:1, :, :], biasF[0:1, :, :], W_SCALE, None, ALU.mult)
                v.tensor_scalar(biasHi[32:33, :, :], biasF[32:33, :, :], W_SCALE, None, ALU.mult).then_inc(bias_split, 1)
                dve.wait_ge(bias_split, 2)
                low(padB[32:33, :, :], biasF[32:33, :, :], W_SCALE, biasHi[32:33, :, :]).then_inc(bias_split, 1)
                dve.wait_ge(bias_split, 3)

            for layer in range(2):
                g0 = layer * NB
                n0 = 2 * layer

                def unit(u):
                    unit_low(g0, 0, u)

                if layer == 0:
                    for c in range(C):
                        dve.wait_ge(ctx0_hi, c + 1)
                        ins = v.tensor_tensor(ctxH[0][:, 1, c, :], ctxF[:, c, :], ctxH[0][:, 0, c, :], ALU.subtract)
                    ins.then_inc(ctx_split, 1)
                    for k in (0, 1):
                        for c in range(C):
                            weight_low(0, k, c)
                    dve.wait_ge(x_in, 16)
                    for b in range(NB):
                        norm_stats(0, b)
                    unit(0)
                    query_biases()
                    unit(1)
                else:
                    unit(0)
                    unit(1)
                    for b in range(NB):
                        x_update(0, b)
                    for b in range(NB):
                        dve.wait_ge(x_new, b + 1)
                        norm_stats(2, b)
                for b in range(NB):
                    norm_moments(n0, b)
                unit(2)
                for b in range(NB):
                    norm_variance(n0, b)
                unit(3)
                for b in range(NB):
                    norm_apply(n0, b)
                unit(4)
                unit(5)
                if layer == 0:
                    for c in range(C):
                        weight_low(0, 2, c)
                for b in range(NB):
                    norm_low(n0, b, T_BANK + b % 2)
                unit(6)
                unit(7)
                queries_low(layer)
                if layer == 0:
                    dve.wait_ge(small_in, 16 * 8)
                    v.tensor_scalar(lnsT[:, :, :], lnsT[:, :, :], W_SCALE, None, ALU.mult).then_inc(lns_scaled, 1)
                else:
                    dve.wait_ge(bo_in, 16)
                    for b in range(NB):
                        v.tensor_tensor(x[0:TQ, b, :], x[0:TQ, b, :], boB[0:TQ, :], ALU.add).then_inc(bo_add, 1)
                for k in range(2):
                    v.memset(Pr[k][0:TQ, NK:KT_TILES * P], 0.0)
                    ins = v.memset(PT[k][:, :, :, TQ:P], 0.0)
                ins.then_inc(pad_set, 1)
                for u in range(8, NU):
                    unit(u)
                with dve.Fori(0, 3) as i:
                    for par in range(2):
                        attend(layer, 2 * i + par, g0 + 2 * i + par, par, True)
                attend(layer, NB - 2, g0 + NB - 2, 0, True, peeled=True)
                attend(layer, NB - 1, g0 + NB - 1, 1, False, peeled=True)
                n1 = 2 * layer + 1
                output_low(layer, NB - 1)
                norm_apply(n1, NB - 2)
                norm_low(n1, NB - 2, J_BANK)
                if layer == 0:
                    for k in range(C):
                        w1_low(0, k)
                output_add(layer, NB - 1)
                norm_moments(n1, NB - 1)
                norm_variance(n1, NB - 1)
                norm_apply(n1, NB - 1)
                if layer == 0:
                    expert0(0, True)
                    with dve.Fori(1, NE) as e:
                        expert0(e, False)
                    y_pieces(NE - 1, range(2 * C))
                else:
                    dve.wait_ge(bh_ps, 1)
                    v.tensor_tensor(biasH[:, :], psum[:, O_BANK + 1, 0:NE], b1T[:, :], ALU.add).then_inc(bh_out, 1)
                    dve.wait_ge(b2_hi, 1)
                    low(b2h[0:NE, 1, :], b2f[0:NE, :], W_SCALE, b2h[0:NE, 0, :]).then_inc(b2_split, 1)
                    expert1()
                    for us, bs in ((range(0, 6), range(0, 4)), (range(6, 8), range(4, 8))):
                        for u in us:
                            half, m = u // C, u % C
                            dve.wait_ge(y_ps, 2 * C * NE + u + 1)
                            v.tensor_scalar(yT[:, m, half * HALF_T:(half + 1) * HALF_T], psum[:, 4 + u % 4, 0:HALF_T],
                                            UNSCALE, None, ALU.mult).then_inc(y_mul, 1)
                        for b in bs:
                            x_update(1, b)


def kernel(x, ctx_1024, L0_xattn_w_q, L0_xattn_w_k, L0_xattn_w_v, L0_xattn_w_o, L0_ffn_gate_w,
           L0_ffn_balance_bias, L0_ffn_w1, L0_ffn_w2, L1_xattn_Wq, L1_xattn_bq, L1_xattn_Wk, L1_xattn_bk,
           L1_xattn_Wv, L1_xattn_bv, L1_xattn_Wo, L1_xattn_bo, L1_ffn_Wg, L1_ffn_ln_scale, L1_ffn_ln_bias,
           L1_ffn_W1, L1_ffn_b1, L1_ffn_W2, L1_ffn_b2):
    import concourse.bacc as bacc
    from concourse.bass_utils import run_bass_kernel_spmd

    def chunks(w):
        w = np.asarray(w)
        return w.reshape(-1, P, w.shape[-1]).transpose(1, 0, 2)

    w1_0, w2_0 = np.asarray(L0_ffn_w1), np.asarray(L0_ffn_w2)
    arrays = {
        "x": np.asarray(x).transpose(1, 0, 2),
        "ctx": np.asarray(ctx_1024).transpose(0, 2, 1).reshape(NB, C, P, NK).transpose(0, 2, 1, 3),
        "wq0": chunks(np.asarray(L0_xattn_w_q).T), "wk0": chunks(np.asarray(L0_xattn_w_k).T),
        "wv0": chunks(np.asarray(L0_xattn_w_v).T), "wo0": chunks(np.asarray(L0_xattn_w_o).T),
        "wq1": chunks(np.asarray(L1_xattn_Wq).T), "wk1": chunks(np.asarray(L1_xattn_Wk).T),
        "wv1": chunks(np.asarray(L1_xattn_Wv).T), "wo1": chunks(np.asarray(L1_xattn_Wo).T),
        "bq": np.asarray(L1_xattn_bq).reshape(1, D), "bk": np.asarray(L1_xattn_bk).reshape(1, D),
        "bv": np.asarray(L1_xattn_bv).reshape(D), "bo": np.asarray(L1_xattn_bo).reshape(D),
        "gate0": chunks(np.asarray(L0_ffn_gate_w).T), "gate1": chunks(np.asarray(L1_ffn_Wg).T),
        "bal": np.asarray(L0_ffn_balance_bias).reshape(NE),
        "w1_0": np.stack([chunks(w1_0[e].T).reshape(P, -1) for e in range(NE)]),
        "w2_0": np.stack([chunks(w2_0[e].T).reshape(P, -1) for e in range(NE)]),
        "w1_1": chunks(np.asarray(L1_ffn_W1).transpose(1, 0, 2).reshape(D, NE * HID1)).reshape(P, -1),
        "w2_1": np.asarray(L1_ffn_W2).transpose(1, 0, 2).reshape(P, -1),
        "lns": chunks(np.asarray(L1_ffn_ln_scale).T), "lnb": chunks(np.asarray(L1_ffn_ln_bias).T),
        "b1": np.asarray(L1_ffn_b1).T, "b2": np.asarray(L1_ffn_b2),
        "ident": np.eye(P, dtype=np.float32),
        "eid": np.arange(NE, dtype=np.float32),
    }
    nc = bacc.Bacc("TRN2", target_bir_lowering=False, num_devices=1)
    feeds, a = {}, {}
    for name, value in arrays.items():
        value = np.ascontiguousarray(value)
        feeds[f"in_{name}"] = value
        a[name] = nc.dram_tensor(f"in_{name}", value.shape, mybir.dt.from_np(value.dtype), kind="ExternalInput").ap()
    a["out"] = nc.dram_tensor("out_rows", (TQ, NB, D), mybir.dt.float32, kind="ExternalOutput").ap()
    build(nc, a)
    r = run_bass_kernel_spmd(nc, [feeds], core_ids=[0])
    return np.ascontiguousarray(r.results[0]["out_rows"].transpose(1, 0, 2))
```

```python
from contextlib import ExitStack

import concourse.bass as bass
import numpy as np
from concourse import mybir

NB, TQ, D = 8, 100, 512
NT = NB * TQ
NK = 722
NH, DH = 16, 32
NE = 8
HID0 = 1024
HID1 = 128
P = 128
C = D // P
HALF_K = NK // 2
HALF_T = NT // 2
KT_TILES = -(-NK // P)
LAST_K = NK - (KT_TILES - 1) * P
HT = HID0 // P
W_SCALE = 256.0
UNSCALE = 1.0 / W_SCALE
Q_UNSCALE = UNSCALE / float(np.sqrt(DH))
LN_EPS = 1e-5


def key_rows(t):
    return LAST_K if t == KT_TILES - 1 else P


UNITS = [("K", 0, 0), ("K", 0, 1), ("V", 0), ("V", 1), ("K", 1, 0), ("V", 2), ("K", 1, 1),
         ("K", 2, 0), ("V", 3), ("K", 2, 1), ("V", 4), ("K", 3, 0), ("V", 5), ("K", 3, 1)]
NU = len(UNITS)
V_FIRST = UNITS.index(("V", 0))
STEPS = NH + 2
K_UNIT = {(u[1], u[2]): n for n, u in enumerate(UNITS) if u[0] == "K"}
PAIR_LAST = [K_UNIT[(1, 1)], K_UNIT[(3, 1)]]


def pass_steps():
    width = [D if u[0] == "V" else HALF_K for u in UNITS]
    total, done = 3 * C * sum(width), 0
    steps = [[] for _ in range(NH)]
    for u in range(NU):
        for c in range(C):
            for k in range(3):
                done += width[u]
                steps[max(0, (done * NH - total // 8) // total)].append((u, c, k))
    return steps


PASSES_AT = pass_steps()
ENDS_AT = [[u for u, c, k in step if (c, k) == (C - 1, 2)] for step in PASSES_AT]
for pair in range(2):
    assert PAIR_LAST[pair] in sum(ENDS_AT[8 * pair + 7:], [])
assert max(map(len, ENDS_AT)) <= 2


def build(nc, a):
    fp32, fp16, u32 = mybir.dt.float32, mybir.dt.float16, mybir.dt.uint32
    ALU = mybir.AluOpType
    ACT = mybir.ActivationFunctionType
    AX = mybir.AxisListType

    ctx = ExitStack()
    with ctx:
        def sb(name, shape, dt=fp32):
            return ctx.enter_context(nc.sbuf_tensor(name, shape, dt))

        def sem(name):
            return ctx.enter_context(nc.semaphore(name))

        x = sb("x", [P, NB, D])
        tok = sb("tok", [P, NB, D])
        xT = sb("xT", [P, 2, C, NT], fp16)
        xTf = sb("xTf", [P, C, NT])
        yT = xTf
        QT = xTf[:, :, :].rearrange("p c t -> p (c t)").bitcast(fp16).rearrange(
            "p (s c t) -> p s c t", s=2, c=C)
        W = sb("W", [P, 4, 2, C, D], fp16)
        ident = sb("ident", [P, P])
        ident16 = sb("ident16", [P, P], fp16)
        eid = sb("eid", [P, 1, NE])
        gateT = sb("gateT", [P, 2, C, NE])
        bal = sb("bal", [P, 1, NE])
        bvB = sb("bvB", [P, D])
        padB = sb("padB", [P, 2, D], fp16)
        ones = sb("ones", [P, 2], fp16)
        lnsT = sb("lnsT", [P, C, NE])
        lnbT = sb("lnbT", [P, C, NE])
        b1T = sb("b1T", [P, NE])
        biasH = sb("biasH", [P, NE])
        bst = sb("bst", [P, NB, 6])
        mv = sb("mv", [P, NB, 2])
        ve = sb("ve", [P, NB])
        mhalf = sb("mhalf", [P, 1])
        rstd = sb("rstd", [P, NB])
        red = sb("red", [P, NH // 2, DH])
        rowsum = sb("rowsum", [P, 2, NH])
        rrec = sb("rrec", [P, NH // 2])
        negmax = sb("negmax", [P, 2])

        AREA = 28144
        arena = sb("arena", [P, AREA])
        at = [0]

        def part(words, dt=fp32):
            v = arena[:, at[0]:at[0] + words]
            at[0] += words
            return v if dt == fp32 else v.bitcast(dt)

        ctxF = part(C * NK).rearrange("p (c n) -> p c n", c=C)
        ctxH = [part(C * NK, fp16).rearrange("p (s c n) -> p s c n", s=2, c=C) for _ in range(2)]
        kt_at = at[0]
        KT = part(C * NK, fp16).rearrange("p (s g n) -> p s g n", s=2, g=C)
        kst_at = at[0]
        Kst = part(NH * NK // 2, fp16).rearrange("p (h n) -> p h n", h=NH)
        V = [part(KT_TILES * NH * DH, fp16).rearrange("p (t h s d) -> p t h s d", t=KT_TILES, h=NH, s=2)
             for _ in range(2)]
        qst_at = at[0]
        Qst = [part(NH * TQ // 2, fp16).rearrange("p (h q) -> p h q", h=NH) for _ in range(2)]
        pr_at = at[0]
        Pr = [part(KT_TILES * P) for _ in range(2)]
        pt_at = at[0]
        PT = [part(KT_TILES * P, fp16).rearrange("p (s t q) -> p s t q", s=2, t=KT_TILES) for _ in range(2)]
        assert at[0] <= AREA

        def stage_at(words):
            return arena[:, words:words + C * D].rearrange("p (c n) -> p c n", c=C)

        out_stage = stage_at(0)
        Wf = [[stage_at(kst_at), stage_at(kst_at + C * D), stage_at(qst_at), out_stage],
              [stage_at(0), stage_at(2 * C * NK), stage_at(C * NK), out_stage]]
        boB = arena[:, pr_at:pr_at + D]

        at[0] = 0
        wf = part(C * HID0)
        w1 = part(C * HID0, fp16).rearrange("p (s c n) -> p s c n", s=2, c=C)
        hs = [part(HALF_T) for _ in range(4)]
        hp = hs[2:]
        hc = part(HT * NT, fp16).rearrange("p (s j t) -> p s j t", s=2, j=HT)
        comb = part(NE * NT).rearrange("p (e t) -> p e t", e=NE)
        w2 = part(C * HID0, fp16).rearrange("p (s j n) -> p s j n", s=2, j=HT)
        ytmp = [part(HALF_T) for _ in range(2)]
        g_e = part(NB * NE).rearrange("p (b e) -> p b e", b=NB)
        g_s = part(NB * NE).rearrange("p (b e) -> p b e", b=NB)
        g_m = part(NB * 8).rearrange("p (b e) -> p b e", b=NB)
        g_i = part(NB * 8, u32).rearrange("p (b e) -> p b e", b=NB)
        g_f = part(NB * 8).rearrange("p (b e) -> p b e", b=NB)
        g_1 = part(NB * NE).rearrange("p (b e) -> p b e", b=NB)
        g_2 = part(NB * NE).rearrange("p (b e) -> p b e", b=NB)
        g_c = part(NB * NE).rearrange("p (b e) -> p b e", b=NB)
        g_h = part(NB * NE, fp16).rearrange("p (s b e) -> p s b e", s=2, b=NB)
        g_n = part(NB)
        assert at[0] <= AREA
        w1m = [arena[:, kt_at + k * HID0:kt_at + (k + 1) * HID0] for k in range(2)]
        wf1 = wf.rearrange("p (c n) -> p c n", c=C)
        wfe = wf.rearrange("p (c e n) -> p c e n", c=C, e=NE)
        Wflat = W[:, :, :, :, :].rearrange("p w s c n -> p (w s c n)")
        b2f = Wflat[:, 0:2 * D].bitcast(fp32)
        b2h = Wflat[:, 2 * D:4 * D].rearrange("p (s n) -> p s n", s=2)
        maskT = Wflat[:, 4 * D:4 * D + NT]
        biasF = arena[:, pt_at:pt_at + 2 * D].rearrange("p (s n) -> p s n", s=2)
        biasHi = arena[:, pt_at + 2 * D:pt_at + 3 * D].bitcast(fp16).rearrange("p (s n) -> p s n", s=2)

        psum = ctx.enter_context(nc.psum_tensor("psum", [P, 8, 512], fp32))
        S_BANK, T_BANK, O_BANK, J_BANK = 0, 2, 4, 6
        hidden_bias = psum[:, O_BANK + 1, 0:NE]
        OT_BANK = [J_BANK] * (NB - 1) + [O_BANK + 1]
        LOGITS_OUT = (15, 20)
        SPREAD_BANKS = (O_BANK + 1, J_BANK + 1)

        x_in, ident_in, small_in, bias_in = sem("x_in"), sem("ident_in"), sem("small_in"), sem("bias_in")
        bo_in, bo_add, const_set, bias_split = sem("bo_in"), sem("bo_add"), sem("const_set"), sem("bias_split")
        pad_set, id16_set, lns_scaled = sem("pad_set"), sem("id16_set"), sem("lns_scaled")
        w_in = [sem(f"w_in{k}") for k in range(4)]
        w_hi, w_split, w_scaled = sem("w_hi"), sem("w_split"), sem("w_scaled")
        ln_st, ln_ag, ln_var, ln_rs, ln_out = sem("ln_st"), sem("ln_ag"), sem("ln_var"), sem("ln_rs"), sem("ln_out")
        ts_ps, ts_hi, ts_lo = sem("ts_ps"), sem("ts_hi"), sem("ts_lo")
        ot_ps, ot_hi, ot_lo = sem("ot_ps"), sem("ot_hi"), sem("ot_lo")
        q_ps, q_hi, q_lo = sem("q_ps"), sem("q_hi"), sem("q_lo")
        qst_in = [sem(f"qst_in{k}") for k in range(2)]
        kst_in = [sem(f"kst_in{k}") for k in range(2)]
        ctx_in, ctx_begun, ctx_hi, ctx_split = sem("ctx_in"), sem("ctx_begun"), sem("ctx_hi"), sem("ctx_split")
        ctx0_hi = sem("ctx0_hi")
        proj_ps, proj_hi, proj_lo = sem("proj_ps"), sem("proj_hi"), sem("proj_lo")
        scores, maxed, probs = sem("scores"), sem("maxed"), sem("probs")
        probsT, pt_hi, pt_lo = sem("probsT"), sem("pt_hi"), sem("pt_lo")
        pv, norm_chain, attn_rows, attn_out = sem("pv"), sem("norm_chain"), sem("attn_rows"), sem("attn_out")
        o_ps, o_add = sem("o_ps"), sem("o_add")
        g_ps, g_pre, g_exp, g_chain, g_done = sem("g_ps"), sem("g_pre"), sem("g_exp"), sem("g_chain"), sem("g_done")
        comb_ps, comb_out = sem("comb_ps"), sem("comb_out")
        w1_begun = sem("w1_begun")
        wf_in, fw_hi, fw_split = sem("wf_in"), sem("fw_hi"), sem("fw_split")
        h_ps, h_act, h_mul, h_hi, h_lo = sem("h_ps"), sem("h_act"), sem("h_mul"), sem("h_hi"), sem("h_lo")
        y_ps, y_mul, y_add = sem("y_ps"), sem("y_mul"), sem("y_add")
        yt_ps, x_new = sem("yt_ps"), sem("x_new")
        b2_in, b2_hi, b2_split = sem("b2_in"), sem("b2_hi"), sem("b2_split")
        mask_ps, mask_out = sem("mask_ps"), sem("mask_out")
        bh_ps, bh_out = sem("bh_ps"), sem("bh_out")
        w1m_scaled, w1m_hi, w1m_lo = sem("w1m_scaled"), sem("w1m_hi"), sem("w1m_lo")
        out_written = sem("out_written")

        OT_AT = {max(2 * k, 1): k for k in range(NB - 1)}
        PROD_AT = {2 * k + 2 + i: (k, i) for k in range(NB - 1) for i in range(2)}
        ADD_AT = {2 * k + 4: k for k in range(NB - 1)}
        MOMENTS_AT = {2 * k + 5: k for k in range(NB - 1)}
        APPLY_AT = {2 * k + 6: k for k in range(6)}
        LNT_AT = {2 * k + 7: k for k in range(6)}

        def weight_chunks_at(s, layer, b):
            if b == NB - 2 and 4 <= s < 8:
                return [(layer, 3, s - 4)]
            if b == NB - 2 and layer == 0 and 8 <= s < 12:
                return [(1, 2, s - 8)]
            if b == NB - 1 and layer == 0 and 3 <= s < 11:
                return [(1, (s - 3) // C, (s - 3) % C)]
            return []

        def expert_chunks_at(s, layer, b):
            if layer == 0 and b == NB - 1 and 11 <= s < 15:
                return [s - 11]
            return []

        SPREAD_AT = ({9: range(0, 2), 10: range(2, 4), 11: range(4, 6), 12: range(6, 8), 13: range(8, 10),
                      14: range(10, 13), 15: range(13, 16)},
                     {3: range(0, 3), 4: range(3, 5), 5: range(5, 8), 6: range(8, 11), 7: range(11, 13),
                      8: range(13, 16)})
        HIDDEN_BIAS_AT = {3: (0,), 4: (1,), 5: (2,), 6: (3,), 7: (4, 5), 8: (6,), 9: (7,)}
        POOL_CHUNKS = C // 2

        NORM_W1_SCALE_AT = {4 + 2 * c: c for c in range(C)}
        NORM_W1_HIGH_AT = {5 + 2 * c: c for c in range(C)}
        NORM_W1_LOW_AT = {6 + 2 * c: c for c in range(C)}

        W_ORDER = ((0, 1, 2, 3), (2, 0, 1, 3))

        def w_count(layer, k, c):
            return 16 * layer + 4 * W_ORDER[layer].index(k) + c + 1

        def head(gb, par, h):
            return (gb, par, h) if h >= 0 else (gb - 1, 1 - par, h + NH)

        block = ctx.enter_context(nc.Block())

        @block.sync
        def _(sp):
            def load_weights(layer, k):
                sp.dma_start(Wf[layer][k], a[("wk", "wv", "wq", "wo")[k] + str(layer)]).then_inc(w_in[k], 16)

            def apart():
                sp.wait_ge(x_in, 16)

            def load_ctx(b):
                sp.dma_start(ctxF[:, :, :], a["ctx"][bass.ds(b, 1), :, :, :].rearrange("o p c n -> p (o c) n"))\
                    .then_inc(ctx_in, 16)

            def stack_q(b, par):
                for r in range(3):
                    for j in range(4):
                        src = QT[32 * j:32 * j + 32, r // 2, :, bass.ds(b * TQ, TQ)]
                        sp.dma_start(Qst[par][32 * r:32 * r + 32, j:NH:4, :], src).then_inc(qst_in[par], 16)

            def stack_k(gb, pair):
                sp.wait_ge(proj_lo, gb * NU + PAIR_LAST[pair] + 1)
                for r in range(3):
                    for j in range(4):
                        sp.dma_start(Kst[32 * r:32 * r + 32, 8 * pair + j:8 * pair + 8:4, :],
                                     KT[32 * j:32 * j + 32, r % 2, 2 * pair:2 * pair + 2, :])\
                            .then_inc(kst_in[pair], 16)

            sp.dma_start(ctxF[:, :, :], a["ctx"][0]).then_inc(ctx_in, 16)
            load_weights(0, 0)
            load_weights(0, 1)
            sp.dma_start(x[0:TQ, :, :], a["x"]).then_inc(x_in, 16)
            load_weights(0, 2)
            sp.dma_start(ident[:, :], a["ident"]).then_inc(ident_in, 16)
            sp.dma_start(biasF[0:1, 0, :], a["bq"]).then_inc(bias_in, 16)
            sp.dma_start(biasF[0:1, 1, :], a["bk"]).then_inc(bias_in, 16)
            sp.dma_start(biasF[32:33, 0, :], a["bq"]).then_inc(bias_in, 16)
            sp.dma_start(biasF[32:33, 1, :], a["bk"]).then_inc(bias_in, 16)
            sp.dma_start(eid[0:TQ, 0, :], a["eid"].partition_broadcast(TQ)).then_inc(small_in, 16)
            sp.dma_start(gateT[:, 0, :, :], a["gate0"]).then_inc(small_in, 16)
            sp.dma_start(gateT[:, 1, :, :], a["gate1"]).then_inc(small_in, 16)
            sp.dma_start(bal[0:TQ, 0, :], a["bal"].partition_broadcast(TQ)).then_inc(small_in, 16)
            sp.dma_start(bvB[0:TQ, :], a["bv"].partition_broadcast(TQ)).then_inc(small_in, 16)
            sp.dma_start(lnsT[:, :, :], a["lns"]).then_inc(small_in, 16)
            sp.dma_start(lnbT[:, :, :], a["lnb"]).then_inc(small_in, 16)
            sp.dma_start(b1T[:, :], a["b1"]).then_inc(small_in, 16)

            for layer in range(2):
                g0 = layer * NB
                if layer == 1:
                    sp.wait_ge(fw_split, 2 * NE)
                    load_ctx(0)
                sp.wait_ge(ctx_split, g0 + 1)
                load_ctx(1)
                if layer == 1:
                    sp.wait_ge(y_ps, 2 * C * NE)
                    sp.dma_start(boB[0:TQ, :], a["bo"].partition_broadcast(TQ)).then_inc(bo_in, 16)
                stack_k(g0, 0)
                sp.wait_ge(q_lo, 8 * layer + C)
                stack_q(0, 0)
                stack_k(g0, 1)

                def next_stacks(b, gb, par, between=lambda: None):
                    stack_q(b + 1, 1 - par)
                    stack_k(gb + 1, 0)
                    between()
                    stack_k(gb + 1, 1)

                with sp.Fori(0, 3) as i:
                    for par in range(2):
                        b, gb = 2 * i + par, g0 + 2 * i + par
                        sp.wait_ge(ctx_split, gb + 2)
                        apart()
                        load_ctx(b + 2)
                        next_stacks(b, gb, par)
                sp.wait_ge(ctx_split, g0 + NB)
                load_weights(layer, 3)
                if layer == 0:
                    sp.wait_ge(proj_ps, (NB - 1) * NU)
                    load_weights(1, 2)

                def next_weights():
                    sp.wait_ge(w_split, w_count(layer, 3, 3))
                    if layer == 0:
                        load_weights(1, 0)
                    else:
                        sp.wait_ge(proj_ps, (g0 + NB - 1) * NU)
                        sp.dma_start(wf, a["w1_1"]).then_inc(wf_in, 16)

                next_stacks(NB - 2, g0 + NB - 2, 0, next_weights)
                sp.wait_ge(proj_ps, (g0 + NB) * NU)

                if layer == 0:
                    load_weights(1, 1)
                    sp.wait_ge(w_split, w_count(1, 0, 3))
                    sp.dma_start(wf, a["w1_0"][0]).then_inc(wf_in, 16)
                    sp.wait_ge(fw_split, 1)
                    sp.dma_start(wf, a["w2_0"][0]).then_inc(wf_in, 16)
                    with sp.Fori(1, NE) as e:
                        sp.wait_ge(fw_split, 2 * e)
                        apart()
                        sp.dma_start(wf, a["w1_0"][bass.ds(e, 1), :, :].rearrange("o p n -> p (o n)"))\
                            .then_inc(wf_in, 16)
                        sp.wait_ge(fw_split, 2 * e + 1)
                        apart()
                        sp.dma_start(wf, a["w2_0"][bass.ds(e, 1), :, :].rearrange("o p n -> p (o n)"))\
                            .then_inc(wf_in, 16)
                else:
                    sp.dma_start(b2f[0:NE, :], a["b2"]).then_inc(b2_in, 16)
                    sp.wait_ge(fw_split, 2 * NE + 1)
                    sp.wait_ge(bh_ps, 1)
                    sp.dma_start(wf, a["w2_1"]).then_inc(wf_in, 16)

            for b in range(NB):
                sp.wait_ge(x_new, NB + b + 1)
                sp.dma_start(a["out"][:, b, :], x[0:TQ, b, :]).then_inc(out_written, 16)
            sp.wait_ge(out_written, 16 * NB)

        @block.gpsimd
        def _(pool):
            def split_ctx(gb, par):
                pool.wait_ge(ctx_in, 16 * (gb + 1))
                pool.sem_inc(ctx_begun, 1)
                nc.gpsimd.tensor_copy(ctxH[par][:, 0, :, :], ctxF[:, :, :]).then_inc(ctx_hi, 1)
                pool.wait_ge(ctx_hi, gb)
                nc.gpsimd.tensor_tensor(ctxH[par][:, 1, :, :], ctxF[:, :, :], ctxH[par][:, 0, :, :], ALU.subtract)\
                    .then_inc(ctx_split, 1)

            def norm_root(n, b):
                pool.wait_ge(ln_var, NB * n + b + 1)
                nc.gpsimd.tensor_tensor(rstd[0:TQ, b:b + 1], ve[0:TQ, b:b + 1], mhalf[0:TQ, :], ALU.pow)\
                    .then_inc(ln_rs, 1)

            def norm_roots(n, half):
                rows = slice(4 * half, 4 * half + 4)
                pool.wait_ge(ln_var, NB * n + 4 * half + 4)
                nc.gpsimd.tensor_tensor(rstd[0:TQ, rows], ve[0:TQ, rows], mhalf[0:TQ, :].broadcast_to([TQ, 4]), ALU.pow)\
                    .then_inc(ln_rs, 4)

            def rescale(weights):
                nc.gpsimd.tensor_scalar(weights, weights, W_SCALE, None, ALU.mult).then_inc(w_scaled, 1)

            def weight_scale(layer, k, c):
                pool.wait_ge(w_in[k], 16 * (layer + 1))
                rescale(Wf[layer][k][:, c, :])

            def norm_w1_scale(c):
                if c == 0:
                    pool.wait_ge(kst_in[1], 2 * NB * 192)
                    pool.wait_ge(wf_in, 16 * (2 * NE + 1))
                    pool.wait_ge(lns_scaled, 1)
                if c >= 2:
                    pool.wait_ge(w1m_lo, c - 1)
                nc.gpsimd.tensor_tensor(w1m[c % 2].rearrange("p (e n) -> p e n", e=NE), wfe[:, c, :, :],
                                        lnsT[:, c, :].unsqueeze(2).broadcast_to([P, NE, P]), ALU.mult)\
                    .then_inc(w1m_scaled, 1)

            def norm_w1_low(c):
                pool.wait_ge(w1m_hi, c + 1)
                nc.gpsimd.tensor_tensor(w1[:, 1, c, :], w1m[c % 2], w1[:, 0, c, :], ALU.subtract).then_inc(w1m_lo, 1)
                if c == C - 1:
                    pool.wait_ge(w1m_lo, C)
                    pool.sem_inc(fw_split, 1)

            def w1_scale(k):
                pool.wait_ge(wf_in, 16)
                rescale(wf1[:, k, :])

            def weight_low(layer, k, c):
                pool.wait_ge(w_hi, w_count(layer, k, c))
                nc.gpsimd.tensor_tensor(W[:, k, 1, c, :], Wf[layer][k][:, c, :], W[:, k, 0, c, :], ALU.subtract)\
                    .then_inc(w_split, 1)

            def w1_low(k):
                pool.wait_ge(fw_hi, k + 1)
                nc.gpsimd.tensor_tensor(w1[:, 1, k, :], wf1[:, k, :], w1[:, 0, k, :], ALU.subtract).then_inc(w1_begun, 1)

            pool.wait_ge(const_set, 1)
            for layer in range(2):
                g0 = layer * NB
                if layer == 1:
                    pool.wait_ge(h_ps, 2 * HT * NE)
                    split_ctx(g0, 0)
                norm_roots(2 * layer, 0)
                norm_roots(2 * layer, 1)
                split_ctx(g0 + 1, 1)
                with pool.Fori(0, 3) as i:
                    for par in range(2):
                        gb = g0 + 2 * i + par
                        pool.wait_ge(proj_ps, (gb + 1) * NU)
                        split_ctx(gb + 2, par)
                for s in range(STEPS):
                    for chunk in weight_chunks_at(s + 1, layer, NB - 1):
                        weight_scale(*chunk)
                    for k in expert_chunks_at(s + 1, layer, NB - 1):
                        if k >= C - POOL_CHUNKS:
                            w1_scale(k)
                    for chunk in weight_chunks_at(s, layer, NB - 1):
                        weight_low(*chunk)
                    for k in expert_chunks_at(s, layer, NB - 1):
                        if k >= C - POOL_CHUNKS:
                            w1_low(k)
                    if layer == 1 and s in NORM_W1_LOW_AT:
                        norm_w1_low(NORM_W1_LOW_AT[s])
                    if layer == 1 and s in NORM_W1_SCALE_AT:
                        norm_w1_scale(NORM_W1_SCALE_AT[s])
                    if s in MOMENTS_AT:
                        norm_root(2 * layer + 1, MOMENTS_AT[s])
                norm_root(2 * layer + 1, NB - 1)
                if layer == 0:
                    pool.wait_ge(g_ps, 1)
                    nc.gpsimd.memset(yT[:, :, :], 0.0).then_inc(y_add, 2)

        @block.tensor
        def _(pe):
            mm = nc.tensor.matmul

            def bank(k, rows, cols):
                return psum[0:rows, k, 0:cols]

            def rows_transpose(k, b, done):
                for c in range(C):
                    last = nc.tensor.transpose(psum[:, k, c * TQ:(c + 1) * TQ],
                                               tok[0:TQ, b, c * P:(c + 1) * P], ident[0:TQ, 0:TQ])
                last.then_inc(done, 1)

            def three(out, lhs, rhs, first=True, last=True, passes=range(3)):
                n = len(lhs)
                for c in range(n):
                    for k in passes:
                        l_, r_ = lhs[c][k == 2], rhs[c][k == 1]
                        ins = mm(out, l_, r_, start=first and c == 0 and k == 0,
                                 stop=last and c == n - 1 and k == 2)
                return ins

            def xT_of(c, cols):
                return tuple(xT[:, s, c, cols] for s in range(2))

            def queries(layer, us):
                for u in us:
                    half, g = u // C, u % C
                    if u == 0:
                        pe.wait_ge(w_split, w_count(layer, 2, 3))
                        pe.wait_ge(ts_lo, NB * 2 * layer + NB)
                    if u >= 2:
                        pe.wait_ge(q_lo, 8 * layer + u - 1)
                    out = bank(O_BANK + u % 2, P, HALF_T)
                    if layer == 1:
                        mm(out, padB[:, 0, g * P:(g + 1) * P], ones[:, 0:1].broadcast_to([P, HALF_T]),
                           start=True, stop=False)
                    cols = slice(g * P, (g + 1) * P)
                    three(out, [(W[:, 2, 0, c, cols], W[:, 2, 1, c, cols]) for c in range(C)],
                          [xT_of(c, slice(half * HALF_T, (half + 1) * HALF_T)) for c in range(C)],
                          first=layer == 0).then_inc(q_ps, 1)

            def project(layer, gb, par, u, c, passes=range(3), static_first=False):
                begins = c == 0 and passes[0] == 0
                if begins:
                    if u == 0:
                        pe.wait_ge(ctx_split, gb + 1)
                    if static_first and u < 2:
                        if u == 0:
                            pe.wait_ge(w_split, w_count(layer, 0, 3))
                        if layer == 1:
                            pe.wait_ge(y_mul, 2 * C * NE)
                    else:
                        pe.wait_ge(proj_lo, gb * NU + u - 1)
                    if static_first and u == V_FIRST:
                        pe.wait_ge(w_split, w_count(layer, 1, 3))
                k = J_BANK + u % 2
                ends = dict(first=c == 0, last=c == C - 1, passes=passes)
                if UNITS[u][0] == "K":
                    _, g, half = UNITS[u]
                    out = bank(k, P, HALF_K)
                    if layer == 1 and begins:
                        mm(out, padB[:, 1, g * P:(g + 1) * P], ones[:, 0:1].broadcast_to([P, HALF_K]),
                           start=True, stop=False)
                    if layer == 1:
                        ends["first"] = False
                    cols = slice(g * P, (g + 1) * P)
                    ins = three(
                        out, [(W[:, 0, 0, c, cols], W[:, 0, 1, c, cols])],
                        [tuple(ctxH[par][:, s, c, half * HALF_K:(half + 1) * HALF_K] for s in range(2))], **ends)
                else:
                    t = UNITS[u][1]
                    r = key_rows(t)
                    ins = three(
                        bank(k, r, D), [tuple(ctxH[par][:, s, c, t * P:t * P + r] for s in range(2))],
                        [(W[:, 1, 0, c, :], W[:, 1, 1, c, :])], **ends)
                if c == C - 1 and passes[-1] == 2:
                    ins.then_inc(proj_ps, 1)

            def score(gb, par, h, first):
                if h % 8 == 0:
                    pe.wait_ge(kst_in[h // 8], 192 * (gb + 1))
                if h > 0 or not first:
                    pe.wait_ge(probs, gb * NH + h)
                for half in range(2):
                    last = mm(psum[0:TQ, S_BANK + half, 0:HALF_K], Qst[par][0:96, h, :],
                              Kst[0:96, h, half * HALF_K:(half + 1) * HALF_K], start=True, stop=True)
                last.then_inc(scores, 1)

            def probs_transpose(gb, h, first):
                pe.wait_ge(probs, gb * NH + h + 1)
                for k in range(2):
                    if h > 0 or not first:
                        pe.wait_ge(pt_lo, 2 * (gb * NH + h) + k - 1)
                    for t in range(3):
                        last = nc.tensor.transpose(psum[:, T_BANK + k, t * TQ:(t + 1) * TQ],
                                                   Pr[h % 2][0:TQ, (3 * k + t) * P:(3 * k + t + 1) * P],
                                                   ident[0:TQ, 0:TQ])
                    last.then_inc(probsT, 1)

            def values(gb, par, h):
                if h == 0:
                    pe.wait_ge(proj_lo, (gb + 1) * NU)
                pe.wait_ge(pt_lo, 2 * (gb * NH + h + 1))
                half, k = h // 8, h % 8
                for t in range(KT_TILES):
                    r = key_rows(t)
                    for s in range(2):
                        last = mm(psum[:, O_BANK + half, k * 2 * DH:(k + 1) * 2 * DH],
                                  PT[h % 2][0:r, s, t, :],
                                  V[par][0:r, t, h, :, :].rearrange("p s d -> p (s d)"),
                                  start=t == 0 and s == 0, stop=t == KT_TILES - 1 and s == 1)
                last.then_inc(pv, 1)

            def output_transpose(layer, k):
                if 4 <= k < NB - 1:
                    pe.wait_ge(ts_lo, NB * (2 * layer + 1) + k - 3)
                elif k == 0:
                    pe.wait_ge(proj_lo, NB * (layer + 1) * NU)
                elif k < NB - 1:
                    pe.wait_ge(ot_lo, NB * layer + k)
                if layer == 0:
                    pe.wait_ge(attn_rows, 2 * k + 2)
                else:
                    pe.wait_ge(attn_out, k + 1)
                rows_transpose(OT_BANK[k], k, ot_ps)

            def output_product(layer, k, half):
                if k == 0 and half == 0:
                    pe.wait_ge(w_split, w_count(layer, 3, 3))
                if half == 0:
                    pe.wait_ge(ot_lo, NB * layer + k + 1)
                    if k > 0:
                        pe.wait_ge(o_add, NB * layer + k)
                cs = (2 * half, 2 * half + 1)
                ins = three(bank(J_BANK + 1, TQ, D), [xT_of(c, slice(k * TQ, (k + 1) * TQ)) for c in cs],
                            [(W[:, 3, 0, c, :], W[:, 3, 1, c, :]) for c in cs], first=half == 0, last=half == 1)
                if half == 1:
                    ins.then_inc(o_ps, 1)

            def norm_transpose(layer, k):
                if k <= 3:
                    pe.wait_ge(ot_lo, NB * layer + k + 4)
                else:
                    pe.wait_ge(ts_lo, NB * (2 * layer + 1) + k)
                pe.wait_ge(ln_out, NB * (2 * layer + 1) + k + 1)
                rows_transpose(J_BANK, k, ts_ps)

            def attend(layer, gb, par, first=False, more=True):
                pe.wait_ge(qst_in[par], (gb - par) * 96 + 192)
                for s in range(NH if more else STEPS):
                    if s < NH:
                        score(gb, par, s, first)
                    if (s > 0 or not first) and s <= NH:
                        probs_transpose(*head(gb, par, s - 1)[::2], first)
                    if not more and layer == 1 and s == 10:
                        pe.wait_ge(bh_out, 1)
                    if s >= 2 or not first:
                        values(*head(gb, par, s - 2))
                    if more:
                        for u, c, k in PASSES_AT[s]:
                            project(layer, gb + 1, 1 - par, u, c, passes=(k,))
                    elif layer == 1 and s in HIDDEN_BIAS_AT:
                        hidden_biases(HIDDEN_BIAS_AT[s])
                    if not more and s in PROD_AT:
                        output_product(layer, *PROD_AT[s])
                    if not more and s in OT_AT:
                        output_transpose(layer, OT_AT[s])
                    if not more and s in LNT_AT:
                        norm_transpose(layer, LNT_AT[s])
                    if not more and s >= NH:
                        for b in (2 * (s - NH), 2 * (s - NH) + 1):
                            gate(layer, b)

            def gate(layer, b):
                if b == 0:
                    pe.wait_ge(small_in, 16 * 8)
                    pe.wait_ge(attn_rows, 2 * NB * (layer + 1) - 1)
                if layer == 1 and b == NB // 2:
                    pe.wait_ge(g_chain, LOGITS_OUT[0])
                pe.wait_ge(ts_lo, NB * (2 * layer + 1) + b + 1)
                for c in range(C):
                    last = mm(psum[0:TQ, O_BANK, b * NE:(b + 1) * NE], xTf[:, c, b * TQ:(b + 1) * TQ],
                              gateT[:, layer, c, :], start=c == 0, stop=c == C - 1)
                if b == NB - 1 or layer == 1 and b == NB // 2 - 1:
                    last.then_inc(g_ps, 1)

            def hidden_biases(es):
                if 0 in es:
                    pe.wait_ge(wf_in, 16 * (2 * NE + 1))
                    pe.wait_ge(attn_rows, 4 * NB - 2)
                for e in es:
                    for c in range(C):
                        last = mm(hidden_bias[:, e:e + 1], wf1[:, c, e * P:(e + 1) * P],
                                  lnbT[:, c, e:e + 1], start=c == 0, stop=c == C - 1)
                if NE - 1 in es:
                    last.then_inc(bh_ps, 1)

            def spread_gates(layer, ns):
                splits = 2 if layer == 0 else 1
                for n in ns:
                    half, e = n // NE, n % NE
                    if e == 0:
                        pe.wait_ge(g_done, 1 if layer == 0 else 2 + half)
                    if n == 0:
                        pe.wait_ge(id16_set, 1)
                        pe.wait_ge(o_add, NB * (layer + 1))
                    if n >= 2:
                        pe.wait_ge(comb_out, 16 * layer + n - 1)
                    for k in range(4):
                        b = 4 * half + k
                        for s in range(splits):
                            last = mm(psum[:, SPREAD_BANKS[n % 2], k * TQ:(k + 1) * TQ],
                                      g_h[0:TQ, s, b, e:e + 1].broadcast_to([TQ, P]), ident16[0:TQ, 0:TQ],
                                      start=s == 0, stop=s == splits - 1)
                    last.then_inc(comb_ps, 1)

            def mask_rows():
                pe.wait_ge(ts_lo, 4 * NB)
                for half in range(2):
                    for k in range(4):
                        last = mm(psum[0:NE, O_BANK + 2 * half, k * TQ:(k + 1) * TQ], g_c[0:TQ, 4 * half + k, :],
                                  ident[0:TQ, 0:TQ], start=True, stop=True)
                    last.then_inc(mask_ps, 1)

            def expert(xe, first, layer, between):
                pe.wait_ge(fw_split, 2 * xe + 1)
                for n in range(2 * HT):
                    half, j = n // HT, n % HT
                    if not (first and n < 4):
                        pe.wait_ge(h_act, xe * 2 * HT + n - 3)
                    if first and n == HT:
                        pe.wait_ge(ts_lo, NB * (2 * layer + 2))
                    cols = slice(j * P, (j + 1) * P)
                    three(bank(n % 4, P, HALF_T), [(w1[:, 0, c, cols], w1[:, 1, c, cols]) for c in range(C)],
                          [xT_of(c, slice(half * HALF_T, (half + 1) * HALF_T)) for c in range(C)]).then_inc(h_ps, 1)
                    for job in between.get(("h", n), []):
                        job()
                pe.wait_ge(fw_split, 2 * xe + 2)
                for u in range(2 * C):
                    half, m = u // C, u % C
                    if not (first and u < 4):
                        pe.wait_ge(y_mul, xe * 2 * C + u - 3)
                    out = bank(4 + u % 4, P, HALF_T)
                    cols = slice(half * HALF_T, (half + 1) * HALF_T)
                    if layer == 1:
                        for s in range(2):
                            mm(out, b2h[0:NE, s, m * P:(m + 1) * P], maskT[0:NE, cols], start=s == 0, stop=False)
                    for j in range(HT):
                        if m == 0:
                            pe.wait_ge(h_lo, xe * 2 * HT + half * HT + j + 1)
                        ins = three(out, [(w2[:, 0, j, m * P:(m + 1) * P], w2[:, 1, j, m * P:(m + 1) * P])],
                                    [tuple(hc[:, s, j, cols] for s in range(2))],
                                    first=j == 0 and layer == 0, last=j == HT - 1)
                    ins.then_inc(y_ps, 1)
                    for job in between.get(("y", u), []):
                        job()

            def y_rows(layer, b):
                if layer == 0:
                    pe.wait_ge(y_add, 2 + 2 * C * NE)
                else:
                    pe.wait_ge(y_mul, 2 * C * NE + C * (b // 4 + 1))
                if b >= 2:
                    pe.wait_ge(x_new, NB * layer + b - 1)
                for c in range(C):
                    last = nc.tensor.transpose(psum[0:TQ, T_BANK + b % 2, c * P:(c + 1) * P],
                                               yT[:, c, b * TQ:(b + 1) * TQ], ident[:, :])
                last.then_inc(yt_ps, 1)

            pe.wait_ge(const_set, 1)
            for layer in range(2):
                g0 = layer * NB

                def units(us):
                    for u in us:
                        for c in range(C):
                            project(layer, g0, 0, u, c, static_first=True)

                def norm_rows(b):
                    if b >= 2:
                        pe.wait_ge(ts_lo, NB * 2 * layer + b - 1)
                    elif layer == 1:
                        pe.wait_ge(x_new, 7 + b)
                    pe.wait_ge(ln_out, NB * 2 * layer + b + 1)
                    rows_transpose(T_BANK + b % 2, b, ts_ps)

                units(range(0, 2))
                for u, bs in ((2, range(0, 4)), (3, range(4, 6)), (4, range(6, 8))):
                    if layer == 1:
                        for b in bs:
                            y_rows(0, b)
                    units([u])
                units([5])
                pe.wait_ge(ident_in, 16)
                for b in range(NB):
                    norm_rows(b)
                    if b % 2 == 1:
                        units([6 + b // 2])
                queries(layer, range(2 * C))
                units(range(10, NU))
                pe.wait_ge(pad_set, layer + 1)
                attend(layer, g0, 0, first=True)
                with pe.Fori(0, 2) as i:
                    attend(layer, g0 + 2 * i + 1, 1)
                    attend(layer, g0 + 2 * i + 2, 0)
                attend(layer, g0 + NB - 3, 1)
                attend(layer, g0 + NB - 2, 0)
                attend(layer, g0 + NB - 1, 1, more=False)

                def last_rows():
                    output_transpose(layer, NB - 1)

                def last_product():
                    norm_transpose(layer, NB - 2)
                    output_product(layer, NB - 1, 0)
                    output_product(layer, NB - 1, 1)
                    for b in range(4, NB - 1):
                        gate(layer, b)

                def last_norm():
                    norm_transpose(layer, NB - 1)

                def last_gate():
                    gate(layer, NB - 1)

                tail = {("h", 2): [last_norm], ("h", 3): [last_gate]}
                if layer == 0:
                    last_rows()
                    last_product()
                else:
                    tail.update({("h", 0): [last_rows], ("h", 1): [last_product]})
                if layer == 0:
                    spread = {("h", n): [lambda ns=ns: spread_gates(0, ns)] for n, ns in SPREAD_AT[0].items()}
                    spread["y", 0] = [lambda: pe.wait_ge(comb_out, 16)]
                    expert(0, True, 0, {**tail, **spread})
                    with pe.Fori(1, NE) as e:
                        expert(e, False, 0, {})
                else:
                    def before_output():
                        pe.wait_ge(comb_out, 32)
                        pe.wait_ge(mask_out, 2)
                        pe.wait_ge(b2_split, 1)

                    expert(NE, True, 1, {
                        **tail, ("h", 3): [last_gate, lambda: spread_gates(1, SPREAD_AT[1][3])],
                        **{("h", n): [lambda ns=ns: spread_gates(1, ns)] for n, ns in SPREAD_AT[1].items() if n > 3},
                        ("h", 9): [mask_rows],
                        ("h", 15): [before_output],
                        ("y", 5): [lambda b=b: y_rows(1, b) for b in range(4)],
                        ("y", 7): [lambda b=b: y_rows(1, b) for b in range(4, 8)]})

        @block.scalar
        def _(act):
            copy = ACT.Copy

            def weight_high(layer, k, c, scale=W_SCALE):
                if c == 0:
                    act.wait_ge(w_in[k], 16 * (layer + 1))
                nc.scalar.activation(W[:, k, 0, c, :], Wf[layer][k][:, c, :], copy, scale=scale).then_inc(w_hi, 1)

            def norm_w1_high(c):
                act.wait_ge(w1m_scaled, c + 1)
                nc.scalar.activation(w1[:, 0, c, :], w1m[c % 2], copy).then_inc(w1m_hi, 1)

            def norm_high(n, b, k, keep):
                act.wait_ge(ts_ps, NB * n + b + 1)
                src = psum[:, k, 0:C * TQ].rearrange("p (c t) -> p c t", c=C)
                if keep:
                    nc.scalar.activation(xTf[:, :, b * TQ:(b + 1) * TQ], src, copy)
                nc.scalar.activation(xT[:, 0, :, b * TQ:(b + 1) * TQ], src, copy).then_inc(ts_hi, 1)

            def output_high(layer, b):
                act.wait_ge(ot_ps, NB * layer + b + 1)
                nc.scalar.activation(xT[:, 0, :, b * TQ:(b + 1) * TQ],
                                     psum[:, OT_BANK[b], 0:C * TQ].rearrange("p (c t) -> p c t", c=C), copy)\
                    .then_inc(ot_hi, 1)

            def queries_high(layer):
                for u in range(2 * C):
                    half, g = u // C, u % C
                    act.wait_ge(q_ps, 8 * layer + u + 1)
                    nc.scalar.activation(QT[:, 0, g, half * HALF_T:(half + 1) * HALF_T],
                                         psum[:, O_BANK + u % 2, 0:HALF_T], copy, scale=Q_UNSCALE)\
                        .then_inc(q_hi, 1)

            def unit_high(gb, par, u, very_first=False):
                act.wait_ge(proj_ps, gb * NU + u + 1)
                k = J_BANK + u % 2
                if UNITS[u][0] == "K":
                    _, g, half = UNITS[u]
                    if half == 0 and g % 2 == 0 and not very_first:
                        act.wait_ge(kst_in[g // 2], 192 * gb)
                    out, src = KT[:, 0, g, half * HALF_K:(half + 1) * HALF_K], psum[:, k, 0:HALF_K]
                else:
                    t = UNITS[u][1]
                    r = key_rows(t)
                    out, src = V[par][0:r, t, :, 0, :], psum[0:r, k, :].rearrange("p (h d) -> p h d", h=NH)
                nc.scalar.activation(out, src, copy, scale=UNSCALE).then_inc(proj_hi, 1)

            def probabilities(gb, par, h):
                act.wait_ge(maxed, gb * NH + h + 1)
                nc.scalar.activation(Pr[h % 2][0:TQ, 0:NK].rearrange("q (s n) -> q s n", s=2),
                                     psum[0:TQ, S_BANK:S_BANK + 2, 0:HALF_K], ACT.Exp,
                                     bias=negmax[0:TQ, h % 2:h % 2 + 1],
                                     accum_out=rowsum[0:TQ, par, h:h + 1]).then_inc(probs, 1)

            def probsT_high(gb, h, first):
                if h >= 2 or not first:
                    act.wait_ge(pv, gb * NH + h - 1)
                for k in range(2):
                    act.wait_ge(probsT, 2 * (gb * NH + h) + k + 1)
                    nc.scalar.activation(PT[h % 2][:, 0, 3 * k:3 * k + 3, 0:TQ],
                                         psum[:, T_BANK + k, 0:3 * TQ].rearrange("p (t q) -> p t q", t=3), copy)\
                        .then_inc(pt_hi, 1)

            def attend(layer, b, gb, par, first=False, more=True):
                last_batch = not more
                for s in range(NH if more else STEPS + 1):
                    if s == 0 and not first:
                        for u in ENDS_AT[NH - 1]:
                            unit_high(gb, par, u)
                    if s > 0 and more:
                        for u in ENDS_AT[s - 1]:
                            unit_high(gb + 1, 1 - par, u)
                    if last_batch and s - 1 in OT_AT:
                        output_high(layer, OT_AT[s - 1])
                    if last_batch and s - 1 in LNT_AT:
                        norm_high(2 * layer + 1, LNT_AT[s - 1], J_BANK, True)
                    if (s > 0 or not first) and s <= NH:
                        probsT_high(*head(gb, par, s - 1)[::2], first)
                    if s < NH:
                        probabilities(gb, par, s)
                    for lay, k, c in weight_chunks_at(s, layer, b):
                        if last_batch:
                            n = 4 * k + c
                            act.wait_ge(w_scaled, n + 1)
                        weight_high(lay, k, c, 1.0 if last_batch else W_SCALE)
                    if last_batch and layer == 1 and s in NORM_W1_HIGH_AT:
                        norm_w1_high(NORM_W1_HIGH_AT[s])
                    for k in expert_chunks_at(s, layer, b):
                        if k == 0:
                            act.wait_ge(w_split, w_count(1, 1, 3))
                        if k >= C - POOL_CHUNKS:
                            act.wait_ge(w_scaled, C + POOL_CHUNKS + k + 1)
                            w1_high(0, k, 1.0)
                        else:
                            w1_high(0, k)

            def piece_high(xe, which, out, src, scale=W_SCALE):
                act.wait_ge(wf_in, 16 * (2 * xe + which + 1))
                nc.scalar.activation(out, src, copy, scale=scale).then_inc(fw_hi, 1)

            def w1_high(xe, k, scale=W_SCALE):
                piece_high(xe, 0, w1[:, 0, k, :], wf1[:, k, :], scale)

            def w2_high(xe, k):
                piece_high(xe, 1, w2[:, 0, 2 * k:2 * k + 2, :],
                           wf[:, 2 * k * D:(2 * k + 2) * D].rearrange("p (j n) -> p j n", j=2))

            def comb_out_of(layer, ns):
                for n in ns:
                    half, e = n // NE, n % NE
                    act.wait_ge(comb_ps, 16 * layer + n + 1)
                    nc.scalar.activation(comb[:, e, half * HALF_T:(half + 1) * HALF_T],
                                         psum[:, SPREAD_BANKS[n % 2], 0:HALF_T], copy).then_inc(comb_out, 1)

            def expert0(xe, first):
                if not first:
                    for k in range(C):
                        w1_high(xe, k)
                for n in range(2 * HT):
                    half, j = n // HT, n % HT
                    act.wait_ge(h_ps, xe * 2 * HT + n + 1)
                    if not (first and n < 4):
                        act.wait_ge(h_lo, xe * 2 * HT + n - 3)
                    src = psum[:, n % 4, 0:HALF_T]
                    nc.scalar.activation(hs[n % 4], src, ACT.Silu, scale=UNSCALE)
                    nc.scalar.activation(hc[:, 0, j, half * HALF_T:(half + 1) * HALF_T], src, ACT.Silu,
                                         scale=UNSCALE).then_inc(h_act, 1)
                    if first and n == 2:
                        norm_high(1, NB - 1, J_BANK, True)
                    if first and n == 4:
                        act.wait_ge(g_pre, 1)
                        nc.scalar.activation(g_e[0:TQ, :, :], g_e[0:TQ, :, :], ACT.Exp, scale=-1.0)\
                            .then_inc(g_exp, 1)
                    if first and n in SPREAD_AT[0]:
                        comb_out_of(0, SPREAD_AT[0][n])
                    if 6 <= n < 14 and n % 2 == 0:
                        w2_high(xe, n // 2 - 3)

            def expert1():
                xe = NE

                def high(n):
                    half, j = n // HT, n % HT
                    act.wait_ge(h_mul, xe * 2 * HT + n + 1 - 2 * HT * NE)
                    nc.scalar.activation(hc[:, 0, j, half * HALF_T:(half + 1) * HALF_T], hp[n % 2], copy)\
                        .then_inc(h_hi, 1)

                def gelu(n):
                    j = n % HT
                    act.wait_ge(h_ps, xe * 2 * HT + n + 1)
                    if n >= 2:
                        act.wait_ge(h_mul, n - 1)
                    nc.scalar.activation(hs[n % 2], psum[:, n % 4, 0:HALF_T], ACT.Gelu, scale=UNSCALE,
                                         bias=biasH[:, j:j + 1]).then_inc(h_act, 1)

                act.wait_ge(bh_out, 1)
                gelu(0)
                norm_high(3, NB - 2, J_BANK, True)
                gelu(1)
                act.wait_ge(b2_in, 16)
                nc.scalar.activation(b2h[0:NE, 0, :], b2f[0:NE, :], copy, scale=W_SCALE).then_inc(b2_hi, 1)
                norm_high(3, NB - 1, J_BANK, True)
                comb_out_of(1, SPREAD_AT[1][3])
                high(0)
                for n in range(2, 2 * HT):
                    gelu(n)
                    high(n - 1)
                    if n + 2 in SPREAD_AT[1]:
                        comb_out_of(1, SPREAD_AT[1][n + 2])
                    if n == 7:
                        for half in range(2):
                            act.wait_ge(mask_ps, half + 1)
                            nc.scalar.activation(maskT[0:NE, half * HALF_T:(half + 1) * HALF_T],
                                                 psum[0:NE, O_BANK + 2 * half, 0:HALF_T], copy).then_inc(mask_out, 1)
                    if 6 <= n < 14 and n % 2 == 0:
                        w2_high(xe, n // 2 - 3)
                high(2 * HT - 1)

            for layer in range(2):
                g0 = layer * NB

                def units(us):
                    for u in us:
                        unit_high(g0, 0, u, very_first=layer == 0)

                if layer == 0:
                    act.wait_ge(ctx_in, 16)
                    for c in range(C):
                        nc.scalar.activation(ctxH[0][:, 0, c, :], ctxF[:, c, :], copy).then_inc(ctx0_hi, 1)
                    for k in (0, 1):
                        for c in range(C):
                            weight_high(0, k, c)
                    act.wait_ge(w_split, w_count(0, 1, 3))
                units(range(0, 6))
                if layer == 0:
                    act.wait_ge(ident_in, 16)
                    nc.scalar.activation(ident16[:, :], ident[:, :], copy).then_inc(id16_set, 1)
                for b in range(NB):
                    norm_high(2 * layer, b, T_BANK + b % 2, False)
                    if b % 2 == 1:
                        units([6 + b // 2])
                        if layer == 0:
                            weight_high(0, 2, b // 2)
                queries_high(layer)
                units(range(10, NU))
                act.wait_ge(pad_set, layer + 1)
                attend(layer, 0, g0, 0, first=True)
                with act.Fori(0, 2) as i:
                    attend(layer, None, g0 + 2 * i + 1, 1)
                    attend(layer, None, g0 + 2 * i + 2, 0)
                attend(layer, NB - 3, g0 + NB - 3, 1)
                attend(layer, NB - 2, g0 + NB - 2, 0)
                attend(layer, NB - 1, g0 + NB - 1, 1, more=False)
                output_high(layer, NB - 1)
                if layer == 0:
                    norm_high(1, NB - 2, J_BANK, True)
                    expert0(0, True)
                    with act.Fori(1, NE) as e:
                        expert0(e, False)
                else:
                    expert1()

        @block.vector
        def _(dve):
            v = nc.vector

            def low(out, src, scale, high):
                return v.scalar_tensor_tensor(out, src, scale, high, ALU.mult, ALU.subtract)

            def weight_low(layer, k, c):
                dve.wait_ge(w_hi, w_count(layer, k, c))
                low(W[:, k, 1, c, :], Wf[layer][k][:, c, :], W_SCALE, W[:, k, 0, c, :]).then_inc(w_split, 1)

            def norm_stats(n, b):
                v.bn_stats(bst[0:TQ, b, :], x[0:TQ, b, :]).then_inc(ln_st, 1)

            def norm_moments(n, b):
                dve.wait_ge(ln_st, NB * n + b + 1)
                v.bn_aggr(mv[0:TQ, b, :], bst[0:TQ, b, :]).then_inc(ln_ag, 1)

            def norm_variance(n, b):
                dve.wait_ge(ln_ag, NB * n + b + 1)
                v.tensor_scalar(ve[0:TQ, b:b + 1], mv[0:TQ, b, 1:2], LN_EPS, None, ALU.add).then_inc(ln_var, 1)

            def norm_half(n, half):
                rows = slice(4 * half, 4 * half + 4)
                for b in range(4 * half, 4 * half + 4):
                    norm_moments(n, b)
                dve.wait_ge(ln_ag, NB * n + 4 * half + 4)
                v.tensor_scalar(ve[0:TQ, rows], mv[0:TQ, rows, 1], LN_EPS, None, ALU.add).then_inc(ln_var, 4)

            def norm_apply(n, b):
                dve.wait_ge(ln_rs, NB * n + b + 1)
                v.tensor_scalar(tok[0:TQ, b, :], x[0:TQ, b, :], mv[0:TQ, b, 0:1], rstd[0:TQ, b:b + 1],
                                ALU.subtract, ALU.mult).then_inc(ln_out, 1)

            def norm_low(n, b, k):
                dve.wait_ge(ts_hi, NB * n + b + 1)
                cols = slice(b * TQ, (b + 1) * TQ)
                low(xT[:, 1, :, cols], psum[:, k, 0:C * TQ].rearrange("p (c t) -> p c t", c=C), 1.0,
                    xT[:, 0, :, cols]).then_inc(ts_lo, 1)

            def output_low(layer, b):
                dve.wait_ge(ot_hi, NB * layer + b + 1)
                cols = slice(b * TQ, (b + 1) * TQ)
                low(xT[:, 1, :, cols], psum[:, OT_BANK[b], 0:C * TQ].rearrange("p (c t) -> p c t", c=C), 1.0,
                    xT[:, 0, :, cols]).then_inc(ot_lo, 1)

            def output_add(layer, b):
                dve.wait_ge(o_ps, NB * layer + b + 1)
                if layer == 1:
                    dve.wait_ge(bo_add, NB)
                v.scalar_tensor_tensor(x[0:TQ, b, :], psum[0:TQ, J_BANK + 1, :], UNSCALE, x[0:TQ, b, :],
                                       ALU.mult, ALU.add).then_inc(o_add, 1)

            def output_stats(layer, b):
                dve.wait_ge(o_add, NB * layer + b + 1)
                norm_stats(2 * layer + 1, b)

            def queries_low(layer):
                for u in range(2 * C):
                    half, g = u // C, u % C
                    dve.wait_ge(q_hi, 8 * layer + u + 1)
                    cols = slice(half * HALF_T, (half + 1) * HALF_T)
                    low(QT[:, 1, g, cols], psum[:, O_BANK + u % 2, 0:HALF_T], Q_UNSCALE, QT[:, 0, g, cols])\
                        .then_inc(q_lo, 1)
                    if layer == 0 and u < 4:
                        (query_bias_high, query_bias_high_again, query_bias_low, query_bias_done)[u]()
                    if layer == 1:
                        if u == 0:
                            dve.wait_ge(bo_in, 16)
                        v.tensor_tensor(x[0:TQ, u, :], x[0:TQ, u, :], boB[0:TQ, :], ALU.add).then_inc(bo_add, 1)

            def unit_low(gb, par, u):
                dve.wait_ge(proj_hi, gb * NU + u + 1)
                k = J_BANK + u % 2
                if UNITS[u][0] == "K":
                    _, g, half = UNITS[u]
                    cols = slice(half * HALF_K, (half + 1) * HALF_K)
                    low(KT[:, 1, g, cols], psum[:, k, 0:HALF_K], UNSCALE, KT[:, 0, g, cols]).then_inc(proj_lo, 1)
                else:
                    t = UNITS[u][1]
                    r = key_rows(t)
                    low(V[par][0:r, t, :, 1, :], psum[0:r, k, :].rearrange("p (h d) -> p h d", h=NH), UNSCALE,
                        V[par][0:r, t, :, 0, :]).then_inc(proj_lo, 1)

            def row_max(gb, h):
                dve.wait_ge(scores, gb * NH + h + 1)
                v.tensor_reduce(negmax[0:TQ, h % 2:h % 2 + 1], psum[0:TQ, S_BANK:S_BANK + 2, 0:HALF_K], AX.XY, ALU.max,
                                negate=True).then_inc(maxed, 1)

            def probsT_low(gb, h):
                for k in range(2):
                    dve.wait_ge(pt_hi, 2 * (gb * NH + h) + k + 1)
                    low(PT[h % 2][:, 1, 3 * k:3 * k + 3, 0:TQ],
                        psum[:, T_BANK + k, 0:3 * TQ].rearrange("p (t q) -> p t q", t=3), 1.0,
                        PT[h % 2][:, 0, 3 * k:3 * k + 3, 0:TQ]).then_inc(pt_lo, 1)

            def normalise(layer, b, gb, par, half):
                n = 2 * gb + half
                dve.wait_ge(pv, gb * NH + 8 * half + 8)
                v.reciprocal(rrec[0:TQ, :], rowsum[0:TQ, par, 8 * half:8 * half + 8]).then_inc(norm_chain, 1)
                v.tensor_reduce(red[0:TQ, :, :], psum[0:TQ, O_BANK + half, :].rearrange("q (h s d) -> q h d s", h=8, s=2),
                                AX.X, ALU.add).then_inc(norm_chain, 1)
                dve.wait_ge(norm_chain, 2 * n + 2)
                w = D // 2
                out = tok[0:TQ, bass.ds(b, 1), half * w:(half + 1) * w].rearrange("q o (h d) -> q (o h) d", h=8)
                v.tensor_tensor(out, red[0:TQ, :, :], rrec[0:TQ, :].unsqueeze(2).broadcast_to([TQ, 8, DH]), ALU.mult)\
                    .then_inc(attn_rows, 1)

            def value_bias(b, gb):
                dve.wait_ge(attn_rows, 2 * gb + 2)
                rows = tok[0:TQ, bass.ds(b, 1), :].rearrange("q o d -> q (o d)")
                v.tensor_tensor(rows, rows, bvB[0:TQ, :], ALU.add).then_inc(attn_out, 1)

            def finish_rows(layer, b, gb, par):
                normalise(layer, b, gb, par, 1)
                if layer == 1:
                    value_bias(b, gb)

            def attend(layer, b, gb, par, first=False, more=True, split_out=False):
                last_batch = not more
                for s in range(NH if more else STEPS + 1):
                    if s == STEPS:
                        finish_rows(layer, b, gb, par)
                    if s < NH:
                        row_max(gb, s)
                    if last_batch and s in ADD_AT:
                        output_add(layer, ADD_AT[s])
                    if last_batch and s - 1 in OT_AT:
                        output_low(layer, OT_AT[s - 1])
                    if last_batch and s - 1 in LNT_AT:
                        norm_low(2 * layer + 1, LNT_AT[s - 1], J_BANK)
                    if s == 0 and not first:
                        for u in ENDS_AT[NH - 1]:
                            unit_low(gb, par, u)
                    if s > 0 and more:
                        for u in ENDS_AT[s - 1][:1]:
                            unit_low(gb + 1, 1 - par, u)
                    if (s > 0 or not first) and s <= NH:
                        probsT_low(*head(gb, par, s - 1)[::2])
                    if s > 0 and more:
                        for u in ENDS_AT[s - 1][1:]:
                            unit_low(gb + 1, 1 - par, u)
                    if s == 2 and not first:
                        finish_rows(layer, b - 1, gb - 1, 1 - par)
                    if s == 9 and last_batch and layer == 1:
                        dve.wait_ge(bh_ps, 1)
                        v.tensor_tensor(biasH[:, :], hidden_bias, b1T[:, :], ALU.add).then_inc(bh_out, 1)
                    if s == 11:
                        normalise(layer, b, gb, par, 0)
                    if last_batch:
                        if s in ADD_AT:
                            output_stats(layer, ADD_AT[s])
                        if s in MOMENTS_AT:
                            norm_moments(2 * layer + 1, MOMENTS_AT[s])
                            norm_variance(2 * layer + 1, MOMENTS_AT[s])
                        if s in APPLY_AT:
                            norm_apply(2 * layer + 1, APPLY_AT[s])
                    if split_out:
                        for chunk in weight_chunks_at(s, layer, NB - 2):
                            weight_low(*chunk)

            def find_top(n, src, bs=range(NB)):
                for b in bs:
                    last = v.max(g_m[0:TQ, b, :], src[0:TQ, b, :])
                last.then_inc(g_chain, 1)
                dve.wait_ge(g_chain, n + 1)
                for b in bs:
                    last = v.max_index(g_i[0:TQ, b, :], g_m[0:TQ, b, :], src[0:TQ, b, :])
                last.then_inc(g_chain, 1)
                dve.wait_ge(g_chain, n + 2)
                rows = slice(bs[0], bs[-1] + 1)
                v.tensor_copy(g_f[0:TQ, rows, :], g_i[0:TQ, rows, :]).then_inc(g_chain, 1)
                dve.wait_ge(g_chain, n + 3)

            full = [TQ, NB, NE]
            expert_ids = eid[0:TQ, :, :].broadcast_to(full)
            logits = psum[0:TQ, O_BANK, 0:NB * NE].rearrange("q (b e) -> q b e", b=NB)

            def route_two():
                dve.wait_ge(g_exp, 1)
                v.tensor_scalar(g_1[0:TQ, :, :], g_e[0:TQ, :, :], 1.0, None, ALU.add).then_inc(g_chain, 1)
                dve.wait_ge(g_chain, 1)
                v.reciprocal(g_s[0:TQ, :, :], g_1[0:TQ, :, :]).then_inc(g_chain, 1)
                dve.wait_ge(g_chain, 2)
                find_top(2, g_s)
                v.tensor_tensor(g_1[0:TQ, :, :], expert_ids, g_f[0:TQ, :, 0:1].broadcast_to(full),
                                ALU.is_equal).then_inc(g_chain, 1)
                v.tensor_tensor(g_2[0:TQ, :, :], expert_ids, g_f[0:TQ, :, 1:2].broadcast_to(full),
                                ALU.is_equal).then_inc(g_chain, 1)
                v.tensor_tensor(g_n[0:TQ, :], g_m[0:TQ, :, 0], g_m[0:TQ, :, 1], ALU.add).then_inc(g_chain, 1)
                dve.wait_ge(g_chain, 8)
                v.tensor_tensor(g_c[0:TQ, :, :], g_1[0:TQ, :, :], g_2[0:TQ, :, :], ALU.add).then_inc(g_chain, 1)
                v.tensor_scalar(g_n[0:TQ, :], g_n[0:TQ, :], 1e-6, None, ALU.add).then_inc(g_chain, 1)
                dve.wait_ge(g_chain, 10)
                v.tensor_tensor(g_1[0:TQ, :, :], g_c[0:TQ, :, :], g_s[0:TQ, :, :], ALU.mult).then_inc(g_chain, 1)
                v.reciprocal(g_m[0:TQ, :, 0], g_n[0:TQ, :]).then_inc(g_chain, 1)
                dve.wait_ge(g_chain, 12)
                v.tensor_tensor(g_c[0:TQ, :, :], g_1[0:TQ, :, :], g_m[0:TQ, :, 0:1].broadcast_to(full),
                                ALU.mult).then_inc(g_chain, 1)
                dve.wait_ge(g_chain, 13)
                v.tensor_copy(g_h[0:TQ, 0, :, :], g_c[0:TQ, :, :]).then_inc(g_chain, 1)
                dve.wait_ge(g_chain, 14)
                v.tensor_tensor(g_h[0:TQ, 1, :, :], g_c[0:TQ, :, :], g_h[0:TQ, 0, :, :], ALU.subtract)\
                    .then_inc(g_done, 1)

            def logits_out(half):
                rows = slice(4 * half, 4 * half + 4)
                dve.wait_ge(g_ps, 2 + half)
                v.tensor_copy(g_s[0:TQ, rows, :], logits[:, rows, :]).then_inc(g_chain, 1)

            def route_one(half):
                bs = range(4 * half, 4 * half + 4)
                rows = slice(bs[0], bs[-1] + 1)
                n = LOGITS_OUT[half]
                dve.wait_ge(g_chain, n)
                find_top(n, g_s, bs)
                ids = eid[0:TQ, :, :].broadcast_to([TQ, 4, NE])
                best = g_f[0:TQ, rows, 0:1].broadcast_to([TQ, 4, NE])
                v.tensor_tensor(g_c[0:TQ, rows, :], ids, best, ALU.is_equal).then_inc(g_chain, 1)
                v.tensor_tensor(g_h[0:TQ, 0, rows, :], ids, best, ALU.is_equal).then_inc(g_done, 1)

            def y_scale(xe, u):
                half, m = u // C, u % C
                dve.wait_ge(y_add, xe * 2 * C + u + 1)
                dve.wait_ge(y_ps, xe * 2 * C + u + 1)
                gates = comb[:, bass.ds(xe, 1), half * HALF_T:(half + 1) * HALF_T].rearrange("p o t -> p (o t)")
                v.scalar_tensor_tensor(ytmp[u % 2], psum[:, 4 + u % 4, 0:HALF_T], UNSCALE, gates, ALU.mult, ALU.mult)\
                    .then_inc(y_mul, 1)

            def y_sum(xe, u):
                half, m = u // C, u % C
                cols = slice(half * HALF_T, (half + 1) * HALF_T)
                dve.wait_ge(y_mul, xe * 2 * C + u + 1)
                v.tensor_tensor(yT[:, m, cols], yT[:, m, cols], ytmp[u % 2], ALU.add).then_inc(y_add, 1)

            def y_pieces(xe, us):
                for u in us:
                    y_scale(xe, u)
                    if u % 2 == 1:
                        y_sum(xe, u - 1)
                        y_sum(xe, u)

            def w1_low(xe, k, first=False):
                dve.wait_ge(fw_hi, 8 * xe + k + 1)
                last = C - 1 - POOL_CHUNKS * first
                if first and k == last:
                    dve.wait_ge(w1_begun, POOL_CHUNKS)
                ins = low(w1[:, 1, k, :], wf1[:, k, :], W_SCALE, w1[:, 0, k, :])
                if k == last:
                    ins.then_inc(fw_split, 1)

            def w2_low(xe, k, done):
                dve.wait_ge(fw_hi, done)
                ins = low(w2[:, 1, 2 * k:2 * k + 2, :].rearrange("p j n -> p (j n)"),
                          wf[:, 2 * k * D:(2 * k + 2) * D], W_SCALE,
                          w2[:, 0, 2 * k:2 * k + 2, :].rearrange("p j n -> p (j n)"))
                if k == C - 1:
                    ins.then_inc(fw_split, 1)

            def last_rows(layer):
                output_add(layer, NB - 1)
                output_stats(layer, NB - 1)
                norm_moments(2 * layer + 1, NB - 1)
                norm_variance(2 * layer + 1, NB - 1)
                norm_apply(2 * layer + 1, NB - 1)

            def expert0(xe, first):
                if not first:
                    for k in range(C):
                        w1_low(xe, k)
                        y_pieces(xe - 1, (2 * k, 2 * k + 1))
                for n in range(2 * HT):
                    half, j = n // HT, n % HT
                    dve.wait_ge(h_act, xe * 2 * HT + n + 1)
                    cols = slice(half * HALF_T, (half + 1) * HALF_T)
                    v.tensor_tensor(hc[:, 1, j, cols], hs[n % 4], hc[:, 0, j, cols], ALU.subtract).then_inc(h_lo, 1)
                    if first and n == 2:
                        norm_low(1, NB - 1, J_BANK)
                    if first and n == 3:
                        dve.wait_ge(g_ps, 1)
                        v.tensor_tensor(g_e[0:TQ, :, :], logits, bal[0:TQ, :, :].broadcast_to(full), ALU.add)\
                            .then_inc(g_pre, 1)
                    if first and n == 4:
                        route_two()
                    if 6 <= n < 14 and n % 2 == 0:
                        k = n // 2 - 3
                        w2_low(xe, k, 8 * xe + 4 + k + 1)

            def expert1():
                def low_half(n):
                    half, j = n // HT, n % HT
                    cols = slice(half * HALF_T, (half + 1) * HALF_T)
                    dve.wait_ge(h_hi, n + 1)
                    v.tensor_tensor(hc[:, 1, j, cols], hp[n % 2], hc[:, 0, j, cols], ALU.subtract).then_inc(h_lo, 1)

                logits_out(0)
                norm_low(3, NB - 2, J_BANK)
                last_rows(1)
                route_one(0)
                norm_low(3, NB - 1, J_BANK)
                dve.wait_ge(b2_hi, 1)
                low(b2h[0:NE, 1, :], b2f[0:NE, :], W_SCALE, b2h[0:NE, 0, :]).then_inc(b2_split, 1)
                for n in range(2 * HT):
                    half, j = n // HT, n % HT
                    dve.wait_ge(h_act, NE * 2 * HT + n + 1)
                    dve.wait_ge(comb_out, 16 + n + 1)
                    if n >= 2:
                        dve.wait_ge(h_lo, NE * 2 * HT + n - 1)
                    v.tensor_tensor(hp[n % 2], hs[n % 2], comb[:, j, half * HALF_T:(half + 1) * HALF_T], ALU.mult)\
                        .then_inc(h_mul, 1)
                    if n >= 1:
                        low_half(n - 1)
                    if n == 1:
                        logits_out(1)
                        route_one(1)
                    if 7 <= n < 15 and n % 2 == 1:
                        k = (n - 7) // 2
                        w2_low(NE, k, 8 * NE + k + 1)
                low_half(2 * HT - 1)

            def x_update(layer, b):
                dve.wait_ge(yt_ps, NB * layer + b + 1)
                v.tensor_tensor(x[0:TQ, b, :], psum[0:TQ, T_BANK + b % 2, :], x[0:TQ, b, :], ALU.add)\
                    .then_inc(x_new, 1)

            v.memset(padB[:, :, :], 0.0).then_inc(bias_split, 1)
            v.memset(mhalf[:, :], -0.5)
            v.memset(ones[:, :], 1.0).then_inc(const_set, 1)

            def query_bias_high():
                dve.wait_ge(bias_in, 64)
                dve.wait_ge(bias_split, 1)
                v.tensor_scalar(padB[0:1, :, :], biasF[0:1, :, :], W_SCALE, None, ALU.mult)

            def query_bias_high_again():
                v.tensor_scalar(biasHi[32:33, :, :], biasF[32:33, :, :], W_SCALE, None, ALU.mult).then_inc(bias_split, 1)

            def query_bias_low():
                dve.wait_ge(bias_split, 2)
                low(padB[32:33, :, :], biasF[32:33, :, :], W_SCALE, biasHi[32:33, :, :]).then_inc(bias_split, 1)

            def query_bias_done():
                dve.wait_ge(bias_split, 3)

            for layer in range(2):
                g0 = layer * NB
                n0 = 2 * layer

                def unit(u):
                    unit_low(g0, 0, u)

                if layer == 0:
                    for c in range(C):
                        dve.wait_ge(ctx0_hi, c + 1)
                        ins = v.tensor_tensor(ctxH[0][:, 1, c, :], ctxF[:, c, :], ctxH[0][:, 0, c, :], ALU.subtract)
                    ins.then_inc(ctx_split, 1)
                    for k in (0, 1):
                        for c in range(C):
                            weight_low(0, k, c)
                    dve.wait_ge(x_in, 16)
                    norm_stats(0, 0)
                    norm_stats(0, 1)
                    unit(0)
                    norm_stats(0, 2)
                    norm_stats(0, 3)
                    unit(1)
                    norm_half(0, 0)
                    unit(2)
                    for b in range(4, NB):
                        norm_stats(0, b)
                    for u in (3, 4):
                        unit(u)
                    norm_apply(0, 0)
                    norm_apply(0, 1)
                    unit(5)
                else:
                    def update(bs):
                        for b in bs:
                            x_update(0, b)

                    def stats(bs):
                        for b in bs:
                            dve.wait_ge(x_new, b + 1)
                            norm_stats(2, b)

                    unit(0)
                    unit(1)
                    update(range(0, 4))
                    unit(2)
                    stats(range(0, 4))
                    norm_half(2, 0)
                    update(range(4, 6))
                    unit(3)
                    update(range(6, 8))
                    unit(4)
                    norm_apply(2, 0)
                    norm_apply(2, 1)
                    stats(range(4, 6))
                    unit(5)
                    stats(range(6, 8))
                norm_half(n0, 1)
                norm_apply(n0, 2)
                norm_apply(n0, 3)
                for b in range(NB):
                    norm_low(n0, b, T_BANK + b % 2)
                    if b % 2 == 1:
                        if b < 4:
                            norm_apply(n0, b + 3)
                            norm_apply(n0, b + 4)
                        unit(6 + b // 2)
                        if layer == 0:
                            weight_low(0, 2, b // 2)
                queries_low(layer)
                if layer == 0:
                    dve.wait_ge(small_in, 16 * 8)
                    v.tensor_scalar(lnsT[:, :, :], lnsT[:, :, :], W_SCALE, None, ALU.mult).then_inc(lns_scaled, 1)
                for k in range(2):
                    v.memset(Pr[k][0:TQ, NK:KT_TILES * P], 0.0)
                    ins = v.memset(PT[k][:, :, :, TQ:P], 0.0)
                ins.then_inc(pad_set, 1)
                for u in range(10, NU):
                    unit(u)
                attend(layer, 0, g0, 0, first=True)
                with dve.Fori(0, 2) as i:
                    attend(layer, 2 * i + 1, g0 + 2 * i + 1, 1)
                    attend(layer, 2 * i + 2, g0 + 2 * i + 2, 0)
                attend(layer, NB - 3, g0 + NB - 3, 1)
                attend(layer, NB - 2, g0 + NB - 2, 0, split_out=True)
                attend(layer, NB - 1, g0 + NB - 1, 1, more=False)
                norm_apply(2 * layer + 1, NB - 2)
                output_low(layer, NB - 1)
                if layer == 0:
                    for k in range(C - POOL_CHUNKS):
                        w1_low(0, k, first=True)
                        if k == 0:
                            norm_low(1, NB - 2, J_BANK)
                    last_rows(0)
                if layer == 0:
                    expert0(0, True)
                    with dve.Fori(1, NE) as e:
                        expert0(e, False)
                    y_pieces(NE - 1, range(2 * C))
                else:
                    expert1()
                    for us, bs in ((range(0, 6), range(0, 4)), (range(6, 8), range(4, 8))):
                        for u in us:
                            half, m = u // C, u % C
                            dve.wait_ge(y_ps, 2 * C * NE + u + 1)
                            v.tensor_scalar(yT[:, m, half * HALF_T:(half + 1) * HALF_T], psum[:, 4 + u % 4, 0:HALF_T],
                                            UNSCALE, None, ALU.mult).then_inc(y_mul, 1)
                        for b in bs:
                            x_update(1, b)


def kernel(x, ctx_1024, L0_xattn_w_q, L0_xattn_w_k, L0_xattn_w_v, L0_xattn_w_o, L0_ffn_gate_w,
           L0_ffn_balance_bias, L0_ffn_w1, L0_ffn_w2, L1_xattn_Wq, L1_xattn_bq, L1_xattn_Wk, L1_xattn_bk,
           L1_xattn_Wv, L1_xattn_bv, L1_xattn_Wo, L1_xattn_bo, L1_ffn_Wg, L1_ffn_ln_scale, L1_ffn_ln_bias,
           L1_ffn_W1, L1_ffn_b1, L1_ffn_W2, L1_ffn_b2):
    import concourse.bacc as bacc
    from concourse.bass_utils import run_bass_kernel_spmd

    def chunks(w):
        w = np.asarray(w)
        return w.reshape(-1, P, w.shape[-1]).transpose(1, 0, 2)

    w1_0, w2_0 = np.asarray(L0_ffn_w1), np.asarray(L0_ffn_w2)
    arrays = {
        "x": np.asarray(x).transpose(1, 0, 2),
        "ctx": np.asarray(ctx_1024).transpose(0, 2, 1).reshape(NB, C, P, NK).transpose(0, 2, 1, 3),
        "wq0": chunks(np.asarray(L0_xattn_w_q).T), "wk0": chunks(np.asarray(L0_xattn_w_k).T),
        "wv0": chunks(np.asarray(L0_xattn_w_v).T), "wo0": chunks(np.asarray(L0_xattn_w_o).T),
        "wq1": chunks(np.asarray(L1_xattn_Wq).T), "wk1": chunks(np.asarray(L1_xattn_Wk).T),
        "wv1": chunks(np.asarray(L1_xattn_Wv).T), "wo1": chunks(np.asarray(L1_xattn_Wo).T),
        "bq": np.asarray(L1_xattn_bq).reshape(1, D), "bk": np.asarray(L1_xattn_bk).reshape(1, D),
        "bv": np.asarray(L1_xattn_bv).reshape(D), "bo": np.asarray(L1_xattn_bo).reshape(D),
        "gate0": chunks(np.asarray(L0_ffn_gate_w).T), "gate1": chunks(np.asarray(L1_ffn_Wg).T),
        "bal": np.asarray(L0_ffn_balance_bias).reshape(NE),
        "w1_0": np.stack([chunks(w1_0[e].T).reshape(P, -1) for e in range(NE)]),
        "w2_0": np.stack([chunks(w2_0[e].T).reshape(P, -1) for e in range(NE)]),
        "w1_1": chunks(np.asarray(L1_ffn_W1).transpose(1, 0, 2).reshape(D, NE * HID1)).reshape(P, -1),
        "w2_1": np.asarray(L1_ffn_W2).transpose(1, 0, 2).reshape(P, -1),
        "lns": chunks(np.asarray(L1_ffn_ln_scale).T), "lnb": chunks(np.asarray(L1_ffn_ln_bias).T),
        "b1": np.asarray(L1_ffn_b1).T, "b2": np.asarray(L1_ffn_b2),
        "ident": np.eye(P, dtype=np.float32),
        "eid": np.arange(NE, dtype=np.float32),
    }
    nc = bacc.Bacc("TRN2", target_bir_lowering=False, num_devices=1)
    feeds, a = {}, {}
    for name, value in arrays.items():
        value = np.ascontiguousarray(value)
        feeds[f"in_{name}"] = value
        a[name] = nc.dram_tensor(f"in_{name}", value.shape, mybir.dt.from_np(value.dtype), kind="ExternalInput").ap()
    a["out"] = nc.dram_tensor("out_rows", (TQ, NB, D), mybir.dt.float32, kind="ExternalOutput").ap()
    build(nc, a)
    r = run_bass_kernel_spmd(nc, [feeds], core_ids=[0])
    return np.ascontiguousarray(r.results[0]["out_rows"].transpose(1, 0, 2))
```
